# Optimizing a Trainium2 kernel written in Bass

```python
import numpy as np
import jax
import jax.numpy as jnp

def _softmax(x, axis=-1):
    return jax.nn.softmax(x, axis=axis)

def _gelu(x):
    return jax.nn.gelu(x, approximate=True)

def _silu(x):
    return jax.nn.silu(x)

def _sigmoid(x):
    return jax.nn.sigmoid(x)

def _layernorm(x, axis=-1, eps=1e-05):
    m = jnp.mean(x, axis=axis, keepdims=True)
    v = jnp.var(x, axis=axis, keepdims=True)
    return (x - m) / jnp.sqrt(v + eps)

def _scatter_add(tgt, idx, src, axis=0):
    return tgt.at[idx].add(src)

def _segment_sum(src, seg, n):
    return jax.ops.segment_sum(src, seg, n)
kernel_name = 'mk_sandwich_d1_jaxref_r8_ecb6a4'

def setup_inputs(seed: int=0):
    np.random.seed(seed)
    _w = jnp.asarray

    def _L0_attn_setup():
        import jax, jax.numpy as jnp
        import numpy as np
        B_SZ = 2
        SEQ = 256
        D_MODEL = 256
        D_INNER = 512
        D_STATE = 128
        D_CONV = 4
        HEADDIM = 64
        NHEADS = D_INNER // HEADDIM
        CHUNK = 32
        EPS = 1e-05

        def segsum(a):
            T = a.shape[-1]
            cs = jnp.cumsum(a, axis=-1)
            ss = cs[..., :, None] - cs[..., None, :]
            mask = jnp.tril(jnp.ones((T, T), dtype=bool))
            return jnp.where(mask, ss, -jnp.inf)
        key = jax.random.key(seed)
        ks = jax.random.split(key, 8)
        conv_dim = D_INNER + 2 * D_STATE
        d_in_proj = 2 * D_INNER + 2 * D_STATE + NHEADS
        x = jax.random.normal(ks[0], (B_SZ, SEQ, D_MODEL), jnp.float32)
        in_proj_w = jax.random.normal(ks[1], (d_in_proj, D_MODEL), jnp.float32) * 0.02
        conv_w = jax.random.normal(ks[2], (conv_dim, D_CONV), jnp.float32) * 0.2
        conv_b = jnp.zeros((conv_dim,), jnp.float32)
        dt0 = jax.random.uniform(ks[3], (NHEADS,), jnp.float32, 0.001, 0.1)
        dt_bias = jnp.log(jnp.expm1(dt0))
        A_log = jnp.log(jax.random.uniform(ks[4], (NHEADS,), jnp.float32, 1.0, 16.0))
        D = jnp.ones((NHEADS,), jnp.float32)
        norm_w = jnp.ones((D_INNER,), jnp.float32)
        out_proj_w = jax.random.normal(ks[5], (D_MODEL, D_INNER), jnp.float32) * 0.02
        return {'x': x, 'in_proj_w': in_proj_w, 'conv_w': conv_w, 'conv_b': conv_b, 'dt_bias': dt_bias, 'A_log': A_log, 'D': D, 'norm_w': norm_w, 'out_proj_w': out_proj_w}
    _L0_attn_in = _L0_attn_setup()

    def _L0_ffn_setup():
        import jax, jax.numpy as jnp
        import numpy as np
        TOP_K = 6
        CAP_FACTOR = 2

        def _shared_swiglu(x, wg, wu, wd):
            return jax.nn.silu(x @ wg.T) * (x @ wu.T) @ wd.T
        key = jax.random.key(seed)
        ks = jax.random.split(key, 8)
        B, S, D, E, F, FS = (4, 256, 256, 64, 176, 352)
        scale = jnp.float32(0.02)
        return {'hidden_states': jax.random.normal(ks[0], (B, S, D), jnp.float32), 'gate_w': jax.random.normal(ks[1], (E, D), jnp.float32) * scale, 'w_gate': jax.random.normal(ks[2], (E, F, D), jnp.float32) * scale, 'w_up': jax.random.normal(ks[3], (E, F, D), jnp.float32) * scale, 'w_down': jax.random.normal(ks[4], (E, D, F), jnp.float32) * scale, 'sh_gate': jax.random.normal(ks[5], (FS, D), jnp.float32) * scale, 'sh_up': jax.random.normal(ks[6], (FS, D), jnp.float32) * scale, 'sh_down': jax.random.normal(ks[7], (D, FS), jnp.float32) * scale}
    _L0_ffn_in = _L0_ffn_setup()
    _d = {'L0_attn_x': _L0_attn_in['x'], 'L0_attn_in_proj_w': _L0_attn_in['in_proj_w'], 'L0_attn_conv_w': _L0_attn_in['conv_w'], 'L0_attn_conv_b': _L0_attn_in['conv_b'], 'L0_attn_dt_bias': _L0_attn_in['dt_bias'], 'L0_attn_A_log': _L0_attn_in['A_log'], 'L0_attn_D': _L0_attn_in['D'], 'L0_attn_norm_w': _L0_attn_in['norm_w'], 'L0_attn_out_proj_w': _L0_attn_in['out_proj_w'], 'L0_ffn_gate_w': _L0_ffn_in['gate_w'], 'L0_ffn_w_gate': _L0_ffn_in['w_gate'], 'L0_ffn_w_up': _L0_ffn_in['w_up'], 'L0_ffn_w_down': _L0_ffn_in['w_down'], 'L0_ffn_sh_gate': _L0_ffn_in['sh_gate'], 'L0_ffn_sh_up': _L0_ffn_in['sh_up'], 'L0_ffn_sh_down': _L0_ffn_in['sh_down']}
    _x0 = _d['L0_attn_x']
    _d['L0_attn_x'] = jax.random.normal(jax.random.fold_in(jax.random.key(seed), 1), (16, 256, 256), dtype=_x0.dtype)
    del _x0
    return _d

def reference(L0_attn_x, L0_attn_in_proj_w, L0_attn_conv_w, L0_attn_conv_b, L0_attn_dt_bias, L0_attn_A_log, L0_attn_D, L0_attn_norm_w, L0_attn_out_proj_w, L0_ffn_gate_w, L0_ffn_w_gate, L0_ffn_w_up, L0_ffn_w_down, L0_ffn_sh_gate, L0_ffn_sh_up, L0_ffn_sh_down):

    def _L0_attn_ref(x, in_proj_w, conv_w, conv_b, dt_bias, A_log, D, norm_w, out_proj_w):
        import jax, jax.numpy as jnp
        import numpy as np
        B_SZ = 2
        SEQ = 256
        D_MODEL = 256
        D_INNER = 512
        D_STATE = 128
        D_CONV = 4
        HEADDIM = 64
        NHEADS = D_INNER // HEADDIM
        CHUNK = 32
        EPS = 1e-05

        def segsum(a):
            T = a.shape[-1]
            cs = jnp.cumsum(a, axis=-1)
            ss = cs[..., :, None] - cs[..., None, :]
            mask = jnp.tril(jnp.ones((T, T), dtype=bool))
            return jnp.where(mask, ss, -jnp.inf)
        b, L, _ = x.shape
        conv_dim = D_INNER + 2 * D_STATE
        zxbcdt = jnp.einsum('bld,ed->ble', x, in_proj_w)
        z = zxbcdt[..., :D_INNER]
        xBC = zxbcdt[..., D_INNER:D_INNER + conv_dim]
        dt = jax.nn.softplus(zxbcdt[..., D_INNER + conv_dim:] + dt_bias)
        xBC_t = jnp.transpose(xBC, (0, 2, 1))
        conv_out = jax.lax.conv_general_dilated(xBC_t, conv_w[:, None, :], window_strides=(1,), padding=[(D_CONV - 1, 0)], feature_group_count=conv_dim)
        xBC = jax.nn.silu(jnp.transpose(conv_out + conv_b[:, None], (0, 2, 1)))
        x_ssm = xBC[..., :D_INNER].reshape(b, L, NHEADS, HEADDIM)
        Bm = xBC[..., D_INNER:D_INNER + D_STATE]
        Cm = xBC[..., D_INNER + D_STATE:]
        A = -jnp.exp(A_log)
        dA = dt * A
        X = x_ssm * dt[..., None]
        nc = L // CHUNK
        Xc = X.reshape(b, nc, CHUNK, NHEADS, HEADDIM)
        dAc = jnp.transpose(dA.reshape(b, nc, CHUNK, NHEADS), (0, 3, 1, 2))
        Bc = Bm.reshape(b, nc, CHUNK, D_STATE)
        Cc = Cm.reshape(b, nc, CHUNK, D_STATE)
        Lmat = jnp.exp(segsum(dAc))
        Y_diag = jnp.einsum('bcln,bcsn,bhcls,bcshp->bclhp', Cc, Bc, Lmat, Xc)
        A_cs = jnp.cumsum(dAc, axis=-1)
        decay_states = jnp.exp(A_cs[..., -1:] - A_cs)
        states = jnp.einsum('bcln,bhcl,bclhp->bchpn', Bc, decay_states, Xc)
        chunk_sum = jnp.pad(A_cs[..., -1], ((0, 0), (0, 0), (1, 0)))
        decay_chunk = jnp.exp(segsum(chunk_sum))
        states_cat = jnp.concatenate([jnp.zeros_like(states[:, :1]), states], axis=1)
        prev = jnp.einsum('bhzc,bchpn->bzhpn', decay_chunk, states_cat)[:, :-1]
        Y_off = jnp.einsum('bcln,bchpn,bhcl->bclhp', Cc, prev, jnp.exp(A_cs))
        Y = (Y_diag + Y_off).reshape(b, L, NHEADS, HEADDIM)
        Y = Y + x_ssm * D[:, None]
        y = Y.reshape(b, L, D_INNER)
        yg = y * jax.nn.silu(z)
        var = jnp.mean(yg * yg, axis=-1, keepdims=True)
        y = yg * jax.lax.rsqrt(var + EPS) * norm_w
        return jnp.einsum('ble,de->bld', y, out_proj_w)

    def _L0_ffn_ref(hidden_states, gate_w, w_gate, w_up, w_down, sh_gate, sh_up, sh_down):
        import jax, jax.numpy as jnp
        import numpy as np
        TOP_K = 6
        CAP_FACTOR = 2

        def _shared_swiglu(x, wg, wu, wd):
            return jax.nn.silu(x @ wg.T) * (x @ wu.T) @ wd.T
        B, S, D = hidden_states.shape
        E = gate_w.shape[0]
        x = hidden_states.reshape(-1, D)
        N = x.shape[0]
        A = N * TOP_K
        C = CAP_FACTOR * ((A + E - 1) // E)
        scores = jax.nn.softmax(x @ gate_w.T, axis=-1)
        topk_w, topk_idx = jax.lax.top_k(scores, TOP_K)
        topk_w = topk_w / (topk_w.sum(-1, keepdims=True) + 1e-20)
        flat_e = topk_idx.reshape(-1)
        flat_w = topk_w.reshape(-1)
        order = jnp.argsort(flat_e)
        se = flat_e[order]
        st = order // TOP_K
        sw = flat_w[order]
        counts = jnp.bincount(flat_e, length=E)
        offsets = jnp.cumsum(counts) - counts
        pos = jnp.arange(A) - offsets[se]
        valid = pos < C
        pos_c = jnp.minimum(pos, C - 1)
        buf = jnp.zeros((E, C, D), x.dtype).at[se, pos_c].add(jnp.where(valid[:, None], x[st], jnp.zeros((), x.dtype)))
        g = jnp.einsum('ecd,efd->ecf', buf, w_gate)
        u = jnp.einsum('ecd,efd->ecf', buf, w_up)
        eo = jnp.einsum('ecf,edf->ecd', jax.nn.silu(g) * u, w_down)
        gathered = eo[se, pos_c] * (sw * valid.astype(sw.dtype))[:, None]
        y = jnp.zeros_like(x).at[st].add(gathered).reshape(B, S, D)
        return y + _shared_swiglu(hidden_states, sh_gate, sh_up, sh_down)
    x = L0_attn_x
    x = x + _layernorm(_L0_attn_ref(_layernorm(x, axis=-1), L0_attn_in_proj_w, L0_attn_conv_w, L0_attn_conv_b, L0_attn_dt_bias, L0_attn_A_log, L0_attn_D, L0_attn_norm_w, L0_attn_out_proj_w), axis=-1)
    x = x + _layernorm(_L0_ffn_ref(_layernorm(x, axis=-1), L0_ffn_gate_w, L0_ffn_w_gate, L0_ffn_w_up, L0_ffn_w_down, L0_ffn_sh_gate, L0_ffn_sh_up, L0_ffn_sh_down), axis=-1)
    return x

_drawn_inputs = setup_inputs


def setup_inputs(seed=0):
    import zlib

    import numpy as np

    out = dict(_drawn_inputs(seed))
    spreads = {'L0_attn_conv_b': (0.0, 0.1), 'L0_attn_D': (1.0, 0.2), 'L0_attn_norm_w': (1.0, 0.2)}
    factors = {}
    for name, (base, spread) in spreads.items():
        noise = np.random.default_rng([zlib.crc32(name.encode()), seed]).standard_normal(out[name].shape)
        drawn = base * np.exp(spread * noise) if base else spread * noise
        out[name] = jnp.asarray(drawn.astype(out[name].dtype))
    for name, factor in factors.items():
        out[name] = (out[name] * factor).astype(out[name].dtype)
    return out
```

```python
from contextlib import ExitStack

import numpy as np
import concourse.bass as bass
from concourse import mybir

FP32 = mybir.dt.float32
BF16 = mybir.dt.bfloat16
I32 = mybir.dt.int32
U32 = mybir.dt.uint32
ALU = mybir.AluOpType
ACT = mybir.ActivationFunctionType
AX = mybir.AxisListType

P = 128
NB, SEQ, DM = 16, 256, 256
NT = NB * SEQ
TPB = SEQ // P
KD = DM // P
DI, DS, NH, HD, KW = 512, 128, 8, 64, 4
CD = DI + 2 * DS
CT = CD // P
XT = DI // P
CB, CC = XT, XT + 1
DIN = 2 * DI + 2 * DS + NH
NE, TOPK, FE, FS = 64, 6, 176, 352
CAP = 2 * ((NT * TOPK + NE - 1) // NE)
CAPT = CAP // P
MAIN = 4
MR = MAIN * P
EXTRA = CAPT - MAIN
F1 = FE - P
UO = 64
GW = 2 * P + UO + F1
FT = (FS + P - 1) // P
F2 = FS - (FT - 1) * P
NSLOT = NE * CAP
NQ = NE * CAPT // P
SKIP = 1 << 20
EPS = 1e-5

PER = dict(
    tensor=dict(a_xT_ps=1, a_xbc_ps=CT, a_z_ps=TPB, a_dt_ps=1,
                b_small_ps=1, b_cum_ps=TPB, b_xs_ps=TPB, b_st_ps=1, b_yd_ps=TPB, b_yo_ps=1, b_yT_ps=TPB,
                b_out_ps=1, c_hT_ps=1, c_lg_ps=1, c_pos_ps=1,
                e_T_ps=KD, e_G_ps=3, e_D_ps=2, e_tail=1, s_U_ps=3, s_D_ps=1),
    scalar=dict(a_xT=1, a_conv0=CT, a_act=1, a_z=TPB, a_sp=3,
                b_exp=4, b_xs=TPB, b_st=1, b_ss=TPB, b_yT=TPB, c_hT=2, c_exp=2 * TPB,
                e_xTa=1, e_silu=2, e_eoa=1, s_silu=2),
    vector=dict(a_stats=5, a_norm=2, a_conv=3 * CT, a_dtx=1, a_dt=2,
                b_small=4, b_dif=TPB * NH, b_xdt=3, b_y=4, b_ms=1, b_ao=7, b_aon=2, b_h=5, b_hn=2,
                c_top=9, c_slot=17, e_xTv=1, e_hid=2, e_eov=1, s_hid=2, s_acc=20),
    gpsimd=dict(a_rstd=1, b_m=TPB, b_skip=TPB, b_yg=TPB, b_rms=1, b_rs=1, b_x1=TPB, b_hrs=1,
                e_gidx=1, e_sidx=1, s_rs=1, s_out=TPB),
)
ROUND = {name: k for per in PER.values() for name, k in per.items()}
CREDIT = 2


def build(nc, T):
    ctx = ExitStack()
    with ctx:
        def sb(name, shape, dt=FP32, stack=ctx):
            return stack.enter_context(nc.sbuf_tensor(name, shape, dt))

        def sem(name):
            return ctx.enter_context(nc.semaphore(name))

        def pair(name):
            return [sem(name + "0"), sem(name + "1")]

        S = {name: sem(name) for name in ROUND}
        ld_x0, ld_x1, ld_w, ld_small, ld_c = (sem("ld_" + n) for n in "x0 x1 w small c".split())
        st_table, st_h, ld_table = sem("st_table"), pair("st_h"), sem("ld_table")
        sc_table, ld_we, ga_x, sc_y, ld_y, st_out = (
            pair(n) for n in "sc_table ld_we ga_x sc_y ld_y st_out".split())
        const_pool, const_dve, const_act = sem("const_pool"), sem("const_dve"), sem("const_act")
        tick_sp, tick_pool, tick_dve = sem("tick_sp"), sem("tick_pool"), sem("tick_dve")
        cnt_ps, cnt_sb, tab_ps, tab_sb = sem("cnt_ps"), sem("cnt_sb"), sem("tab_ps"), sem("tab_sb")
        y_zero, y_ready = sem("y_zero"), sem("y_ready")
        t_idx, t_ga, t_T_ps, t_xT, t_G_ps, t_silu, t_hid, t_D_ps, t_eo, t_sc = (
            sem("t_" + n) for n in "idx ga T_ps xT G_ps silu hid D_ps eo sc".split())

        x_all = sb("x_all", [P, NT // P * DM])
        hT_all = sb("hT_all", [P, KD, NT])
        w_all = sb("w_all", [P, NT // P * TOPK])
        ident = sb("ident", [P, P])
        ones = sb("ones", [P, P])
        neghalf = sb("neghalf", [P, TPB])
        zero_row = sb("zero_row", [P, DM])
        wsu = sb("wsu", [P, KD, 2 * FS])
        wsd = sb("wsd", [P, FT, DM])
        cnt_i = sb("cnt_i", [P, NE + 1], I32)
        we = [sb(f"we{i}", [P, KD * GW + DM]) for i in range(2)]
        we1 = [sb(f"we1{i}", [P, DM]) for i in range(2)]
        tok_idx = sb("tok_idx", [P, NE * CAPT], I32)
        row_idx = sb("row_idx", [P, NE * CAPT], I32)

        pa = ExitStack()

        def sa(name, shape, dt=FP32):
            return sb(name, shape, dt, pa)

        tri = sa("tri", [P, P])
        tri_strict = sa("tri_strict", [P, P], BF16)
        ones16 = sa("ones16", [P, P], BF16)
        cnt = sa("cnt", [P, NE])
        cnt16 = sa("cnt16", [P, NE], BF16)
        win = sa("win", [P, KD, DIN])
        wo = sa("wo", [P, XT, DM])
        wg = sa("wg", [P, KD, NE])
        convp = sa("convp", [P, CT, KW + 1])
        normw = sa("normw", [P, XT])
        hpar = sa("hpar", [P, 3, NH])
        expA = sa("expA", [P, NH])
        negA = sa("negA", [P, NH])
        Dx = sa("Dx", [P, NH, HD])
        iota_e = sa("iota_e", [P, NE])
        table0 = sa("table0", [P, NSLOT // P, 2])
        pay = [sa(f"pay{i}", [P, TPB * TOPK, 2]) for i in range(2)]
        step_pay = sa("step_pay", [P, TPB * TOPK, 2])
        a_st, a_mv, a_ve, a_rs = sa("a_st", [P, TPB, 6]), sa("a_mv", [P, TPB, 2]), sa("a_ve", [P, TPB]), sa("a_rs", [P, TPB])
        xn = sa("xn", [P, TPB, DM])
        xT = sa("xT", [P, KD, SEQ])
        acc = sa("acc", [P, CT, SEQ])
        xbc = [sa(f"xbc{i}", [P, CT, SEQ]) for i in range(2)]
        zs = [sa(f"zs{i}", [P, TPB, DI]) for i in range(2)]
        dtx, dta, dte, dtl = (sa(n, [P, TPB, NH]) for n in "dtx dta dte dtl".split())
        dt = [sa(f"dt{i}", [P, TPB, NH]) for i in range(2)]
        dA = [sa(f"dA{i}", [P, TPB, NH]) for i in range(2)]
        Gm = sa("Gm", [P, TPB, P])
        cum = sa("cum", [P, TPB, NH])
        left = sa("left", [P, NH])
        BT = sa("BT", [P, P])
        M = sa("M", [P, TPB, NH, P])
        xs, xdt, skip, yg, yT = (sa(n, [P, TPB, DI]) for n in "xs xdt skip yg yT".split())
        xw, state, yoff, junk = (sa(n, [P, DI]) for n in "xw state yoff junk".split())
        wleft, ecum = sa("wleft", [P, NH]), sa("ecum", [P, NH])
        ss, ms, rms = (sa(n, [P, TPB]) for n in "ss ms rms".split())
        ao, aon, h = (sa(n, [P, TPB, DM]) for n in "ao aon h".split())
        b_stt, b_mv, b_ve, b_rst = sa("b_stt", [P, TPB, 6]), sa("b_mv", [P, TPB, 2]), sa("b_ve", [P, TPB]), sa("b_rst", [P, TPB])
        h_st, h_mv, h_ve, h_rst = sa("h_st", [P, TPB, 6]), sa("h_mv", [P, TPB, 2]), sa("h_ve", [P, TPB]), sa("h_rst", [P, TPB])
        hTb = sa("hTb", [P, KD, SEQ])
        lg = sa("lg", [P, TPB, NE])
        mx = sa("mx", [P, TPB, 8])
        ix = sa("ix", [P, TPB, 8], U32)
        nmx, esum, rsum, s6, s6e, r6 = (sa(n, [P, TPB]) for n in "nmx esum rsum s6 s6e r6".split())
        e64 = sa("e64", [P, TPB, NE])
        ixf, e6, pk, slot, over, fits, p6, w6 = (
            sa(n, [P, TPB, TOPK]) for n in "ixf e6 pk slot over fits p6 w6".split())
        oh = sa("oh", [P, TPB, TOPK, NE])
        sel = sa("sel", [P, TPB, TOPK, NE])
        chosen = sa("chosen", [P, TPB, NE], BF16)
        slot_i = [sa(f"slot_i{i}", [P, TPB * TOPK], I32) for i in range(2)]
        pa.close()

        pb = ExitStack()

        def sbb(name, shape, dt=FP32):
            return sb(name, shape, dt, pb)

        tab = sbb("tab", [P, NQ, P, 2])
        xg = [sbb(f"xg{i}", [P, MAIN, DM]) for i in range(2)]
        xgT = [sbb(f"xgT{i}", [P, KD, MR]) for i in range(2)]
        g_idx = [sbb(f"g_idx{i}", [P, MAIN], I32) for i in range(2)]
        s_idx = [sbb(f"s_idx{i}", [P, MAIN], I32) for i in range(2)]
        sg = [sbb(f"sg{i}", [P, 2, MR]) for i in range(2)]
        hid = [sbb(f"hid{i}", [P, 2, MR]) for i in range(2)]
        eo = [sbb(f"eo{i}", [P, MAIN, DM]) for i in range(2)]
        t_xg, t_out = sbb("t_xg", [P, DM]), sbb("t_out", [P, DM])
        t_xgT, t_sg, t_hd = (sbb(n, [P, 2, P]) for n in "t_xgT t_sg t_hd".split())
        t_i = sbb("t_i", [P, 2], I32)
        s_sg, s_hd = sbb("s_sg", [P, FT, SEQ]), sbb("s_hd", [P, FT, SEQ])
        yb = [sbb(f"yb{i}", [P, TPB, TOPK, DM]) for i in range(2)]
        wb = sbb("wb", [P, TPB, TOPK])
        cacc, cn = sbb("cacc", [P, TPB, DM]), sbb("cn", [P, TPB, DM])
        c_st, c_mv, c_ve, c_rs = sbb("c_st", [P, TPB, 6]), sbb("c_mv", [P, TPB, 2]), sbb("c_ve", [P, TPB]), sbb("c_rs", [P, TPB])
        fin = [sbb(f"fin{i}", [P, TPB, DM]) for i in range(2)]
        pb.close()

        bank = [ctx.enter_context(nc.psum_tensor(f"bank{i}", [P, 512], FP32)) for i in range(8)]

        h_dram = nc.dram_tensor("h_rows", [NT, DM], FP32, kind="Internal").ap()
        table = nc.dram_tensor("slot_table", [NSLOT, 2], FP32, kind="Internal").ap()
        y_rows = nc.dram_tensor("y_rows", [NT * TOPK, DM], FP32, kind="Internal").ap()

        def start(eng, which):
            for name, k in PER[which].items():
                eng.sem_inc(S[name], CREDIT * k)

        def hold(eng):
            if eng is nc.gpsimd:
                eng.sem_inc(tick_pool, 1)
            elif eng is nc.sync:
                eng.sem_inc(tick_sp, 1)

        def hold_dve(i):
            if not isinstance(i, int):
                nc.vector.sem_inc(tick_dve, 1)

        def wait(eng, s, value):
            if isinstance(value, int) and value == 0:
                return
            eng.wait_ge(s, value)
            if not isinstance(value, int):
                hold(eng)

        def need(eng, name, i, n=None):
            if isinstance(i, int) and i < 0:
                return
            k = ROUND[name]
            wait(eng, S[name], i * k + ((k if n is None else n) + CREDIT * k))

        def pipeline(eng, items, lags, work, peel=0):
            lo = max(lags) + max(lags) % 2 + peel
            hi = items + min(lags)
            hi -= (hi - lo) % 2

            def at(m, par, n=None):
                out = []
                for lag in lags:
                    q = par - lag
                    on = n is None or 0 <= n - lag < items
                    out.append((m * 2 + q, m + q // 2, q % 2) if on else None)
                return out

            for n in range(min(lags), lo):
                work(*at(n // 2, n % 2, n))
            with eng.Fori(lo // 2, hi // 2) as m:
                for par in range(2):
                    work(*at(m, par))
            for n in range(hi, items + max(lags)):
                work(*at(n // 2, n % 2, n))

        def phase_a_over(eng):
            eng.wait_ge(cnt_sb, 3)
            for q in range(2):
                eng.wait_ge(sc_table[q], NB // 2 * TPB * TOPK * 16)
                eng.wait_ge(st_h[q], (NB // 2 + 1) * 16)

        block = ctx.enter_context(nc.Block())

        @block.sync
        def _(sp):
            for q in range(2):
                sp.sem_inc(st_h[q], 16)
            sp.dma_start(x_all[:, 0:TPB * DM].rearrange("p (t d) -> p t d", d=DM),
                         T["x"][0:SEQ].rearrange("(t p) d -> p t d", p=P)).then_inc(ld_x0, 16)
            sp.dma_start(hpar[:], T["hpar"][None, :, :].to_broadcast([P, 3, NH])).then_inc(ld_small, 16)
            sp.dma_start(convp[:], T["convp"]).then_inc(ld_small, 16)
            sp.dma_start(normw[:], T["normw"]).then_inc(ld_small, 16)
            sp.dma_start(wo[:], T["wo"]).then_inc(ld_small, 16)
            sp.dma_start(wg[:], T["wg"]).then_inc(ld_small, 16)
            sp.dma_start(win[:], T["win"]).then_inc(ld_w, 16)
            sp.dma_start(x_all[:, TPB * DM:].rearrange("p (t d) -> p t d", d=DM),
                         T["x"][SEQ:].rearrange("(t p) d -> p t d", p=P)).then_inc(ld_x1, 16)
            sp.dma_start(wsu[:], T["wsu"]).then_inc(ld_c, 16)
            sp.dma_start(wsd[:], T["wsd"]).then_inc(ld_c, 16)
            sp.wait_ge(const_pool, 2)
            sp.dma_start(table.rearrange("(p s) c -> p s c", p=P), table0[:]).then_inc(st_table, 16)

            def load_expert(e, m, par):
                need(sp, "e_D_ps", e - 2)
                need(sp, "e_tail", e - 2)
                sp.dma_start(we[par][:], T["we"][bass.ts(e, P), :]).then_inc(ld_we[par], 16)
                sp.dma_start(we1[par][0:F1, :], T["we1"][bass.ts(e, F1), :]).then_inc(ld_we[par], 16)

            load_expert(0, 0, 0)
            load_expert(1, 0, 1)

            def store_h(b):
                if b:
                    need(sp, "b_hn", b[0])
                    sp.dma_start(h_dram[bass.ts(b[0], SEQ), :].rearrange("(t p) d -> p t d", p=P), h[:]
                                 ).then_inc(st_h[b[2]], 16)

            pipeline(sp, NB, [1], store_h)
            phase_a_over(sp)
            sp.dma_start(tab[:], table.rearrange("(q g s) c -> g q s c", g=P, s=P)).then_inc(ld_table, 16)
            most = sp.value_load(cnt_i[0:1, NE:NE + 1])
            with sp.If(most > CAP):
                sp.dma_start(y_rows.rearrange("(p r) d -> p r d", p=P),
                             zero_row[:, None, :].to_broadcast([P, NT * TOPK // P, DM])).then_inc(y_zero, 16)
                sp.wait_ge(y_zero, 16)
                sp.sem_inc(tick_sp, 1)
            sp.sem_inc(y_ready, 1)

            with sp.Fori(1, NE // 2) as m:
                for par in range(2):
                    load_expert(m * 2 + par, m, par)

            def load_y(b, m, par):
                need(sp, "s_acc", b - 2, 12)
                sp.dma_start(yb[par][:], y_rows[bass.ts(b, SEQ * TOPK), :].rearrange(
                    "(t p k) d -> p t k d", p=P, k=TOPK)).then_inc(ld_y[par], 16)

            def store_out(b, m, par):
                need(sp, "s_out", b)
                sp.dma_start(T["out"][bass.ts(b, SEQ), :].rearrange("(t p) d -> p t d", p=P), fin[par][:]
                             ).then_inc(st_out[par], 16)

            for q in range(2):
                sp.wait_ge(sc_y[q], NE // 2 * MAIN * 16)
            sp.wait_ge(y_ready, 1)
            sp.wait_ge(const_pool, 6)
            load_y(0, 0, 0)
            load_y(1, 0, 1)
            with sp.Fori(1, NB // 2) as m:
                for par in range(2):
                    store_out(m * 2 + par - 2, m - 1, par)
                    load_y(m * 2 + par, m, par)
            for b in range(NB - 2, NB):
                store_out(b, b // 2, b % 2)
            for q in range(2):
                sp.wait_ge(st_out[q], (NB // 2 + 1) * 16)

        @block.gpsimd
        def _(pool):
            start(pool, "gpsimd")
            for q in range(2):
                pool.sem_inc(st_out[q], 16)
            pool.memset(table0[:, :, 0:1], 0.0)
            pool.memset(table0[:, :, 1:2], float(SKIP)).then_inc(const_pool, 1)
            pool.memset(we1[0][:], 0.0)
            pool.memset(we1[1][:], 0.0).then_inc(const_pool, 1)
            pool.memset(ident[:], 0.0)
            pool.memset(ones[:], 1.0)
            pool.memset(neghalf[:], -0.5)
            pool.memset(zero_row[:], 0.0)
            pool.memset(step_pay[:, :, 0:1], float(SEQ))
            pool.memset(step_pay[:, :, 1:2], float(SEQ * TOPK))
            pool.memset(ones16[:], 1.0).then_inc(const_pool, 1)
            pool.wait_ge(const_pool, 3)
            pool.affine_select(out=ident[:], in_=ident[:], compare_op=ALU.not_equal, fill=1.0, base=0,
                               pattern=[[-1, P]], channel_multiplier=1)
            pool.affine_select(out=tri[:], in_=ones[:], compare_op=ALU.is_ge, fill=0.0, base=0,
                               pattern=[[1, P]], channel_multiplier=-1)
            pool.affine_select(out=tri_strict[:], in_=ones[:], compare_op=ALU.is_gt, fill=0.0, base=0,
                               pattern=[[1, P]], channel_multiplier=-1)
            pool.iota(iota_e[:], pattern=[[1, NE]], base=0, channel_multiplier=0,
                      allow_small_or_imprecise_dtypes=True)
            pool.iota(pay[1][:, :, 0].rearrange("p (t k) -> p t k", t=TPB), pattern=[[P, TPB], [0, TOPK]],
                      base=-SEQ, channel_multiplier=1, allow_small_or_imprecise_dtypes=True)
            pool.iota(pay[1][:, :, 1].rearrange("p (t k) -> p t k", t=TPB),
                      pattern=[[P * TOPK, TPB], [1, TOPK]], base=-SEQ * TOPK, channel_multiplier=TOPK,
                      allow_small_or_imprecise_dtypes=True).then_inc(const_pool, 1)
            pool.wait_ge(const_dve, 3)
            pool.wait_ge(st_table, 16)

            def scatter_slots(c, t):
                for k in range(t * TOPK, (t + 1) * TOPK):
                    pool.indirect_dma_start(
                        table, bass.IndirectOffsetOnAxis(ap=slot_i[c[2]][:, k:k + 1], axis=0),
                        pay[c[2]][:, k, :], None, bounds_check=NSLOT - 1, oob_is_err=False
                    ).then_inc(sc_table[c[2]], 16)

            def rows(a, b, c):
                if a:
                    need(pool, "a_stats", a[0])
                    need(pool, "a_norm", a[0] - 1)
                    pool.tensor_tensor(a_rs[:], a_ve[:], neghalf[:], ALU.pow).then_inc(S["a_rstd"], 1)
                if b:
                    need(pool, "b_small", b[0])
                    for t in range(TPB):
                        need(pool, "b_exp", b[0], t + 1)
                        pool.tensor_tensor(M[:, t], M[:, t], Gm[:, t:t + 1, :].to_broadcast([P, NH, P]),
                                           ALU.mult).then_inc(S["b_m"], 1)
                    need(pool, "b_y", b[0] - 1)
                    for t in range(TPB):
                        need(pool, "b_xs", b[0], t + 1)
                        pool.tensor_tensor(skip[:, t], xs[:, t], Dx[:].rearrange("p h d -> p (h d)"), ALU.mult
                                           ).then_inc(S["b_skip"], 1)
                    for t in range(TPB):
                        need(pool, "b_y", b[0], 1 if t == 0 else 4)
                        pool.tensor_tensor(yg[:, t], yg[:, t], zs[b[2]][:, t], ALU.mult).then_inc(S["b_yg"], 1)
                if c:
                    need(pool, "c_slot", c[0])
                    scatter_slots(c, 0)
                if b:
                    need(pool, "b_ms", b[0])
                    pool.tensor_tensor(rms[:], ms[:], neghalf[:], ALU.pow).then_inc(S["b_rms"], 1)
                    need(pool, "b_ao", b[0])
                    pool.tensor_tensor(b_rst[:], b_ve[:], neghalf[:], ALU.pow).then_inc(S["b_rs"], 1)
                    for t in range(TPB):
                        need(pool, "b_aon", b[0], t + 1)
                        xrow = x_all[:, bass.ts(b[0] * TPB + t, DM)]
                        pool.tensor_tensor(xrow, xrow, aon[:, t], ALU.add).then_inc(S["b_x1"], 1)
                    need(pool, "b_h", b[0])
                    pool.tensor_tensor(h_rst[:], h_ve[:], neghalf[:], ALU.pow).then_inc(S["b_hrs"], 1)
                if c:
                    scatter_slots(c, 1)

            pipeline(pool, NB, [0, 1, 2], rows)

            phase_a_over(pool)
            for i in range(2):
                pool.memset(hid[i][:], 0.0)
            pool.memset(t_hd[:], 0.0).then_inc(const_pool, 1)
            pool.wait_ge(tab_sb, 2 * NQ)
            pool.wait_ge(y_ready, 1)
            tails = pool.alloc_register("pool_tails")
            pool.reg_mov(tails, 0)

            def gather(e, m, par):
                need(pool, "e_T_ps", e - 2)
                wait(pool, ga_x[par], m * (MAIN * 16))
                pool.tensor_copy(g_idx[par][:], tok_idx[:, bass.ds(e * CAPT, MAIN)]).then_inc(S["e_gidx"], 1)
                need(pool, "e_gidx", e)
                for j in range(MAIN):
                    pool.indirect_dma_start(
                        xg[par][:, j, :], None, h_dram,
                        bass.IndirectOffsetOnAxis(ap=g_idx[par][:, j:j + 1], axis=0),
                        bounds_check=NT - 1, oob_is_err=False).then_inc(ga_x[par], 16)

            def scatter(e, m, par):
                wait(pool, sc_y[par], m * (MAIN * 16))
                pool.tensor_copy(s_idx[par][:], row_idx[:, bass.ds(e * CAPT, MAIN)]).then_inc(S["e_sidx"], 1)
                need(pool, "e_sidx", e)
                need(pool, "e_eoa", e)
                need(pool, "e_eov", e)
                for j in range(MAIN):
                    pool.indirect_dma_start(
                        y_rows, bass.IndirectOffsetOnAxis(ap=s_idx[par][:, j:j + 1], axis=0),
                        eo[par][:, j, :], None, bounds_check=NT * TOPK - 1, oob_is_err=False
                    ).then_inc(sc_y[par], 16)

            def tail(e):
                n = pool.value_load(cnt_i[0:1, bass.ds(e, 1)])
                with pool.If(n > MR):
                    r = pool.snap(tails)
                    for j in range(EXTRA):
                        i = r * EXTRA + j
                        if j:
                            wait(pool, t_sc, i * 16)
                        pool.tensor_copy(t_i[:, 0:1], tok_idx[:, bass.ds(e * CAPT + (MAIN + j), 1)])
                        pool.tensor_copy(t_i[:, 1:2], row_idx[:, bass.ds(e * CAPT + (MAIN + j), 1)]).then_inc(t_idx, 1)
                        wait(pool, t_idx, i + 1)
                        pool.indirect_dma_start(t_xg[:], None, h_dram,
                                                bass.IndirectOffsetOnAxis(ap=t_i[:, 0:1], axis=0),
                                                bounds_check=NT - 1, oob_is_err=False).then_inc(t_ga, 16)
                        wait(pool, t_eo, i + 1)
                        pool.indirect_dma_start(y_rows, bass.IndirectOffsetOnAxis(ap=t_i[:, 1:2], axis=0),
                                                t_out[:], None, bounds_check=NT * TOPK - 1, oob_is_err=False
                                                ).then_inc(t_sc, 16)
                    wait(pool, t_sc, (r * EXTRA + EXTRA) * 16)
                    pool.reg_add(tails, tails, 1)
                pool.sem_inc(tick_pool, 1)

            def expert_rows(g, d):
                if g:
                    gather(*g)
                if d:
                    scatter(*d)
                    tail(d[0])

            pipeline(pool, NE, [0, 3], expert_rows, peel=2)
            pool.sem_inc(const_pool, 1)

            def finish(b):
                if b:
                    need(pool, "s_acc", b[0], 18)
                    pool.tensor_tensor(c_rs[:], c_ve[:], neghalf[:], ALU.pow).then_inc(S["s_rs"], 1)
                    wait(pool, st_out[b[2]], (b[1] + 1) * 16)
                    for t in range(TPB):
                        need(pool, "s_acc", b[0], 19 + t)
                        pool.tensor_tensor(fin[b[2]][:, t], cn[:, t], x_all[:, bass.ts(b[0] * TPB + t, DM)],
                                           ALU.add).then_inc(S["s_out"], 1)

            pipeline(pool, NB, [1], finish)

        @block.tensor
        def _(pe):
            start(pe, "tensor")

            def mm(out, lhsT, rhs, first=True, last=True):
                return nc.tensor.matmul(out, lhsT, rhs, start=first, stop=last)

            def rotate(out, in_):
                return nc.tensor.transpose(out, in_, ident[:])

            pe.wait_ge(const_pool, 4)
            pe.wait_ge(ld_w, 16)
            pe.wait_ge(ld_small, 80)
            pe.wait_ge(const_dve, 2 + XT)

            def mamba(a, b, c):
                if b:
                    B = xbc[b[2]]
                    need(pe, "a_act", b[0])
                    need(pe, "a_dt", b[0])
                    need(pe, "b_yT", b[0] - 1)
                    for t in range(TPB):
                        mm(bank[1][:, bass.ts(t, P)], B[:, CB, bass.ts(t, P)], B[:, CC, bass.ts(t, P)])
                    for t in range(TPB):
                        mm(bank[1][:, 256 + t * NH:256 + (t + 1) * NH], tri[:], dA[b[2]][:, t, :])
                    mm(bank[1][:, 272:272 + NH], ones[:], dA[b[2]][:, 0, :])
                    rotate(bank[1][:, 384:512], B[:, CB, 0:P]).then_inc(S["b_small_ps"], 1)
                    need(pe, "a_conv", b[0])
                    need(pe, "b_ao", b[0] - 1, 2)
                    for t in range(TPB):
                        for hh in range(NH):
                            last = mm(bank[2 + 2 * t + hh // 4][:, bass.ts(hh % 4, P)],
                                      dA[b[2]][:, t, hh:hh + 1].to_broadcast([P, P]), tri[:])
                        last.then_inc(S["b_cum_ps"], 1)
                    need(pe, "b_yT", b[0] - 1, 1)
                    need(pe, "c_slot", b[0] - 2, 1)
                    for t in range(TPB):
                        for k in range(XT):
                            last = rotate(bank[6 + t][:, bass.ts(k, P)], B[:, k, bass.ts(t, P)])
                        last.then_inc(S["b_xs_ps"], 1)
                if a:
                    need(pe, "a_norm", a[0])
                    need(pe, "b_st", a[0] - 2)
                    for k in range(KD):
                        for t in range(TPB):
                            last = rotate(bank[0][:, k * SEQ + t * P:k * SEQ + (t + 1) * P],
                                          xn[:, t, bass.ts(k, P)])
                    last.then_inc(S["a_xT_ps"], 1)
                if c:
                    need(pe, "b_hn", c[0])
                    if a:
                        need(pe, "a_xT", a[0])
                    else:
                        need(pe, "b_st", c[0])
                    for k in range(KD):
                        for t in range(TPB):
                            last = rotate(bank[0][:, k * SEQ + t * P:k * SEQ + (t + 1) * P],
                                          h[:, t, bass.ts(k, P)])
                    last.then_inc(S["c_hT_ps"], 1)
                if a:
                    need(pe, "a_xT", a[0])
                    need(pe, "b_dif", a[0] - 1)
                    for k in range(CT):
                        for d in range(KD):
                            last = mm(bank[2 + k // 2][:, bass.ts(k % 2, SEQ)],
                                      win[:, d, DI + k * P:DI + (k + 1) * P], xT[:, d, :], d == 0, d == KD - 1)
                        last.then_inc(S["a_xbc_ps"], 1)
                    need(pe, "b_xs", a[0] - 1)
                    for t in range(TPB):
                        for d in range(KD):
                            last = mm(bank[5 + t][:], xT[:, d, bass.ts(t, P)], win[:, d, 0:DI], d == 0, d == KD - 1)
                        last.then_inc(S["a_z_ps"], 1)
                    need(pe, "c_hT", a[0] - 2)
                    for t in range(TPB):
                        for d in range(KD):
                            last = mm(bank[0][:, bass.ts(t, NH)], xT[:, d, bass.ts(t, P)],
                                      win[:, d, DI + CD:DIN], d == 0, d == KD - 1)
                    last.then_inc(S["a_dt_ps"], 1)
                if b:
                    need(pe, "b_xdt", b[0])
                    if a:
                        need(pe, "a_dtx", a[0])
                        need(pe, "a_z", a[0], 1)
                    elif c:
                        need(pe, "c_hT", c[0])
                    need(pe, "b_small", b[0])
                    mm(bank[0][:], BT[:], xw[:]).then_inc(S["b_st_ps"], 1)
                    need(pe, "b_xs", b[0])
                    for t in range(TPB):
                        need(pe, "b_m", b[0], t + 1)
                        for hh in range(NH):
                            last = mm(bank[7 if t == 0 else 1][:, bass.ts(hh, HD)], M[:, t, hh, :],
                                      xdt[:, t, bass.ts(hh, HD)])
                        last.then_inc(S["b_yd_ps"], 1)
                    need(pe, "b_dif", b[0])
                    need(pe, "b_st", b[0])
                    mm(bank[5][:], B[:, CC, P:2 * P], state[:]).then_inc(S["b_yo_ps"], 1)
                if c:
                    need(pe, "c_hT", c[0])
                    if a:
                        need(pe, "a_z", a[0])
                    elif b:
                        need(pe, "b_xs", b[0])
                    for t in range(TPB):
                        for d in range(KD):
                            last = mm(bank[6][:, bass.ts(t, NE)], hTb[:, d, bass.ts(t, P)], wg[:, d, :],
                                      d == 0, d == KD - 1)
                    last.then_inc(S["c_lg_ps"], 1)
                if b:
                    for t in range(TPB):
                        need(pe, "b_yg", b[0], t + 1)
                        for k in range(XT):
                            last = rotate(bank[7 if t == 0 else 1][:, bass.ts(k, P)], yg[:, t, bass.ts(k, P)])
                        last.then_inc(S["b_yT_ps"], 1)
                if c:
                    need(pe, "c_top", c[0])
                    need(pe, "c_slot", c[0] - 1)
                    for t in range(TPB):
                        out = bank[6][:, 2 * NE + t * NE:2 * NE + (t + 1) * NE]
                        mm(out, tri_strict[:], chosen[:, t, :], True, False)
                        if t:
                            mm(out, ones16[:], chosen[:, 0, :], False, False)
                        last = mm(out, ones16[:], cnt16[:], False, True)
                    last.then_inc(S["c_pos_ps"], 1)
                if b:
                    need(pe, "b_y", b[0])
                    for t in range(TPB):
                        need(pe, "b_yT", b[0], t + 1)
                        for k in range(XT):
                            last = mm(bank[5][:, bass.ts(t, DM)], yT[:, t, bass.ts(k, P)], wo[:, k, :],
                                      k == 0, k == XT - 1)
                    last.then_inc(S["b_out_ps"], 1)

            pipeline(pe, NB, [0, 1, 2], mamba)

            need(pe, "c_slot", NB - 1)
            mm(bank[0][:, 0:NE], ones16[:], cnt16[:]).then_inc(cnt_ps, 1)

            phase_a_over(pe)
            pe.wait_ge(ld_table, 16)
            for q in range(NQ):
                for f in range(2):
                    rotate(bank[f][:, bass.ts(q, P)], tab[:, q, :, f]).then_inc(tab_ps, 1)
            pe.wait_ge(tab_sb, 2 * NQ)
            pe.wait_ge(const_pool, 5)
            tails = pe.alloc_register("pe_tails")
            pe.reg_mov(tails, 0)

            def gate_up(par, out, xT_, cols):
                for k, (at, n) in enumerate(((0, P), (P, P), (2 * P, UO + F1))):
                    for d in range(KD):
                        last = mm(out(k)[0:n], we[par][:, d * GW + at:d * GW + at + n], xT_[:, d, cols],
                                  d == 0, d == KD - 1)
                    yield last

            def down(par, out, hd, cols):
                mm(out, hd[:, 0, cols], we[par][:, KD * GW:], True, False)
                return mm(out, hd[:, 1, cols], we1[par][:], False, True)

            def expert(t, g, d):
                if t:
                    wait(pe, ga_x[t[2]], (t[1] + 1) * (MAIN * 16))
                    need(pe, "e_xTa", t[0] - 1)
                    need(pe, "e_xTv", t[0] - 1)
                    for k in range(KD):
                        for j in range(MAIN):
                            last = rotate(bank[k][:, bass.ts(j, P)], xg[t[2]][:, j, bass.ts(k, P)])
                        last.then_inc(S["e_T_ps"], 1)
                if g:
                    wait(pe, ld_we[g[2]], (g[1] + 1) * 32)
                    need(pe, "e_xTa", g[0])
                    need(pe, "e_xTv", g[0])
                    need(pe, "e_silu", g[0] - 1)
                    need(pe, "e_hid", g[0] - 1)
                    for last in gate_up(g[2], lambda k: bank[2 + k], xgT[g[2]], slice(0, MR)):
                        last.then_inc(S["e_G_ps"], 1)
                if d:
                    need(pe, "e_hid", d[0])
                    need(pe, "e_eoa", d[0] - 1)
                    need(pe, "e_eov", d[0] - 1)
                    for j in range(MAIN):
                        last = down(d[2], bank[5 + j // 2][:, bass.ts(j % 2, DM)], hid[d[2]], bass.ts(j, P))
                        if j % 2:
                            last.then_inc(S["e_D_ps"], 1)
                    n = pe.value_load(cnt_i[0:1, bass.ds(d[0], 1)])
                    with pe.If(n > MR):
                        r = pe.snap(tails)
                        for j in range(EXTRA):
                            i = r * EXTRA + j
                            pe.wait_ge(t_ga, (i + 1) * 16)
                            for k in range(KD):
                                last = rotate(bank[7][:, bass.ts(k, P)], t_xg[:, bass.ts(k, P)])
                            last.then_inc(t_T_ps, 1)
                            pe.wait_ge(t_xT, i + 1)
                            for last in gate_up(d[2], lambda k: bank[7][:, bass.ts(k, P)], t_xgT, slice(0, P)):
                                pass
                            last.then_inc(t_G_ps, 1)
                            pe.wait_ge(t_hid, (i + 1) * 2)
                            down(d[2], bank[7][:, 0:DM], t_hd, slice(0, P)).then_inc(t_D_ps, 1)
                        pe.wait_ge(t_eo, r * EXTRA + EXTRA)
                        pe.reg_add(tails, tails, 1)
                    pe.sem_inc(S["e_tail"], 1)

            pipeline(pe, NE, [1, 2, 3], expert)

            need(pe, "e_eoa", NE - 1)
            need(pe, "e_eov", NE - 1)
            need(pe, "e_hid", NE - 1)
            pe.wait_ge(ld_c, 32)

            def shared(u, d):
                if u:
                    o = 3 * u[2]
                    need(pe, "s_hid", u[0] - 2)
                    cols = bass.ts(u[0], SEQ)
                    for k, parts in enumerate((((0, P), (P, P)), ((FS, P), (FS + P, P)),
                                               ((2 * P, F2), (FS + 2 * P, F2)))):
                        for i, (at, n) in enumerate(parts):
                            for dd in range(KD):
                                last = mm(bank[o + k][0:n, bass.ts(i, SEQ)], wsu[:, dd, at:at + n],
                                          hT_all[:, dd, cols], dd == 0, dd == KD - 1)
                        last.then_inc(S["s_U_ps"], 1)
                if d:
                    need(pe, "s_hid", d[0])
                    need(pe, "s_acc", d[0] - 2, 3)
                    for t in range(TPB):
                        for f in range(FT):
                            n = P if f < FT - 1 else F2
                            last = mm(bank[6 + d[2]][:, bass.ts(t, DM)], s_hd[0:n, f, bass.ts(t, P)],
                                      wsd[0:n, f, :], f == 0, f == FT - 1)
                    last.then_inc(S["s_D_ps"], 1)

            pipeline(pe, NB, [0, 1], shared)

        @block.scalar
        def _(act):
            start(act, "scalar")
            f = nc.scalar.activation
            act.wait_ge(ld_small, 80)
            act.preload_act_table_set("natural_log_exp_and_others")
            f(expA[:], hpar[:, 1, :], ACT.Exp).then_inc(const_act, 1)

            def mamba(a, b, c):
                if b:
                    act.preload_act_table_set("natural_log_exp_and_others")
                    need(act, "b_m", b[0] - 1)
                    for t in range(TPB):
                        need(act, "b_dif", b[0], (t + 1) * NH)
                        f(M[:, t], M[:, t], ACT.Exp).then_inc(S["b_exp"], 1)
                    need(act, "b_small", b[0])
                    need(act, "b_xdt", b[0] - 1)
                    need(act, "b_y", b[0] - 1)
                    f(wleft[:], left[:], ACT.Exp).then_inc(S["b_exp"], 1)
                    f(ecum[:], cum[:, 1, :], ACT.Exp).then_inc(S["b_exp"], 1)
                    need(act, "b_skip", b[0] - 1)
                    for t in range(TPB):
                        need(act, "b_xs_ps", b[0], t + 1)
                        f(xs[:, t], bank[6 + t][:], ACT.Copy).then_inc(S["b_xs"], 1)
                if a:
                    need(act, "a_xT_ps", a[0])
                    need(act, "a_dt_ps", a[0] - 1)
                    f(xT[:].rearrange("p k s -> p (k s)"), bank[0][:], ACT.Copy).then_inc(S["a_xT"], 1)
                if c:
                    need(act, "c_hT_ps", c[0])
                    need(act, "c_lg_ps", c[0] - 1)
                    f(hTb[:].rearrange("p k s -> p (k s)"), bank[0][:], ACT.Copy).then_inc(S["c_hT"], 1)
                    f(hT_all[:, :, bass.ts(c[0], SEQ)], bank[0][:].rearrange("p (k s) -> p k s", k=KD), ACT.Copy
                      ).then_inc(S["c_hT"], 1)
                if a:
                    need(act, "a_act", a[0] - 1)
                    for k in range(CT):
                        if k % 2 == 0:
                            need(act, "a_xbc_ps", a[0], k + 2)
                        f(acc[:, k, :], bank[2 + k // 2][:, bass.ts(k % 2, SEQ)], ACT.Identity,
                          bias=convp[:, k, KW:KW + 1], scale=convp[:, k, KW - 1:KW]).then_inc(S["a_conv0"], 1)
                    need(act, "b_yg", a[0] - 2)
                    for t in range(TPB):
                        need(act, "a_z_ps", a[0], t + 1)
                        f(zs[a[2]][:, t], bank[5 + t][:], ACT.Silu).then_inc(S["a_z"], 1)
                    need(act, "a_conv", a[0])
                    need(act, "b_yo_ps", a[0] - 2)
                    f(xbc[a[2]][:], acc[:], ACT.Silu).then_inc(S["a_act"], 1)
                if b:
                    need(act, "b_st_ps", b[0])
                    need(act, "b_yo_ps", b[0] - 1)
                    f(state[:], bank[0][:], ACT.Copy).then_inc(S["b_st"], 1)
                    need(act, "b_ms", b[0] - 1)
                    for t in range(TPB):
                        need(act, "b_yg", b[0], t + 1)
                        if t:
                            need(act, "b_ss", b[0], t)
                        else:
                            need(act, "b_ss", b[0] - 1)
                        f(junk[:], yg[:, t], ACT.Square, accum_out=ss[:, t:t + 1]).then_inc(S["b_ss"], 1)
                    need(act, "b_out_ps", b[0] - 1)
                    for t in range(TPB):
                        need(act, "b_yT_ps", b[0], t + 1)
                        f(yT[:, t], bank[7 if t == 0 else 1][:], ACT.Copy).then_inc(S["b_yT"], 1)
                act.preload_act_table_set("natural_log_exp_and_others")
                if a:
                    need(act, "a_dtx", a[0])
                    need(act, "a_dt", a[0] - 1)
                    f(dta[:], dtx[:], ACT.Abs).then_inc(S["a_sp"], 1)
                    need(act, "a_sp", a[0], 1)
                    f(dte[:], dta[:], ACT.Exp, scale=-1.0).then_inc(S["a_sp"], 1)
                    need(act, "a_sp", a[0], 2)
                    f(dtl[:], dte[:], ACT.Ln, bias=1.0).then_inc(S["a_sp"], 1)
                if c:
                    need(act, "c_top", c[0], 7)
                    need(act, "c_slot", c[0] - 1)
                    for t in range(TPB):
                        f(e64[:, t], lg[:, t], ACT.Exp, bias=nmx[:, t:t + 1], accum_out=esum[:, t:t + 1]
                          ).then_inc(S["c_exp"], 1)
                        f(e6[:, t], mx[:, t, 0:TOPK], ACT.Exp, bias=nmx[:, t:t + 1]).then_inc(S["c_exp"], 1)

            pipeline(act, NB, [0, 1, 2], mamba)

            phase_a_over(act)
            tails = act.alloc_register("act_tails")
            act.reg_mov(tails, 0)

            def expert(t, g, d):
                if t:
                    need(act, "e_T_ps", t[0], 1)
                    need(act, "e_G_ps", t[0] - 2)
                    f(xgT[t[2]][:, 0, :], bank[0][:], ACT.Copy).then_inc(S["e_xTa"], 1)
                if g:
                    need(act, "e_hid", g[0] - 2)
                    need(act, "e_G_ps", g[0], 1)
                    f(sg[g[2]][:, 0, :], bank[2][:], ACT.Silu).then_inc(S["e_silu"], 1)
                    need(act, "e_G_ps", g[0])
                    f(sg[g[2]][0:F1, 1, :], bank[4][0:F1], ACT.Silu).then_inc(S["e_silu"], 1)
                if d:
                    need(act, "e_D_ps", d[0], 1)
                    wait(act, sc_y[d[2]], d[1] * (MAIN * 16))
                    f(eo[d[2]][:, 0:2, :].rearrange("p j d -> p (j d)"), bank[5][:], ACT.Copy
                      ).then_inc(S["e_eoa"], 1)
                    n = act.value_load(cnt_i[0:1, bass.ds(d[0], 1)])
                    with act.If(n > MR):
                        r = act.snap(tails)
                        for j in range(EXTRA):
                            i = r * EXTRA + j
                            act.wait_ge(t_T_ps, i + 1)
                            f(t_xgT[:].rearrange("p k s -> p (k s)"), bank[7][:, 0:KD * P], ACT.Copy).then_inc(t_xT, 1)
                            act.wait_ge(t_G_ps, i + 1)
                            f(t_sg[:, 0, :], bank[7][:, 0:P], ACT.Silu).then_inc(t_silu, 1)
                            f(t_sg[0:F1, 1, :], bank[7][0:F1, 2 * P:3 * P], ACT.Silu).then_inc(t_silu, 1)
                            act.wait_ge(t_D_ps, i + 1)
                            f(t_out[:], bank[7][:, 0:DM], ACT.Copy).then_inc(t_eo, 1)
                        act.reg_add(tails, tails, 1)
                    act.nop()

            pipeline(act, NE, [1, 2, 3], expert, peel=2)

            def shared(u):
                if u:
                    o = 3 * u[2]
                    need(act, "s_hid", u[0] - 1)
                    need(act, "s_U_ps", u[0], 1)
                    f(s_sg[:, 0:2, :].rearrange("p k s -> p (k s)"), bank[o][:], ACT.Silu).then_inc(S["s_silu"], 1)
                    need(act, "s_U_ps", u[0])
                    f(s_sg[0:F2, 2, :], bank[o + 2][0:F2, 0:SEQ], ACT.Silu).then_inc(S["s_silu"], 1)

            pipeline(act, NB, [0], shared)

        @block.vector
        def _(dve):
            start(dve, "vector")
            v = nc.vector
            dve.wait_ge(const_pool, 4)
            dve.wait_ge(ld_small, 80)
            dve.wait_ge(const_act, 1)
            v.tensor_scalar(negA[:], expA[:], -1.0, None, ALU.mult).then_inc(const_dve, 1)
            v.tensor_copy(Dx[:], hpar[:, 2, :][:, :, None].to_broadcast([P, NH, HD])).then_inc(const_dve, 1)
            for k in range(XT):
                v.tensor_scalar(wo[:, k, :], wo[:, k, :], normw[:, k:k + 1], None, ALU.mult).then_inc(const_dve, 1)
            v.memset(cnt[:], 0.0).then_inc(const_dve, 1)
            v.memset(cnt16[:], 0.0).then_inc(const_dve, 1)
            dve.wait_ge(const_dve, 4 + XT)
            dve.wait_ge(ld_x0, 16)

            def moments(name, n, src, st, mv, ve):
                item, base = name
                hold_dve(base)
                for t in range(TPB):
                    v.bn_stats(out=st[:, t, :], in_=src(t)).then_inc(S[item], 1)
                need(dve, item, base, n + 2)
                hold_dve(base)
                for t in range(TPB):
                    v.bn_aggr(out=mv[:, t, :], in_=st[:, t, :]).then_inc(S[item], 1)
                need(dve, item, base, n + 4)
                v.tensor_scalar(ve[:], mv[:, :, 1], EPS, None, ALU.add).then_inc(S[item], 1)

            def bc(ap, n):
                shape = list(ap.shape) + [n]
                return ap[(slice(None),) * len(ap.shape) + (None,)].to_broadcast(shape)

            def heads(ap):
                return ap.rearrange("p (h d) -> p h d", h=NH)

            def mamba(a, b, c):
                if a:
                    if isinstance(a[0], int) and a[0] == 1:
                        dve.wait_ge(ld_x1, 16)
                    need(dve, "a_rstd", a[0] - 1)
                    need(dve, "a_norm", a[0] - 1)
                    moments(("a_stats", a[0]), 0, lambda t: x_all[:, bass.ts(a[0] * TPB + t, DM)], a_st, a_mv, a_ve)
                if b:
                    need(dve, "b_small_ps", b[0])
                    need(dve, "b_m", b[0] - 1)
                    need(dve, "b_exp", b[0] - 1)
                    need(dve, "b_st_ps", b[0] - 1)
                    v.tensor_tensor(Gm[:], bank[1][:, 0:TPB * P].rearrange("p (t l) -> p t l", t=TPB),
                                    tri[:, None, :].to_broadcast([P, TPB, P]), ALU.mult).then_inc(S["b_small"], 1)
                    v.tensor_copy(cum[:].rearrange("p t h -> p (t h)"), bank[1][:, 256:272]).then_inc(S["b_small"], 1)
                    v.tensor_copy(BT[:], bank[1][:, 384:512]).then_inc(S["b_small"], 1)
                    need(dve, "b_small", b[0], 2)
                    v.tensor_tensor(left[:], bank[1][:, 272:272 + NH], cum[:, 0, :], ALU.subtract
                                    ).then_inc(S["b_small"], 1)
                if a:
                    need(dve, "a_rstd", a[0])
                    need(dve, "a_xT_ps", a[0] - 1)
                    for t in range(TPB):
                        v.tensor_scalar(xn[:, t], x_all[:, bass.ts(a[0] * TPB + t, DM)], a_mv[:, t, 0:1],
                                        a_rs[:, t:t + 1], ALU.subtract, ALU.mult).then_inc(S["a_norm"], 1)
                if b:
                    need(dve, "b_yd_ps", b[0] - 1)
                    for t in range(TPB):
                        need(dve, "b_cum_ps", b[0], t + 1)
                        for hh in range(NH):
                            v.tensor_scalar(M[:, t, hh, :], bank[2 + 2 * t + hh // 4][:, bass.ts(hh % 4, P)],
                                            cum[:, t, hh:hh + 1], 0.0, ALU.subtract, ALU.min
                                            ).then_inc(S["b_dif"], 1)
                    for t in range(TPB):
                        need(dve, "b_xs", b[0], t + 1)
                        v.tensor_tensor(heads(xdt[:, t]), heads(xs[:, t]), bc(dt[b[2]][:, t, :], HD), ALU.mult
                                        ).then_inc(S["b_xdt"], 1)
                    need(dve, "b_exp", b[0], 3)
                    need(dve, "b_xdt", b[0], 1)
                    v.tensor_tensor(heads(xw[:]), heads(xdt[:, 0]), bc(wleft[:], HD), ALU.mult
                                    ).then_inc(S["b_xdt"], 1)
                if a:
                    for s in range(1, KW):
                        for k in range(CT):
                            if s == 1:
                                if k % 2 == 0:
                                    need(dve, "a_conv0", a[0], k + 2)
                            else:
                                need(dve, "a_conv", a[0], (s - 2) * CT + k + 1)
                            v.scalar_tensor_tensor(
                                out=acc[:, k, s:], in0=bank[2 + k // 2][:, k % 2 * SEQ:(k % 2 + 1) * SEQ - s],
                                scalar=convp[:, k, KW - 1 - s:KW - s], in1=acc[:, k, s:],
                                op0=ALU.mult, op1=ALU.add).then_inc(S["a_conv"], 1)
                    need(dve, "a_dt_ps", a[0])
                    need(dve, "a_dt", a[0] - 1)
                    v.tensor_tensor(dtx[:], bank[0][:, 0:TPB * NH].rearrange("p (t h) -> p t h", t=TPB),
                                    hpar[:, 0:1, :].to_broadcast([P, TPB, NH]), ALU.add).then_inc(S["a_dtx"], 1)
                if b:
                    need(dve, "b_skip", b[0])
                    need(dve, "b_yd_ps", b[0], 1)
                    need(dve, "b_yT_ps", b[0] - 1)
                    need(dve, "b_ss", b[0] - 1)
                    v.tensor_tensor(yg[:, 0], bank[7][:], skip[:, 0], ALU.add).then_inc(S["b_y"], 1)
                    need(dve, "b_yo_ps", b[0])
                    need(dve, "b_exp", b[0])
                    v.tensor_tensor(heads(yoff[:]), heads(bank[5][:]), bc(ecum[:], HD), ALU.mult
                                    ).then_inc(S["b_y"], 1)
                    need(dve, "b_y", b[0], 2)
                    v.tensor_tensor(yoff[:], yoff[:], skip[:, 1], ALU.add).then_inc(S["b_y"], 1)
                    need(dve, "b_y", b[0], 3)
                    v.tensor_tensor(yg[:, 1], bank[1][:], yoff[:], ALU.add).then_inc(S["b_y"], 1)
                if c:
                    need(dve, "c_lg_ps", c[0])
                    need(dve, "c_exp", c[0] - 1)
                    need(dve, "c_slot", c[0] - 1)
                    need(dve, "c_pos_ps", c[0] - 1)
                    v.tensor_copy(lg[:].rearrange("p t e -> p (t e)"), bank[6][:, 0:TPB * NE]).then_inc(S["c_top"], 1)
                    need(dve, "c_top", c[0], 1)
                    hold_dve(c[0])
                    for t in range(TPB):
                        v.max(mx[:, t, :], lg[:, t, :]).then_inc(S["c_top"], 1)
                    need(dve, "c_top", c[0], 3)
                    hold_dve(c[0])
                    for t in range(TPB):
                        v.max_index(ix[:, t, :], mx[:, t, :], lg[:, t, :]).then_inc(S["c_top"], 1)
                    v.tensor_scalar(nmx[:], mx[:, :, 0], -1.0, None, ALU.mult).then_inc(S["c_top"], 1)
                    need(dve, "c_top", c[0], 5)
                    v.tensor_copy(ixf[:], ix[:, :, 0:TOPK]).then_inc(S["c_top"], 1)
                    need(dve, "c_top", c[0], 7)
                    v.tensor_tensor(oh[:], iota_e[:, None, None, :].to_broadcast([P, TPB, TOPK, NE]),
                                    bc(ixf[:], NE), ALU.is_equal).then_inc(S["c_top"], 1)
                    need(dve, "c_top", c[0], 8)
                    with nc.allow_low_precision("sums of 0 and 1"):
                        v.tensor_reduce(out=chosen[:], in_=oh[:].rearrange("p t k e -> p t e k"), axis=AX.X,
                                        op=ALU.add).then_inc(S["c_top"], 1)
                if a:
                    need(dve, "a_sp", a[0])
                    need(dve, "b_xdt", a[0] - 2)
                    need(dve, "b_cum_ps", a[0] - 2)
                    v.scalar_tensor_tensor(out=dt[a[2]][:], in0=dtx[:], scalar=0.0, in1=dtl[:], op0=ALU.max,
                                           op1=ALU.add).then_inc(S["a_dt"], 1)
                    need(dve, "a_dt", a[0], 1)
                    v.tensor_tensor(dA[a[2]][:], dt[a[2]][:], negA[:, None, :].to_broadcast([P, TPB, NH]),
                                    ALU.mult).then_inc(S["a_dt"], 1)
                if b:
                    need(dve, "b_ss", b[0])
                    need(dve, "b_rms", b[0] - 1)
                    v.tensor_scalar(ms[:], ss[:], 1.0 / DI, EPS, ALU.mult, ALU.add).then_inc(S["b_ms"], 1)
                if c:
                    def nth(n):
                        need(dve, "c_slot", c[0], n)

                    def done(ins):
                        ins.then_inc(S["c_slot"], 1)

                    need(dve, "c_pos_ps", c[0])
                    done(v.tensor_tensor(sel[:], oh[:], bank[6][:, 2 * NE:4 * NE].rearrange(
                        "p (t e) -> p t e", t=TPB)[:, :, None, :].to_broadcast([P, TPB, TOPK, NE]), ALU.mult))
                    done(v.tensor_tensor(cnt[:], cnt[:], chosen[:, 0, :], ALU.add))
                    nth(1)
                    done(v.tensor_reduce(out=pk[:], in_=sel[:], axis=AX.X, op=ALU.add))
                    nth(2)
                    done(v.tensor_tensor(cnt[:], cnt[:], chosen[:, 1, :], ALU.add))
                    need(dve, "c_exp", c[0])
                    done(v.reciprocal(rsum[:], esum[:]))
                    nth(4)
                    done(v.tensor_copy(cnt16[:], cnt[:]))
                    done(v.scalar_tensor_tensor(out=slot[:], in0=ixf[:], scalar=float(CAP), in1=pk[:],
                                                op0=ALU.mult, op1=ALU.add))
                    done(v.tensor_scalar(over[:], pk[:], float(CAP), float(SKIP), ALU.is_ge, ALU.mult))
                    nth(5)
                    done(v.tensor_tensor(p6[:], e6[:], bc(rsum[:], TOPK), ALU.mult))
                    done(v.tensor_scalar(fits[:], pk[:], float(CAP), None, ALU.is_lt))
                    nth(9)
                    done(v.tensor_reduce(out=s6[:], in_=p6[:], axis=AX.X, op=ALU.add))
                    wait(dve, sc_table[c[2]], c[1] * (TPB * TOPK * 16))
                    done(v.tensor_tensor(slot_i[c[2]][:].rearrange("p (t k) -> p t k", t=TPB), slot[:], over[:],
                                         ALU.add))
                    nth(11)
                    done(v.tensor_scalar(s6e[:], s6[:], 1e-20, None, ALU.add))
                    done(v.tensor_tensor(pay[c[2]][:], pay[1 - c[2]][:], step_pay[:], ALU.add))
                    nth(13)
                    done(v.reciprocal(r6[:], s6e[:]))
                    nth(15)
                    done(v.tensor_tensor(w6[:], p6[:], bc(r6[:], TOPK), ALU.mult))
                    nth(16)
                    done(v.tensor_tensor(w_all[:, bass.ts(c[0], TPB * TOPK)].rearrange("p (t k) -> p t k", t=TPB),
                                         w6[:], fits[:], ALU.mult))
                if b:
                    need(dve, "b_rms", b[0])
                    need(dve, "b_out_ps", b[0])
                    for t in range(TPB):
                        v.tensor_scalar(ao[:, t], bank[5][:, bass.ts(t, DM)], rms[:, t:t + 1], None, ALU.mult
                                        ).then_inc(S["b_ao"], 1)
                    need(dve, "b_ao", b[0], 2)
                    moments(("b_ao", b[0]), 2, lambda t: ao[:, t], b_stt, b_mv, b_ve)
                    need(dve, "b_rs", b[0])
                    for t in range(TPB):
                        v.tensor_scalar(aon[:, t], ao[:, t], b_mv[:, t, 0:1], b_rst[:, t:t + 1],
                                        ALU.subtract, ALU.mult).then_inc(S["b_aon"], 1)
                    need(dve, "b_x1", b[0])
                    moments(("b_h", b[0]), 0, lambda t: x_all[:, bass.ts(b[0] * TPB + t, DM)], h_st, h_mv, h_ve)
                    need(dve, "b_hrs", b[0])
                    need(dve, "c_hT_ps", b[0] - 1)
                    wait(dve, st_h[1 - b[2]], (b[1] + (1 if b[2] == 0 else 2)) * 16)
                    for t in range(TPB):
                        v.tensor_scalar(h[:, t], x_all[:, bass.ts(b[0] * TPB + t, DM)], h_mv[:, t, 0:1],
                                        h_rst[:, t:t + 1], ALU.subtract, ALU.mult).then_inc(S["b_hn"], 1)

            pipeline(dve, NB, [0, 1, 2], mamba, peel=2)
            dve.wait_ge(cnt_ps, 1)
            v.tensor_copy(cnt_i[:, 0:NE], bank[0][:, 0:NE]).then_inc(cnt_sb, 1)
            v.tensor_reduce(out=cnt[:, 0:1], in_=bank[0][:, 0:NE], axis=AX.X, op=ALU.max).then_inc(cnt_sb, 1)
            dve.wait_ge(cnt_sb, 2)
            v.tensor_copy(cnt_i[:, NE:NE + 1], cnt[:, 0:1]).then_inc(cnt_sb, 1)

            phase_a_over(dve)
            dve.wait_ge(tab_ps, 2 * NQ)
            for q in range(NQ):
                v.tensor_copy(tok_idx[:, bass.ts(q, P)], bank[0][:, bass.ts(q, P)]).then_inc(tab_sb, 1)
                v.tensor_copy(row_idx[:, bass.ts(q, P)], bank[1][:, bass.ts(q, P)]).then_inc(tab_sb, 1)
            dve.wait_ge(const_pool, 5)
            tails = dve.alloc_register("dve_tails")
            dve.reg_mov(tails, 0)

            def expert(t, g, d):
                if t:
                    need(dve, "e_T_ps", t[0])
                    need(dve, "e_G_ps", t[0] - 2)
                    v.tensor_copy(xgT[t[2]][:, 1, :], bank[1][:]).then_inc(S["e_xTv"], 1)
                if g:
                    need(dve, "e_D_ps", g[0] - 2)
                    need(dve, "e_G_ps", g[0])
                    need(dve, "e_silu", g[0], 1)
                    v.tensor_tensor(hid[g[2]][:, 0, :], sg[g[2]][:, 0, :], bank[3][:], ALU.mult
                                    ).then_inc(S["e_hid"], 1)
                    need(dve, "e_silu", g[0])
                    v.tensor_tensor(hid[g[2]][0:F1, 1, :], sg[g[2]][0:F1, 1, :], bank[4][UO:UO + F1], ALU.mult
                                    ).then_inc(S["e_hid"], 1)
                if d:
                    need(dve, "e_D_ps", d[0])
                    wait(dve, sc_y[d[2]], d[1] * (MAIN * 16))
                    v.tensor_copy(eo[d[2]][:, 2:4, :].rearrange("p j d -> p (j d)"), bank[6][:]
                                  ).then_inc(S["e_eov"], 1)
                    n = dve.value_load(cnt_i[0:1, bass.ds(d[0], 1)])
                    with dve.If(n > MR):
                        r = dve.snap(tails)
                        for j in range(EXTRA):
                            i = r * EXTRA + j
                            dve.wait_ge(t_silu, (i + 1) * 2)
                            v.tensor_tensor(t_hd[:, 0, :], t_sg[:, 0, :], bank[7][:, P:2 * P], ALU.mult
                                            ).then_inc(t_hid, 1)
                            v.tensor_tensor(t_hd[0:F1, 1, :], t_sg[0:F1, 1, :], bank[7][UO:UO + F1, 2 * P:3 * P],
                                            ALU.mult).then_inc(t_hid, 1)
                        dve.reg_add(tails, tails, 1)
                    dve.nop()

            pipeline(dve, NE, [1, 2, 3], expert, peel=2)

            def shared(u, d):
                if u:
                    o = 3 * u[2]
                    need(dve, "s_D_ps", u[0] - 1)
                    need(dve, "s_U_ps", u[0])
                    need(dve, "s_silu", u[0])
                    v.tensor_tensor(s_hd[:, 0:2, :].rearrange("p k s -> p (k s)"),
                                    s_sg[:, 0:2, :].rearrange("p k s -> p (k s)"), bank[o + 1][:], ALU.mult
                                    ).then_inc(S["s_hid"], 1)
                    v.tensor_tensor(s_hd[0:F2, 2, :], s_sg[0:F2, 2, :], bank[o + 2][0:F2, SEQ:2 * SEQ], ALU.mult
                                    ).then_inc(S["s_hid"], 1)
                if d:
                    def nth(n):
                        need(dve, "s_acc", d[0], n)

                    def done(ins):
                        ins.then_inc(S["s_acc"], 1)

                    need(dve, "s_acc", d[0] - 1)
                    done(v.tensor_copy(wb[:].rearrange("p t k -> p (t k)"),
                                       w_all[:, bass.ts(d[0], TPB * TOPK)]))
                    nth(1)
                    wait(dve, ld_y[d[2]], (d[1] + 1) * 16)
                    need(dve, "s_D_ps", d[0])
                    for k in range(TOPK):
                        for t in range(TPB):
                            if k:
                                nth(2 * k + t)
                            prev = cacc[:, t] if k else bank[6 + d[2]][:, bass.ts(t, DM)]
                            done(v.scalar_tensor_tensor(out=cacc[:, t], in0=yb[d[2]][:, t, k, :],
                                                        scalar=wb[:, t, k:k + 1], in1=prev,
                                                        op0=ALU.mult, op1=ALU.add))
                    nth(13)
                    moments(("s_acc", d[0]), 13, lambda t: cacc[:, t], c_st, c_mv, c_ve)
                    need(dve, "s_rs", d[0])
                    need(dve, "s_out", d[0] - 1)
                    for t in range(TPB):
                        done(v.tensor_scalar(cn[:, t], cacc[:, t], c_mv[:, t, 0:1], c_rs[:, t:t + 1],
                                             ALU.subtract, ALU.mult))

            pipeline(dve, NB, [0, 1], shared)


def kernel(**inputs):
    import concourse.bacc as bacc
    from concourse.bass_utils import run_bass_kernel_spmd

    g = {n.removeprefix("L0_"): np.asarray(a) for n, a in inputs.items()}

    def on_partitions(a):
        return np.ascontiguousarray(a.reshape(-1, P, a.shape[-1]).transpose(1, 0, 2))

    gate_t, up_t, down_t = (g[n].transpose(0, 2, 1) for n in ("ffn_w_gate", "ffn_w_up", "ffn_w_down"))
    gu = np.zeros((NE, DM, GW), np.float32)
    gu[:, :, 0:P], gu[:, :, P:2 * P] = gate_t[:, :, 0:P], up_t[:, :, 0:P]
    gu[:, :, 2 * P:2 * P + F1], gu[:, :, 2 * P + UO:] = gate_t[:, :, P:], up_t[:, :, P:]
    gu = gu.reshape(NE, KD, P, GW).transpose(0, 2, 1, 3).reshape(NE, P, KD * GW)
    sd = np.zeros((FT * P, DM), np.float32)
    sd[:FS] = g["ffn_sh_down"].T
    arrays = dict(
        x=np.ascontiguousarray(g["attn_x"].reshape(NT, DM)),
        win=on_partitions(g["attn_in_proj_w"].T),
        wo=on_partitions(g["attn_out_proj_w"].T),
        convp=on_partitions(np.concatenate([g["attn_conv_w"], g["attn_conv_b"][:, None]], axis=1)),
        normw=np.ascontiguousarray(g["attn_norm_w"].reshape(XT, P).T),
        hpar=np.stack([g["attn_dt_bias"], g["attn_A_log"], g["attn_D"]]),
        wg=on_partitions(g["ffn_gate_w"].T),
        wsu=on_partitions(np.concatenate([g["ffn_sh_gate"].T, g["ffn_sh_up"].T], axis=1)),
        wsd=on_partitions(sd),
        we=np.ascontiguousarray(np.concatenate([gu, down_t[:, 0:P, :]], axis=2).reshape(NE * P, -1)),
        we1=np.ascontiguousarray(down_t[:, P:, :].reshape(NE * F1, DM)),
    )
    nc = bacc.Bacc("TRN2", target_bir_lowering=False, num_devices=1)
    T = {n: nc.dram_tensor("in_" + n, a.shape, mybir.dt.from_np(a.dtype), kind="ExternalInput").ap()
         for n, a in arrays.items()}
    T["out"] = nc.dram_tensor("out", (NT, DM), FP32, kind="ExternalOutput").ap()
    build(nc, T)
    r = run_bass_kernel_spmd(nc, [{"in_" + n: a for n, a in arrays.items()}], core_ids=[0])
    return r.results[0]["out"].reshape(NB, SEQ, DM)
```

```python
from contextlib import ExitStack

import numpy as np
import concourse.bass as bass
from concourse import mybir

FP32 = mybir.dt.float32
BF16 = mybir.dt.bfloat16
I32 = mybir.dt.int32
U32 = mybir.dt.uint32
ALU = mybir.AluOpType
ACT = mybir.ActivationFunctionType
AX = mybir.AxisListType

P = 128
NB, SEQ, DM = 16, 256, 256
NT = NB * SEQ
TPB = SEQ // P
KD = DM // P
DI, DS, NH, HD, KW = 512, 128, 8, 64, 4
CD = DI + 2 * DS
CT = CD // P
XT = DI // P
CB, CC = XT, XT + 1
DIN = 2 * DI + 2 * DS + NH
NE, TOPK, FE, FS = 64, 6, 176, 352
CAP = 2 * ((NT * TOPK + NE - 1) // NE)
CAPT = CAP // P
MAIN = 4
MR = MAIN * P
EXTRA = CAPT - MAIN
F1 = FE - P
UO = 64
GW = 2 * P + UO + F1
FT = (FS + P - 1) // P
F2 = FS - (FT - 1) * P
NSLOT = NE * CAP
NQ = NE * CAPT // P
SKIP = 1 << 20
EPS = 1e-5
LOW = -1e30

PER = dict(
    tensor=dict(a_xT_ps=1, a_xbc_ps=CT // 2, a_z_ps=TPB, a_dt_ps=1,
                b_small_ps=1, b_cum_ps=TPB, b_xs_ps=TPB, b_st_ps=1, b_yd_ps=TPB, b_yo_ps=1,
                d_yT_ps=TPB, d_out_ps=1, c_hT_ps=1, c_lg_ps=1, p_pos_ps=1,
                e_T_ps=KD, e_G_ps=3, e_tail=1, e_D_ps=2, s_U_ps=3, s_D_ps=1),
    scalar=dict(a_xT=1, a_conv0=CT, a_act=1, a_z=TPB, a_sp=3,
                b_edge=2, b_exp=TPB * NH, b_xs=TPB, b_st=1, d_ss=TPB, d_yT=TPB, c_hT=2, p_exp=2 * TPB,
                e_xTa=1, e_silu=2, e_eoa=1, s_silu=2),
    vector=dict(n_stats=5, n_norm=TPB, a_conv=(KW - 1) * CT, a_dtx=1, a_dt=2,
                b_small=4, b_xdt=3, b_m1=1, b_y=4, d_ms=1, d_ao=7, d_aon=TPB, d_h=5, d_hn=TPB,
                c_top=9, p_slot=17, e_xTv=1, e_hid=2, e_eov=1, s_hid=2, s_acc=20),
    gpsimd=dict(n_rstd=1, b_m0=1, b_skip=TPB, b_yg=TPB, d_rms=1, d_rs=1, d_x1=TPB, d_hrs=1,
                e_gidx=1, e_sidx=1, s_rs=1, s_out=TPB),
)
ROUND = {name: k for per in PER.values() for name, k in per.items()}
CREDIT = 2


def build(nc, T):
    ctx = ExitStack()
    with ctx:
        def sb(name, shape, dt=FP32, stack=ctx):
            return stack.enter_context(nc.sbuf_tensor(name, shape, dt))

        def sem(name):
            return ctx.enter_context(nc.semaphore(name))

        def pair(name):
            return [sem(name + "0"), sem(name + "1")]

        S = {name: sem(name) for name in ROUND}
        ld_x0, ld_x1, ld_w, ld_small, ld_c = (sem("ld_" + n) for n in "x0 x1 w small c".split())
        st_table, st_h, ld_table = sem("st_table"), pair("st_h"), sem("ld_table")
        sc_table, ld_gu, ld_dn, ga_x, sc_y, ld_y, st_out = (
            pair(n) for n in "sc_table ld_gu ld_dn ga_x sc_y ld_y st_out".split())
        const_pool, const_dve, const_act = sem("const_pool"), sem("const_dve"), sem("const_act")
        tick_sp, tick_pool, tick_dve = sem("tick_sp"), sem("tick_pool"), sem("tick_dve")
        cnt_ps, cnt_sb, tab_ps, tab_sb = sem("cnt_ps"), sem("cnt_sb"), sem("tab_ps"), sem("tab_sb")
        y_zero, y_ready = sem("y_zero"), sem("y_ready")
        t_idx, t_ga, t_T_ps, t_xT, t_G_ps, t_silu, t_hid, t_D_ps, t_eo, t_sc = (
            sem("t_" + n) for n in "idx ga T_ps xT G_ps silu hid D_ps eo sc".split())

        x_all = sb("x_all", [P, NT // P * DM])
        hT_all = sb("hT_all", [P, KD, NT])
        w_all = sb("w_all", [P, NT // P * TOPK])
        ident = sb("ident", [P, P])
        ones = sb("ones", [P, P])
        neghalf = sb("neghalf", [P, TPB])
        zero_row = sb("zero_row", [P, DM])
        wsu = sb("wsu", [P, KD, 2 * FS])
        wsd = sb("wsd", [P, FT, DM])
        cnt_i = sb("cnt_i", [P, NE + 1], I32)
        we = [sb(f"we{i}", [P, KD * GW + DM]) for i in range(2)]
        we1 = [sb(f"we1{i}", [P, DM]) for i in range(2)]
        tok_idx = sb("tok_idx", [P, NE * CAPT], I32)
        row_idx = sb("row_idx", [P, NE * CAPT], I32)

        pa = ExitStack()

        def sa(name, shape, dt=FP32):
            return sb(name, shape, dt, pa)

        tri = sa("tri", [P, P])
        tri_strict = sa("tri_strict", [P, P], BF16)
        ones16 = sa("ones16", [P, P], BF16)
        ident16 = sa("ident16", [P, P], BF16)
        mask4 = sa("mask4", [P, NH // 2 * P], BF16)
        cnt = sa("cnt", [P, NE])
        cnt16 = sa("cnt16", [P, NE], BF16)
        win = sa("win", [P, KD, DIN])
        wo = sa("wo", [P, XT, DM])
        wg = sa("wg", [P, KD, NE])
        convp = sa("convp", [P, CT, KW + 1])
        normw = sa("normw", [P, XT])
        hpar = sa("hpar", [P, 3, NH])
        expA = sa("expA", [P, NH])
        negA = sa("negA", [P, NH])
        Dx = sa("Dx", [P, NH, HD])
        iota_e = sa("iota_e", [P, NE])
        table0 = sa("table0", [P, NSLOT // P, 2])
        pay = [sa(f"pay{i}", [P, TPB * TOPK, 2]) for i in range(2)]
        step_pay = sa("step_pay", [P, TPB * TOPK, 2])
        a_st, a_mv, a_ve, a_rs = sa("a_st", [P, TPB, 6]), sa("a_mv", [P, TPB, 2]), sa("a_ve", [P, TPB]), sa("a_rs", [P, TPB])
        xn = sa("xn", [P, TPB, DM])
        xT = sa("xT", [P, KD, SEQ])
        acc = sa("acc", [P, CT, SEQ])
        xbc = [sa(f"xbc{i}", [P, CT, SEQ]) for i in range(2)]
        zs = [sa(f"zs{i}", [P, TPB, DI]) for i in range(2)]
        dtx, dta, dte, dtl = (sa(n, [P, TPB, NH]) for n in "dtx dta dte dtl".split())
        dt = [sa(f"dt{i}", [P, TPB, NH]) for i in range(2)]
        dA = [sa(f"dA{i}", [P, TPB, NH]) for i in range(2)]
        Gm = sa("Gm", [P, TPB, P])
        ncum = sa("ncum", [P, TPB, NH])
        left = sa("left", [P, NH])
        BT = sa("BT", [P, P])
        M = sa("M", [P, TPB, NH, P])
        xs, xdt, skip, yg, yT = (sa(n, [P, TPB, DI]) for n in "xs xdt skip yg yT".split())
        xw, state, yoff, junk = (sa(n, [P, DI]) for n in "xw state yoff junk".split())
        wleft, ecum = sa("wleft", [P, NH]), sa("ecum", [P, NH])
        ss, ms, rms = (sa(n, [P, TPB]) for n in "ss ms rms".split())
        ao, aon, h = (sa(n, [P, TPB, DM]) for n in "ao aon h".split())
        b_stt, b_mv, b_ve, b_rst = sa("b_stt", [P, TPB, 6]), sa("b_mv", [P, TPB, 2]), sa("b_ve", [P, TPB]), sa("b_rst", [P, TPB])
        h_st, h_mv, h_ve, h_rst = sa("h_st", [P, TPB, 6]), sa("h_mv", [P, TPB, 2]), sa("h_ve", [P, TPB]), sa("h_rst", [P, TPB])
        hTb = sa("hTb", [P, KD, SEQ])
        lg = sa("lg", [P, TPB, NE])
        mx = sa("mx", [P, TPB, 8])
        ix = sa("ix", [P, TPB, 8], U32)
        nmx, esum, rsum, s6, s6e, r6 = (sa(n, [P, TPB]) for n in "nmx esum rsum s6 s6e r6".split())
        e64 = sa("e64", [P, TPB, NE])
        ixf, e6, pk, slot, over, fits, p6, w6 = (
            sa(n, [P, TPB, TOPK]) for n in "ixf e6 pk slot over fits p6 w6".split())
        oh = sa("oh", [P, TPB, TOPK, NE])
        sel = sa("sel", [P, TPB, TOPK, NE])
        chosen = sa("chosen", [P, TPB, NE], BF16)
        slot_i = [sa(f"slot_i{i}", [P, TPB * TOPK], I32) for i in range(2)]
        pa.close()

        pb = ExitStack()

        def sbb(name, shape, dt=FP32):
            return sb(name, shape, dt, pb)

        tab = sbb("tab", [P, NQ, P, 2])
        xg = [sbb(f"xg{i}", [P, MAIN, DM]) for i in range(2)]
        xgT = [sbb(f"xgT{i}", [P, KD, MR]) for i in range(2)]
        g_idx = [sbb(f"g_idx{i}", [P, MAIN], I32) for i in range(2)]
        s_idx = [sbb(f"s_idx{i}", [P, MAIN], I32) for i in range(2)]
        sg = [sbb(f"sg{i}", [P, 2, MR]) for i in range(2)]
        hid = [sbb(f"hid{i}", [P, 2, MR]) for i in range(2)]
        eo = [sbb(f"eo{i}", [P, MAIN, DM]) for i in range(2)]
        t_xg, t_out = sbb("t_xg", [P, DM]), sbb("t_out", [P, DM])
        t_xgT, t_sg, t_hd = (sbb(n, [P, 2, P]) for n in "t_xgT t_sg t_hd".split())
        t_i = sbb("t_i", [P, 2], I32)
        s_sg, s_hd = sbb("s_sg", [P, FT, SEQ]), sbb("s_hd", [P, FT, SEQ])
        yb = [sbb(f"yb{i}", [P, TPB, TOPK, DM]) for i in range(2)]
        wb = sbb("wb", [P, TPB, TOPK])
        cacc, cn = sbb("cacc", [P, TPB, DM]), sbb("cn", [P, TPB, DM])
        c_st, c_mv, c_ve, c_rs = sbb("c_st", [P, TPB, 6]), sbb("c_mv", [P, TPB, 2]), sbb("c_ve", [P, TPB]), sbb("c_rs", [P, TPB])
        fin = [sbb(f"fin{i}", [P, TPB, DM]) for i in range(2)]
        pb.close()

        bank = [ctx.enter_context(nc.psum_tensor(f"bank{i}", [P, 512], FP32)) for i in range(8)]

        h_dram = nc.dram_tensor("h_rows", [NT, DM], FP32, kind="Internal").ap()
        table = nc.dram_tensor("slot_table", [NSLOT, 2], FP32, kind="Internal").ap()
        y_rows = nc.dram_tensor("y_rows", [NT * TOPK, DM], FP32, kind="Internal").ap()

        def start(eng, which):
            for name, k in PER[which].items():
                eng.sem_inc(S[name], CREDIT * k)

        def hold(eng):
            if eng is nc.gpsimd:
                eng.sem_inc(tick_pool, 1)
            elif eng is nc.sync:
                eng.sem_inc(tick_sp, 1)

        def hold_dve(i):
            if not isinstance(i, int):
                nc.vector.sem_inc(tick_dve, 1)

        def wait(eng, s, value):
            if isinstance(value, int) and value == 0:
                return
            eng.wait_ge(s, value)
            if not isinstance(value, int):
                hold(eng)

        def need(eng, name, i, n=None):
            if isinstance(i, int):
                if i < 0:
                    return
                if name[0] in "nabdcp":
                    i = min(i, NB - 1)
            k = ROUND[name]
            wait(eng, S[name], i * k + ((k if n is None else n) + CREDIT * k))

        def pipeline(eng, items, lags, work, peel=0):
            lo = max(lags) + max(lags) % 2 + peel
            hi = items + min(lags)
            hi -= (hi - lo) % 2

            def at(m, par, n=None):
                out = []
                for lag in lags:
                    q = par - lag
                    on = n is None or 0 <= n - lag < items
                    out.append((m * 2 + q, m + q // 2, q % 2) if on else None)
                return out

            for n in range(min(lags), lo):
                work(*at(n // 2, n % 2, n))
            with eng.Fori(lo // 2, hi // 2) as m:
                for par in range(2):
                    work(*at(m, par))
            for n in range(hi, items + max(lags)):
                work(*at(n // 2, n % 2, n))

        def phase_a_over(eng):
            eng.wait_ge(cnt_sb, 3)
            for q in range(2):
                eng.wait_ge(sc_table[q], NB // 2 * TPB * TOPK * 16)
                eng.wait_ge(st_h[q], (NB // 2 + 1) * 16)

        block = ctx.enter_context(nc.Block())

        @block.sync
        def _(sp):
            for q in range(2):
                sp.sem_inc(st_h[q], 16)
            sp.dma_start(x_all[:, 0:TPB * DM].rearrange("p (t d) -> p t d", d=DM),
                         T["x"][0:SEQ].rearrange("(t p) d -> p t d", p=P)).then_inc(ld_x0, 16)
            sp.dma_start(hpar[:], T["hpar"][None, :, :].to_broadcast([P, 3, NH])).then_inc(ld_small, 16)
            sp.dma_start(convp[:], T["convp"]).then_inc(ld_small, 16)
            sp.dma_start(normw[:], T["normw"]).then_inc(ld_small, 16)
            sp.dma_start(wo[:], T["wo"]).then_inc(ld_small, 16)
            sp.dma_start(wg[:], T["wg"]).then_inc(ld_small, 16)
            sp.dma_start(win[:], T["win"]).then_inc(ld_w, 16)
            sp.dma_start(x_all[:, TPB * DM:].rearrange("p (t d) -> p t d", d=DM),
                         T["x"][SEQ:].rearrange("(t p) d -> p t d", p=P)).then_inc(ld_x1, 16)
            sp.dma_start(wsu[:], T["wsu"]).then_inc(ld_c, 16)
            sp.dma_start(wsd[:], T["wsd"]).then_inc(ld_c, 16)
            sp.wait_ge(const_pool, 2)
            sp.dma_start(table.rearrange("(p s) c -> p s c", p=P), table0[:]).then_inc(st_table, 16)

            def load_gate_up(e, m, par):
                need(sp, "e_G_ps", e - 2)
                need(sp, "e_tail", e - 2)
                sp.dma_start(we[par][:, 0:KD * GW], T["we"][bass.ts(e, P), 0:KD * GW]).then_inc(ld_gu[par], 16)

            def load_down(e, m, par):
                need(sp, "e_D_ps", e - 2)
                need(sp, "e_tail", e - 2)
                sp.dma_start(we[par][:, KD * GW:], T["we"][bass.ts(e, P), KD * GW:]).then_inc(ld_dn[par], 16)
                sp.dma_start(we1[par][0:F1, :], T["we1"][bass.ts(e, F1), :]).then_inc(ld_dn[par], 16)

            for e in range(2):
                load_gate_up(e, 0, e)
                load_down(e, 0, e)

            def store_h(b):
                if b:
                    need(sp, "d_hn", b[0])
                    sp.dma_start(h_dram[bass.ts(b[0], SEQ), :].rearrange("(t p) d -> p t d", p=P), h[:]
                                 ).then_inc(st_h[b[2]], 16)

            pipeline(sp, NB, [3], store_h)
            phase_a_over(sp)
            sp.dma_start(tab[:], table.rearrange("(q g s) c -> g q s c", g=P, s=P)).then_inc(ld_table, 16)
            most = sp.value_load(cnt_i[0:1, NE:NE + 1])
            with sp.If(most > CAP):
                sp.dma_start(y_rows.rearrange("(p r) d -> p r d", p=P),
                             zero_row[:, None, :].to_broadcast([P, NT * TOPK // P, DM])).then_inc(y_zero, 16)
                sp.wait_ge(y_zero, 16)
                sp.sem_inc(tick_sp, 1)
            sp.sem_inc(y_ready, 1)

            load_gate_up(2, 1, 0)
            load_gate_up(3, 1, 1)
            load_down(2, 1, 0)
            with sp.Fori(2, NE // 2) as m:
                for par in range(2):
                    load_gate_up(m * 2 + par, m, par)
                    load_down(m * 2 + par - 1, m - 1 + par, 1 - par)
            load_down(NE - 1, NE // 2 - 1, 1)

            def load_y(b, m, par):
                need(sp, "s_acc", b - 2, 12)
                sp.dma_start(yb[par][:], y_rows[bass.ts(b, SEQ * TOPK), :].rearrange(
                    "(t p k) d -> p t k d", p=P, k=TOPK)).then_inc(ld_y[par], 16)

            def store_out(b, m, par):
                need(sp, "s_out", b)
                sp.dma_start(T["out"][bass.ts(b, SEQ), :].rearrange("(t p) d -> p t d", p=P), fin[par][:]
                             ).then_inc(st_out[par], 16)

            for q in range(2):
                sp.wait_ge(sc_y[q], NE // 2 * MAIN * 16)
            sp.wait_ge(y_ready, 1)
            sp.wait_ge(const_pool, 6)
            load_y(0, 0, 0)
            load_y(1, 0, 1)
            with sp.Fori(1, NB // 2) as m:
                for par in range(2):
                    store_out(m * 2 + par - 2, m - 1, par)
                    load_y(m * 2 + par, m, par)
            for b in range(NB - 2, NB):
                store_out(b, b // 2, b % 2)
            for q in range(2):
                sp.wait_ge(st_out[q], (NB // 2 + 1) * 16)

        @block.gpsimd
        def _(pool):
            start(pool, "gpsimd")
            for q in range(2):
                pool.sem_inc(st_out[q], 16)
            pool.memset(table0[:, :, 0:1], 0.0)
            pool.memset(table0[:, :, 1:2], float(SKIP)).then_inc(const_pool, 1)
            pool.memset(we1[0][:], 0.0)
            pool.memset(we1[1][:], 0.0).then_inc(const_pool, 1)
            pool.memset(ident[:], 0.0)
            pool.memset(ones[:], 1.0)
            pool.memset(neghalf[:], -0.5)
            pool.memset(zero_row[:], 0.0)
            pool.memset(step_pay[:, :, 0:1], float(SEQ))
            pool.memset(step_pay[:, :, 1:2], float(SEQ * TOPK))
            pool.memset(mask4[:], 0.0)
            pool.memset(ones16[:], 1.0).then_inc(const_pool, 1)
            pool.wait_ge(const_pool, 3)
            pool.affine_select(out=ident[:], in_=ident[:], compare_op=ALU.not_equal, fill=1.0, base=0,
                               pattern=[[-1, P]], channel_multiplier=1)
            pool.affine_select(out=tri[:], in_=ones[:], compare_op=ALU.is_ge, fill=0.0, base=0,
                               pattern=[[1, P]], channel_multiplier=-1)
            pool.affine_select(out=ident16[:], in_=ones[:], compare_op=ALU.is_equal, fill=0.0, base=0,
                               pattern=[[-1, P]], channel_multiplier=1)
            pool.affine_select(out=mask4[:].rearrange("p (h l) -> p h l", h=NH // 2),
                               in_=mask4[:].rearrange("p (h l) -> p h l", h=NH // 2), compare_op=ALU.is_ge,
                               fill=LOW, base=0, pattern=[[0, NH // 2], [1, P]], channel_multiplier=-1)
            pool.affine_select(out=tri_strict[:], in_=ones[:], compare_op=ALU.is_gt, fill=0.0, base=0,
                               pattern=[[1, P]], channel_multiplier=-1)
            pool.iota(iota_e[:], pattern=[[1, NE]], base=0, channel_multiplier=0,
                      allow_small_or_imprecise_dtypes=True)
            pool.iota(pay[1][:, :, 0].rearrange("p (t k) -> p t k", t=TPB), pattern=[[P, TPB], [0, TOPK]],
                      base=-SEQ, channel_multiplier=1, allow_small_or_imprecise_dtypes=True)
            pool.iota(pay[1][:, :, 1].rearrange("p (t k) -> p t k", t=TPB),
                      pattern=[[P * TOPK, TPB], [1, TOPK]], base=-SEQ * TOPK, channel_multiplier=TOPK,
                      allow_small_or_imprecise_dtypes=True).then_inc(const_pool, 1)
            pool.wait_ge(const_dve, 3)
            pool.wait_ge(st_table, 16)

            def scatter_slots(f, part):
                for k in range(part * 3, part * 3 + 3):
                    pool.indirect_dma_start(
                        table, bass.IndirectOffsetOnAxis(ap=slot_i[f[2]][:, k:k + 1], axis=0),
                        pay[f[2]][:, k, :], None, bounds_check=NSLOT - 1, oob_is_err=False
                    ).then_inc(sc_table[f[2]], 16)

            def rows(n, b, d, f):
                if f:
                    need(pool, "p_slot", f[0])
                    scatter_slots(f, 0)
                if n:
                    need(pool, "n_stats", n[0])
                    need(pool, "n_norm", n[0] - 1)
                    pool.tensor_tensor(a_rs[:], a_ve[:], neghalf[:], ALU.pow).then_inc(S["n_rstd"], 1)
                if f:
                    scatter_slots(f, 1)
                if d:
                    need(pool, "d_ms", d[0])
                    pool.tensor_tensor(rms[:], ms[:], neghalf[:], ALU.pow).then_inc(S["d_rms"], 1)
                if b:
                    need(pool, "b_small", b[0])
                    need(pool, "b_exp", b[0], NH)
                    pool.tensor_tensor(M[:, 0], M[:, 0], Gm[:, 0:1, :].to_broadcast([P, NH, P]), ALU.mult
                                       ).then_inc(S["b_m0"], 1)
                if f:
                    scatter_slots(f, 2)
                if b:
                    need(pool, "b_y", b[0] - 1)
                    for t in range(TPB):
                        need(pool, "b_xs", b[0], t + 1)
                        pool.tensor_tensor(skip[:, t], xs[:, t], Dx[:].rearrange("p h d -> p (h d)"), ALU.mult
                                           ).then_inc(S["b_skip"], 1)
                if d:
                    need(pool, "d_ao", d[0])
                    pool.tensor_tensor(b_rst[:], b_ve[:], neghalf[:], ALU.pow).then_inc(S["d_rs"], 1)
                    for t in range(TPB):
                        need(pool, "d_aon", d[0], t + 1)
                        xrow = x_all[:, bass.ts(d[0] * TPB + t, DM)]
                        pool.tensor_tensor(xrow, xrow, aon[:, t], ALU.add).then_inc(S["d_x1"], 1)
                    need(pool, "d_h", d[0])
                    pool.tensor_tensor(h_rst[:], h_ve[:], neghalf[:], ALU.pow).then_inc(S["d_hrs"], 1)
                if f:
                    scatter_slots(f, 3)
                if b:
                    for t in range(TPB):
                        need(pool, "b_y", b[0], 1 if t == 0 else 4)
                        pool.tensor_tensor(yg[:, t], yg[:, t], zs[b[2]][:, t], ALU.mult).then_inc(S["b_yg"], 1)

            pipeline(pool, NB, [0, 2, 3, 6], rows)

            phase_a_over(pool)
            for i in range(2):
                pool.memset(hid[i][:], 0.0)
            pool.memset(t_hd[:], 0.0).then_inc(const_pool, 1)
            pool.wait_ge(tab_sb, 2 * NQ)
            pool.wait_ge(y_ready, 1)
            tails = pool.alloc_register("pool_tails")
            pool.reg_mov(tails, 0)

            def gather(e, m, par):
                need(pool, "e_T_ps", e - 2)
                wait(pool, ga_x[par], m * (MAIN * 16))
                pool.tensor_copy(g_idx[par][:], tok_idx[:, bass.ds(e * CAPT, MAIN)]).then_inc(S["e_gidx"], 1)
                need(pool, "e_gidx", e)
                for j in range(MAIN):
                    pool.indirect_dma_start(
                        xg[par][:, j, :], None, h_dram,
                        bass.IndirectOffsetOnAxis(ap=g_idx[par][:, j:j + 1], axis=0),
                        bounds_check=NT - 1, oob_is_err=False).then_inc(ga_x[par], 16)

            def scatter(e, m, par):
                wait(pool, sc_y[par], m * (MAIN * 16))
                pool.tensor_copy(s_idx[par][:], row_idx[:, bass.ds(e * CAPT, MAIN)]).then_inc(S["e_sidx"], 1)
                need(pool, "e_sidx", e)
                need(pool, "e_eoa", e)
                need(pool, "e_eov", e)
                for j in range(MAIN):
                    pool.indirect_dma_start(
                        y_rows, bass.IndirectOffsetOnAxis(ap=s_idx[par][:, j:j + 1], axis=0),
                        eo[par][:, j, :], None, bounds_check=NT * TOPK - 1, oob_is_err=False
                    ).then_inc(sc_y[par], 16)

            def tail(e):
                n = pool.value_load(cnt_i[0:1, bass.ds(e, 1)])
                with pool.If(n > MR):
                    r = pool.snap(tails)
                    for j in range(EXTRA):
                        i = r * EXTRA + j
                        if j:
                            wait(pool, t_sc, i * 16)
                        pool.tensor_copy(t_i[:, 0:1], tok_idx[:, bass.ds(e * CAPT + (MAIN + j), 1)])
                        pool.tensor_copy(t_i[:, 1:2], row_idx[:, bass.ds(e * CAPT + (MAIN + j), 1)]).then_inc(t_idx, 1)
                        wait(pool, t_idx, i + 1)
                        pool.indirect_dma_start(t_xg[:], None, h_dram,
                                                bass.IndirectOffsetOnAxis(ap=t_i[:, 0:1], axis=0),
                                                bounds_check=NT - 1, oob_is_err=False).then_inc(t_ga, 16)
                        wait(pool, t_eo, i + 1)
                        pool.indirect_dma_start(y_rows, bass.IndirectOffsetOnAxis(ap=t_i[:, 1:2], axis=0),
                                                t_out[:], None, bounds_check=NT * TOPK - 1, oob_is_err=False
                                                ).then_inc(t_sc, 16)
                    wait(pool, t_sc, (r * EXTRA + EXTRA) * 16)
                    pool.reg_add(tails, tails, 1)
                pool.sem_inc(tick_pool, 1)

            def expert_rows(g, t, d):
                if d:
                    scatter(*d)
                if g:
                    gather(*g)
                if t:
                    tail(t[0])

            pipeline(pool, NE, [0, 3, 5], expert_rows, peel=2)
            pool.sem_inc(const_pool, 1)

            def finish(b):
                if b:
                    need(pool, "s_acc", b[0], 18)
                    pool.tensor_tensor(c_rs[:], c_ve[:], neghalf[:], ALU.pow).then_inc(S["s_rs"], 1)
                    wait(pool, st_out[b[2]], (b[1] + 1) * 16)
                    for t in range(TPB):
                        need(pool, "s_acc", b[0], 19 + t)
                        pool.tensor_tensor(fin[b[2]][:, t], cn[:, t], x_all[:, bass.ts(b[0] * TPB + t, DM)],
                                           ALU.add).then_inc(S["s_out"], 1)

            pipeline(pool, NB, [1], finish)

        @block.tensor
        def _(pe):
            start(pe, "tensor")

            def mm(out, lhsT, rhs, first=True, last=True):
                return nc.tensor.matmul(out, lhsT, rhs, start=first, stop=last)

            def rotate(out, in_):
                return nc.tensor.transpose(out, in_, ident[:])

            pe.wait_ge(const_pool, 4)
            pe.wait_ge(ld_w, 16)
            pe.wait_ge(ld_small, 80)
            pe.wait_ge(const_dve, 2 + XT)

            def transposed(out, src):
                for k in range(KD):
                    for t in range(TPB):
                        last = rotate(out[:, k * SEQ + t * P:k * SEQ + (t + 1) * P], src[:, t, bass.ts(k, P)])
                return last

            def cumulate(b, t, banks):
                for half in range(2):
                    out = bank[banks[half]]
                    mm(out[:], ident16[:], mask4[:], True, False)
                    for hh in range(NH // 2):
                        at = half * (NH // 2) + hh
                        last = mm(out[:, bass.ts(hh, P)], dA[b[2]][:, t, at:at + 1].to_broadcast([P, P]), tri[:],
                                  False, hh == NH // 2 - 1)
                last.then_inc(S["b_cum_ps"], 1)

            def project(a, k0, out):
                for k in range(k0, k0 + 2):
                    for dd in range(KD):
                        last = mm(out[:, bass.ts(k % 2, SEQ)], win[:, dd, DI + k * P:DI + (k + 1) * P],
                                  xT[:, dd, :], dd == 0, dd == KD - 1)
                last.then_inc(S["a_xbc_ps"], 1)

            def within(b, t, out):
                for hh in range(NH):
                    last = mm(out[:, bass.ts(hh, HD)], M[:, t, hh, :], xdt[:, t, bass.ts(hh, HD)])
                last.then_inc(S["b_yd_ps"], 1)

            def mamba(a, b, d, c, p):
                if a:
                    need(pe, "n_norm", a[0])
                    need(pe, "a_z", a[0] - 1, 1)
                    transposed(bank[2], xn).then_inc(S["a_xT_ps"], 1)
                if b:
                    B = xbc[b[2]]
                    need(pe, "a_act", b[0])
                    need(pe, "a_dt", b[0])
                    need(pe, "c_top", b[0] - 3, 1)
                    for t in range(TPB):
                        mm(bank[4][:, bass.ts(t, P)], B[:, CB, bass.ts(t, P)], B[:, CC, bass.ts(t, P)])
                    for t in range(TPB):
                        mm(bank[4][:, 256 + t * NH:256 + (t + 1) * NH], tri[:], dA[b[2]][:, t, :])
                    mm(bank[4][:, 272:272 + NH], ones[:], dA[b[2]][:, 0, :])
                    rotate(bank[4][:, 384:512], B[:, CB, 0:P]).then_inc(S["b_small_ps"], 1)
                if p:
                    need(pe, "c_top", p[0])
                    need(pe, "p_slot", p[0] - 1)
                    need(pe, "b_y", p[0] + 2, 1)
                    for t in range(TPB):
                        out = bank[5][:, bass.ts(t, NE)]
                        mm(out, tri_strict[:], chosen[:, t, :], True, False)
                        if t:
                            mm(out, ones16[:], chosen[:, 0, :], False, False)
                        last = mm(out, ones16[:], cnt16[:], False, True)
                    last.then_inc(S["p_pos_ps"], 1)
                if b:
                    need(pe, "b_y", b[0] - 1, 2)
                    need(pe, "b_exp", b[0] - 1)
                    cumulate(b, 0, (7, 1))
                if d:
                    need(pe, "b_exp", d[0])
                    need(pe, "a_z", d[0] + 1)
                    for t in range(TPB):
                        need(pe, "b_yg", d[0], t + 1)
                        for k in range(XT):
                            last = rotate(bank[3 * t][:, bass.ts(k, P)], yg[:, t, bass.ts(k, P)])
                        last.then_inc(S["d_yT_ps"], 1)
                if c:
                    need(pe, "d_hn", c[0])
                    need(pe, "b_y", c[0] + 1, 1)
                    need(pe, "p_slot", c[0] - 1, 1)
                    transposed(bank[5], h).then_inc(S["c_hT_ps"], 1)
                if a:
                    need(pe, "a_xT", a[0])
                    need(pe, "b_y", a[0] - 2)
                    project(a, 0, bank[6])
                if d:
                    for t in range(TPB):
                        need(pe, "d_yT", d[0], t + 1)
                        for k in range(XT):
                            last = mm(bank[0][:, bass.ts(t, DM)], yT[:, t, bass.ts(k, P)], wo[:, k, :],
                                      k == 0, k == XT - 1)
                    last.then_inc(S["d_out_ps"], 1)
                if b:
                    need(pe, "a_xT", b[0] + 1)
                    need(pe, "d_yT", b[0] - 1)
                    for t in range(TPB):
                        for k in range(XT):
                            last = rotate(bank[2 + t][:, bass.ts(k, P)], B[:, k, bass.ts(t, P)])
                        last.then_inc(S["b_xs_ps"], 1)
                if a:
                    need(pe, "c_hT", a[0] - 3)
                    project(a, 2, bank[5])
                    need(pe, "b_exp", a[0] - 1, NH // 2)
                    project(a, 4, bank[7])
                    need(pe, "b_small", a[0] - 1)
                    for t in range(TPB):
                        for dd in range(KD):
                            last = mm(bank[4][:, bass.ts(t, NH)], xT[:, dd, bass.ts(t, P)],
                                      win[:, dd, DI + CD:DIN], dd == 0, dd == KD - 1)
                    last.then_inc(S["a_dt_ps"], 1)
                if c:
                    need(pe, "c_hT", c[0])
                    need(pe, "b_small", c[0] + 2)
                    for t in range(TPB):
                        for dd in range(KD):
                            last = mm(bank[4][:, P + t * NE:P + (t + 1) * NE], hTb[:, dd, bass.ts(t, P)], wg[:, dd, :],
                                      dd == 0, dd == KD - 1)
                    last.then_inc(S["c_lg_ps"], 1)
                if b:
                    need(pe, "b_exp", b[0], NH)
                    need(pe, "d_ao", b[0] - 1, 2)
                    cumulate(b, 1, (1, 0))
                if a:
                    need(pe, "b_xs", a[0] - 1)
                    for t in range(TPB):
                        for dd in range(KD):
                            last = mm(bank[2 + t][:], xT[:, dd, bass.ts(t, P)], win[:, dd, 0:DI],
                                      dd == 0, dd == KD - 1)
                        last.then_inc(S["a_z_ps"], 1)
                if b:
                    need(pe, "b_xdt", b[0])
                    need(pe, "b_small", b[0])
                    need(pe, "a_conv", b[0] + 1, 6)
                    mm(bank[6][:], BT[:], xw[:]).then_inc(S["b_st_ps"], 1)
                    need(pe, "b_m0", b[0])
                    need(pe, "a_conv", b[0] + 1, 12)
                    within(b, 0, bank[5])
                    need(pe, "b_st", b[0])
                    need(pe, "a_conv", b[0] + 1)
                    mm(bank[7][:], B[:, CC, P:2 * P], state[:]).then_inc(S["b_yo_ps"], 1)
                    need(pe, "b_m1", b[0])
                    within(b, 1, bank[6])

            pipeline(pe, NB, [1, 2, 3, 4, 5], mamba)

            need(pe, "p_slot", NB - 1)
            mm(bank[0][:, 0:NE], ones16[:], cnt16[:]).then_inc(cnt_ps, 1)

            phase_a_over(pe)
            pe.wait_ge(ld_table, 16)
            for q in range(NQ):
                for f in range(2):
                    rotate(bank[f][:, bass.ts(q, P)], tab[:, q, :, f]).then_inc(tab_ps, 1)
            pe.wait_ge(tab_sb, 2 * NQ)
            pe.wait_ge(const_pool, 5)
            tails = pe.alloc_register("pe_tails")
            pe.reg_mov(tails, 0)

            def gate_up(par, out, xT_, cols):
                for k, (at, n) in enumerate(((0, P), (P, P), (2 * P, UO + F1))):
                    for d in range(KD):
                        last = mm(out(k)[0:n], we[par][:, d * GW + at:d * GW + at + n], xT_[:, d, cols],
                                  d == 0, d == KD - 1)
                    yield last

            def down(par, out, hd, cols):
                mm(out, hd[:, 0, cols], we[par][:, KD * GW:], True, False)
                return mm(out, hd[:, 1, cols], we1[par][:], False, True)

            def expert(t, g, d):
                if t:
                    wait(pe, ga_x[t[2]], (t[1] + 1) * (MAIN * 16))
                    need(pe, "e_xTa", t[0] - 1)
                    need(pe, "e_xTv", t[0] - 1)
                    for k in range(KD):
                        for j in range(MAIN):
                            last = rotate(bank[k][:, bass.ts(j, P)], xg[t[2]][:, j, bass.ts(k, P)])
                        last.then_inc(S["e_T_ps"], 1)
                if g:
                    wait(pe, ld_gu[g[2]], (g[1] + 1) * 16)
                    need(pe, "e_xTa", g[0])
                    need(pe, "e_xTv", g[0])
                    need(pe, "e_silu", g[0] - 1)
                    need(pe, "e_hid", g[0] - 1)
                    for last in gate_up(g[2], lambda k: bank[2 + k], xgT[g[2]], slice(0, MR)):
                        last.then_inc(S["e_G_ps"], 1)
                    n = pe.value_load(cnt_i[0:1, bass.ds(g[0], 1)])
                    with pe.If(n > MR):
                        r = pe.snap(tails)
                        wait(pe, ld_dn[g[2]], (g[1] + 1) * 32)
                        for j in range(EXTRA):
                            i = r * EXTRA + j
                            pe.wait_ge(t_ga, (i + 1) * 16)
                            for k in range(KD):
                                last = rotate(bank[7][:, bass.ts(k, P)], t_xg[:, bass.ts(k, P)])
                            last.then_inc(t_T_ps, 1)
                            pe.wait_ge(t_xT, i + 1)
                            for last in gate_up(g[2], lambda k: bank[7][:, bass.ts(k, P)], t_xgT, slice(0, P)):
                                pass
                            last.then_inc(t_G_ps, 1)
                            pe.wait_ge(t_hid, (i + 1) * 2)
                            down(g[2], bank[7][:, 0:DM], t_hd, slice(0, P)).then_inc(t_D_ps, 1)
                        pe.wait_ge(t_eo, r * EXTRA + EXTRA)
                        pe.reg_add(tails, tails, 1)
                    pe.sem_inc(S["e_tail"], 1)
                if d:
                    wait(pe, ld_dn[d[2]], (d[1] + 1) * 32)
                    need(pe, "e_hid", d[0])
                    need(pe, "e_eoa", d[0] - 1)
                    need(pe, "e_eov", d[0] - 1)
                    for j in range(MAIN):
                        last = down(d[2], bank[5 + j // 2][:, bass.ts(j % 2, DM)], hid[d[2]], bass.ts(j, P))
                        if j % 2:
                            last.then_inc(S["e_D_ps"], 1)
            pipeline(pe, NE, [2, 3, 4], expert)

            need(pe, "e_eoa", NE - 1)
            need(pe, "e_eov", NE - 1)
            need(pe, "e_hid", NE - 1)
            pe.wait_ge(ld_c, 32)

            def shared(u, d):
                if u:
                    o = 3 * u[2]
                    need(pe, "s_hid", u[0] - 2)
                    cols = bass.ts(u[0], SEQ)
                    for k, parts in enumerate((((0, P), (P, P)), ((FS, P), (FS + P, P)),
                                               ((2 * P, F2), (FS + 2 * P, F2)))):
                        for i, (at, n) in enumerate(parts):
                            for dd in range(KD):
                                last = mm(bank[o + k][0:n, bass.ts(i, SEQ)], wsu[:, dd, at:at + n],
                                          hT_all[:, dd, cols], dd == 0, dd == KD - 1)
                        last.then_inc(S["s_U_ps"], 1)
                if d:
                    need(pe, "s_hid", d[0])
                    need(pe, "s_acc", d[0] - 2, 3)
                    for t in range(TPB):
                        for f in range(FT):
                            n = P if f < FT - 1 else F2
                            last = mm(bank[6 + d[2]][:, bass.ts(t, DM)], s_hd[0:n, f, bass.ts(t, P)],
                                      wsd[0:n, f, :], f == 0, f == FT - 1)
                    last.then_inc(S["s_D_ps"], 1)

            pipeline(pe, NB, [0, 1], shared)

        @block.scalar
        def _(act):
            start(act, "scalar")
            f = nc.scalar.activation
            act.wait_ge(ld_small, 80)
            act.preload_act_table_set("natural_log_exp_and_others")
            f(expA[:], hpar[:, 1, :], ACT.Exp).then_inc(const_act, 1)

            def decays(b, t, banks):
                need(act, "b_cum_ps", b[0], t + 1)
                for hh in range(NH):
                    f(M[:, t, hh, :], bank[banks[hh // 4]][:, bass.ts(hh % 4, P)], ACT.Exp,
                      bias=ncum[:, t, hh:hh + 1]).then_inc(S["b_exp"], 1)

            def last_tap(a, k0, out):
                need(act, "a_xbc_ps", a[0], k0 // 2 + 1)
                for k in range(k0, k0 + 2):
                    f(acc[:, k, :], out[:, bass.ts(k % 2, SEQ)], ACT.Identity,
                      bias=convp[:, k, KW:KW + 1], scale=convp[:, k, KW - 1:KW]).then_inc(S["a_conv0"], 1)

            def mamba(a, b, d, c, p):
                act.preload_act_table_set("natural_log_exp_and_others")
                if d:
                    need(act, "d_ms", d[0] - 1)
                    for t in range(TPB):
                        need(act, "b_yg", d[0], t + 1)
                        if t:
                            need(act, "d_ss", d[0], t)
                        else:
                            need(act, "d_ss", d[0] - 1)
                        f(junk[:], yg[:, t], ACT.Square, accum_out=ss[:, t:t + 1]).then_inc(S["d_ss"], 1)
                if a:
                    need(act, "a_xT_ps", a[0])
                    need(act, "a_z_ps", a[0] - 1)
                    f(xT[:].rearrange("p k s -> p (k s)"), bank[2][:], ACT.Copy).then_inc(S["a_xT"], 1)
                if p:
                    need(act, "c_top", p[0], 7)
                    need(act, "p_slot", p[0] - 1)
                    for t in range(TPB):
                        f(e64[:, t], lg[:, t], ACT.Exp, bias=nmx[:, t:t + 1], accum_out=esum[:, t:t + 1]
                          ).then_inc(S["p_exp"], 1)
                        f(e6[:, t], mx[:, t, 0:TOPK], ACT.Exp, bias=nmx[:, t:t + 1]).then_inc(S["p_exp"], 1)
                if b:
                    need(act, "b_small", b[0], 2)
                    need(act, "b_xdt", b[0] - 1)
                    need(act, "b_y", b[0] - 1)
                    f(wleft[:], left[:], ACT.Exp).then_inc(S["b_edge"], 1)
                    f(ecum[:], ncum[:, 1, :], ACT.Exp, scale=-1.0).then_inc(S["b_edge"], 1)
                    need(act, "b_yd_ps", b[0] - 1)
                    decays(b, 0, (7, 1))
                if d:
                    need(act, "d_out_ps", d[0] - 1)
                    for t in range(TPB):
                        need(act, "d_yT_ps", d[0], t + 1)
                        f(yT[:, t], bank[3 * t][:], ACT.Copy).then_inc(S["d_yT"], 1)
                if c:
                    need(act, "c_hT_ps", c[0])
                    need(act, "c_lg_ps", c[0] - 1)
                    f(hTb[:].rearrange("p k s -> p (k s)"), bank[5][:], ACT.Copy).then_inc(S["c_hT"], 1)
                    f(hT_all[:, :, bass.ts(c[0], SEQ)], bank[5][:].rearrange("p (k s) -> p k s", k=KD), ACT.Copy
                      ).then_inc(S["c_hT"], 1)
                if a:
                    need(act, "a_act", a[0] - 1)
                    last_tap(a, 0, bank[6])
                if b:
                    need(act, "b_skip", b[0] - 1)
                    need(act, "b_xdt", b[0] - 1)
                    for t in range(TPB):
                        need(act, "b_xs_ps", b[0], t + 1)
                        f(xs[:, t], bank[2 + t][:], ACT.Copy).then_inc(S["b_xs"], 1)
                if a:
                    last_tap(a, 2, bank[5])
                    last_tap(a, 4, bank[7])
                if b:
                    decays(b, 1, (1, 0))
                if a:
                    need(act, "a_dtx", a[0])
                    need(act, "a_dt", a[0] - 1)
                    f(dta[:], dtx[:], ACT.Abs).then_inc(S["a_sp"], 1)
                    need(act, "a_sp", a[0], 1)
                    f(dte[:], dta[:], ACT.Exp, scale=-1.0).then_inc(S["a_sp"], 1)
                    need(act, "a_sp", a[0], 2)
                    f(dtl[:], dte[:], ACT.Ln, bias=1.0).then_inc(S["a_sp"], 1)
                    act.preload_act_table_set("silu_and_others")
                    need(act, "b_yg", a[0] - 2)
                    for t in range(TPB):
                        need(act, "a_z_ps", a[0], t + 1)
                        f(zs[a[2]][:, t], bank[2 + t][:], ACT.Silu).then_inc(S["a_z"], 1)
                if b:
                    need(act, "b_st_ps", b[0])
                    need(act, "b_yo_ps", b[0] - 1)
                    f(state[:], bank[6][:], ACT.Copy).then_inc(S["b_st"], 1)
                if a:
                    need(act, "a_conv", a[0])
                    need(act, "b_yo_ps", a[0] - 2)
                    f(xbc[a[2]][:], acc[:], ACT.Silu).then_inc(S["a_act"], 1)

            pipeline(act, NB, [1, 2, 3, 4, 5], mamba)

            phase_a_over(act)
            tails = act.alloc_register("act_tails")
            act.reg_mov(tails, 0)

            def expert(t, g, d):
                if t:
                    need(act, "e_T_ps", t[0], 1)
                    need(act, "e_G_ps", t[0] - 2)
                    f(xgT[t[2]][:, 0, :], bank[0][:], ACT.Copy).then_inc(S["e_xTa"], 1)
                if g:
                    need(act, "e_hid", g[0] - 2)
                    need(act, "e_G_ps", g[0], 1)
                    f(sg[g[2]][:, 0, :], bank[2][:], ACT.Silu).then_inc(S["e_silu"], 1)
                    need(act, "e_G_ps", g[0])
                    f(sg[g[2]][0:F1, 1, :], bank[4][0:F1], ACT.Silu).then_inc(S["e_silu"], 1)
                    n = act.value_load(cnt_i[0:1, bass.ds(g[0], 1)])
                    with act.If(n > MR):
                        r = act.snap(tails)
                        for j in range(EXTRA):
                            i = r * EXTRA + j
                            act.wait_ge(t_T_ps, i + 1)
                            f(t_xgT[:].rearrange("p k s -> p (k s)"), bank[7][:, 0:KD * P], ACT.Copy).then_inc(t_xT, 1)
                            act.wait_ge(t_G_ps, i + 1)
                            f(t_sg[:, 0, :], bank[7][:, 0:P], ACT.Silu).then_inc(t_silu, 1)
                            f(t_sg[0:F1, 1, :], bank[7][0:F1, 2 * P:3 * P], ACT.Silu).then_inc(t_silu, 1)
                            act.wait_ge(t_D_ps, i + 1)
                            f(t_out[:], bank[7][:, 0:DM], ACT.Copy).then_inc(t_eo, 1)
                        act.reg_add(tails, tails, 1)
                    act.nop()
                if d:
                    need(act, "e_D_ps", d[0], 1)
                    wait(act, sc_y[d[2]], d[1] * (MAIN * 16))
                    f(eo[d[2]][:, 0:2, :].rearrange("p j d -> p (j d)"), bank[5][:], ACT.Copy
                      ).then_inc(S["e_eoa"], 1)
            pipeline(act, NE, [2, 3, 4], expert, peel=2)

            def shared(u):
                if u:
                    o = 3 * u[2]
                    need(act, "s_hid", u[0] - 1)
                    need(act, "s_U_ps", u[0], 1)
                    f(s_sg[:, 0:2, :].rearrange("p k s -> p (k s)"), bank[o][:], ACT.Silu).then_inc(S["s_silu"], 1)
                    need(act, "s_U_ps", u[0])
                    f(s_sg[0:F2, 2, :], bank[o + 2][0:F2, 0:SEQ], ACT.Silu).then_inc(S["s_silu"], 1)

            pipeline(act, NB, [0], shared)

        @block.vector
        def _(dve):
            start(dve, "vector")
            v = nc.vector
            dve.wait_ge(const_pool, 4)
            dve.wait_ge(ld_small, 80)
            dve.wait_ge(const_act, 1)
            v.tensor_scalar(negA[:], expA[:], -1.0, None, ALU.mult).then_inc(const_dve, 1)
            v.tensor_copy(Dx[:], hpar[:, 2, :][:, :, None].to_broadcast([P, NH, HD])).then_inc(const_dve, 1)
            for k in range(XT):
                v.tensor_scalar(wo[:, k, :], wo[:, k, :], normw[:, k:k + 1], None, ALU.mult).then_inc(const_dve, 1)
            v.memset(cnt[:], 0.0).then_inc(const_dve, 1)
            v.memset(cnt16[:], 0.0).then_inc(const_dve, 1)
            dve.wait_ge(const_dve, 4 + XT)
            dve.wait_ge(ld_x0, 16)

            def moments(name, n, src, st, mv, ve):
                item, base = name
                hold_dve(base)
                for t in range(TPB):
                    v.bn_stats(out=st[:, t, :], in_=src(t)).then_inc(S[item], 1)
                need(dve, item, base, n + 2)
                hold_dve(base)
                for t in range(TPB):
                    v.bn_aggr(out=mv[:, t, :], in_=st[:, t, :]).then_inc(S[item], 1)
                need(dve, item, base, n + 4)
                v.tensor_scalar(ve[:], mv[:, :, 1], EPS, None, ALU.add).then_inc(S[item], 1)

            def bc(ap, n):
                shape = list(ap.shape) + [n]
                return ap[(slice(None),) * len(ap.shape) + (None,)].to_broadcast(shape)

            def heads(ap):
                return ap.rearrange("p (h d) -> p h d", h=NH)

            def taps(a, k0, out):
                need(dve, "a_conv0", a[0], k0 + 2)
                for s in range(1, KW):
                    for k in range(k0, k0 + 2):
                        if s > 1:
                            need(dve, "a_conv", a[0], k0 * (KW - 1) + (s - 2) * 2 + k % 2 + 1)
                        v.scalar_tensor_tensor(
                            out=acc[:, k, s:], in0=out[:, k % 2 * SEQ:(k % 2 + 1) * SEQ - s],
                            scalar=convp[:, k, KW - 1 - s:KW - s], in1=acc[:, k, s:],
                            op0=ALU.mult, op1=ALU.add).then_inc(S["a_conv"], 1)

            def mamba(n, a, b, d, c, p):
                if n:
                    if isinstance(n[0], int) and n[0] == 1:
                        dve.wait_ge(ld_x1, 16)
                    need(dve, "n_rstd", n[0] - 1)
                    need(dve, "n_norm", n[0] - 1)
                    moments(("n_stats", n[0]), 0, lambda t: x_all[:, bass.ts(n[0] * TPB + t, DM)], a_st, a_mv, a_ve)
                if b:
                    need(dve, "b_small_ps", b[0])
                    need(dve, "b_exp", b[0] - 1)
                    need(dve, "b_m0", b[0] - 1)
                    need(dve, "b_st_ps", b[0] - 1)
                    v.tensor_scalar(ncum[:].rearrange("p t h -> p (t h)"), bank[4][:, 256:272], -1.0, None, ALU.mult
                                    ).then_inc(S["b_small"], 1)
                    need(dve, "b_small", b[0], 1)
                    v.tensor_tensor(left[:], bank[4][:, 272:272 + NH], ncum[:, 0, :], ALU.add
                                    ).then_inc(S["b_small"], 1)
                    v.tensor_copy(Gm[:].rearrange("p t l -> p (t l)"), bank[4][:, 0:TPB * P]).then_inc(S["b_small"], 1)
                    v.tensor_copy(BT[:], bank[4][:, 384:512]).then_inc(S["b_small"], 1)
                if d:
                    need(dve, "d_ss", d[0])
                    need(dve, "d_rms", d[0] - 1)
                    v.tensor_scalar(ms[:], ss[:], 1.0 / DI, EPS, ALU.mult, ALU.add).then_inc(S["d_ms"], 1)
                if n:
                    need(dve, "n_rstd", n[0])
                    need(dve, "a_xT_ps", n[0] - 1)
                    for t in range(TPB):
                        v.tensor_scalar(xn[:, t], x_all[:, bass.ts(n[0] * TPB + t, DM)], a_mv[:, t, 0:1],
                                        a_rs[:, t:t + 1], ALU.subtract, ALU.mult).then_inc(S["n_norm"], 1)
                if p:
                    places(p)
                if a:
                    taps(a, 0, bank[6])
                if d:
                    need(dve, "d_rms", d[0])
                    need(dve, "d_out_ps", d[0])
                    for t in range(TPB):
                        v.tensor_scalar(ao[:, t], bank[0][:, bass.ts(t, DM)], rms[:, t:t + 1], None, ALU.mult
                                        ).then_inc(S["d_ao"], 1)
                    need(dve, "d_ao", d[0], 2)
                    moments(("d_ao", d[0]), 2, lambda t: ao[:, t], b_stt, b_mv, b_ve)
                if b:
                    need(dve, "b_yd_ps", b[0] - 1)
                    for t in range(TPB):
                        need(dve, "b_xs", b[0], t + 1)
                        v.tensor_tensor(heads(xdt[:, t]), heads(xs[:, t]), bc(dt[b[2]][:, t, :], HD), ALU.mult
                                        ).then_inc(S["b_xdt"], 1)
                    need(dve, "b_edge", b[0], 1)
                    need(dve, "b_xdt", b[0], 1)
                    v.tensor_tensor(heads(xw[:]), heads(xdt[:, 0]), bc(wleft[:], HD), ALU.mult
                                    ).then_inc(S["b_xdt"], 1)
                if d:
                    need(dve, "d_rs", d[0])
                    for t in range(TPB):
                        v.tensor_scalar(aon[:, t], ao[:, t], b_mv[:, t, 0:1], b_rst[:, t:t + 1],
                                        ALU.subtract, ALU.mult).then_inc(S["d_aon"], 1)
                if a:
                    taps(a, 2, bank[5])
                if d:
                    need(dve, "d_x1", d[0])
                    moments(("d_h", d[0]), 0, lambda t: x_all[:, bass.ts(d[0] * TPB + t, DM)], h_st, h_mv, h_ve)
                if a:
                    taps(a, 4, bank[7])
                if d:
                    need(dve, "d_hrs", d[0])
                    need(dve, "c_hT_ps", d[0] - 1)
                    wait(dve, st_h[1 - d[2]], (d[1] + (1 if d[2] == 0 else 2)) * 16)
                    for t in range(TPB):
                        v.tensor_scalar(h[:, t], x_all[:, bass.ts(d[0] * TPB + t, DM)], h_mv[:, t, 0:1],
                                        h_rst[:, t:t + 1], ALU.subtract, ALU.mult).then_inc(S["d_hn"], 1)
                if a:
                    need(dve, "a_dt_ps", a[0])
                    need(dve, "c_lg_ps", a[0] - 3)
                    need(dve, "a_dt", a[0] - 1)
                    v.tensor_tensor(dtx[:], bank[4][:, 0:TPB * NH].rearrange("p (t h) -> p t h", t=TPB),
                                    hpar[:, 0:1, :].to_broadcast([P, TPB, NH]), ALU.add).then_inc(S["a_dtx"], 1)
                if c:
                    need(dve, "c_lg_ps", c[0])
                    need(dve, "p_exp", c[0] - 1)
                    v.tensor_copy(lg[:].rearrange("p t e -> p (t e)"), bank[4][:, P:P + TPB * NE]).then_inc(S["c_top"], 1)
                if b:
                    need(dve, "b_exp", b[0])
                    v.tensor_tensor(M[:, 1], M[:, 1], Gm[:, 1:2, :].to_broadcast([P, NH, P]), ALU.mult
                                    ).then_inc(S["b_m1"], 1)
                if c:
                    need(dve, "p_pos_ps", c[0] - 1)
                    need(dve, "p_slot", c[0] - 1)
                    need(dve, "c_top", c[0], 1)
                    hold_dve(c[0])
                    for t in range(TPB):
                        v.max(mx[:, t, :], lg[:, t, :]).then_inc(S["c_top"], 1)
                    need(dve, "c_top", c[0], 3)
                    hold_dve(c[0])
                    for t in range(TPB):
                        v.max_index(ix[:, t, :], mx[:, t, :], lg[:, t, :]).then_inc(S["c_top"], 1)
                    v.tensor_scalar(nmx[:], mx[:, :, 0], -1.0, None, ALU.mult).then_inc(S["c_top"], 1)
                    need(dve, "c_top", c[0], 5)
                    v.tensor_copy(ixf[:], ix[:, :, 0:TOPK]).then_inc(S["c_top"], 1)
                    need(dve, "c_top", c[0], 7)
                    v.tensor_tensor(oh[:], iota_e[:, None, None, :].to_broadcast([P, TPB, TOPK, NE]),
                                    bc(ixf[:], NE), ALU.is_equal).then_inc(S["c_top"], 1)
                if a:
                    need(dve, "a_sp", a[0])
                    need(dve, "b_xdt", a[0] - 2)
                    need(dve, "b_cum_ps", a[0] - 2)
                    v.scalar_tensor_tensor(out=dt[a[2]][:], in0=dtx[:], scalar=0.0, in1=dtl[:], op0=ALU.max,
                                           op1=ALU.add).then_inc(S["a_dt"], 1)
                    need(dve, "a_dt", a[0], 1)
                    v.tensor_tensor(dA[a[2]][:], dt[a[2]][:], negA[:, None, :].to_broadcast([P, TPB, NH]),
                                    ALU.mult).then_inc(S["a_dt"], 1)
                if c:
                    need(dve, "c_top", c[0], 8)
                    with nc.allow_low_precision("sums of 0 and 1"):
                        v.tensor_reduce(out=chosen[:], in_=oh[:].rearrange("p t k e -> p t e k"), axis=AX.X,
                                        op=ALU.add).then_inc(S["c_top"], 1)
                if b:
                    need(dve, "b_skip", b[0])
                    need(dve, "b_yd_ps", b[0], 1)
                    need(dve, "d_yT_ps", b[0] - 1)
                    need(dve, "d_ss", b[0] - 1)
                    v.tensor_tensor(yg[:, 0], bank[5][:], skip[:, 0], ALU.add).then_inc(S["b_y"], 1)
                    need(dve, "b_yo_ps", b[0])
                    need(dve, "b_edge", b[0])
                    v.tensor_tensor(heads(yoff[:]), heads(bank[7][:]), bc(ecum[:], HD), ALU.mult
                                    ).then_inc(S["b_y"], 1)
                    need(dve, "b_y", b[0], 2)
                    v.tensor_tensor(yoff[:], yoff[:], skip[:, 1], ALU.add).then_inc(S["b_y"], 1)
                    need(dve, "b_yd_ps", b[0])
                    need(dve, "b_y", b[0], 3)
                    v.tensor_tensor(yg[:, 1], bank[6][:], yoff[:], ALU.add).then_inc(S["b_y"], 1)

            def places(p):
                def nth(i):
                    need(dve, "p_slot", p[0], i)

                def done(ins):
                    ins.then_inc(S["p_slot"], 1)

                need(dve, "p_pos_ps", p[0])
                done(v.tensor_tensor(sel[:], oh[:], bank[5][:, 0:TPB * NE].rearrange(
                    "p (t e) -> p t e", t=TPB)[:, :, None, :].to_broadcast([P, TPB, TOPK, NE]), ALU.mult))
                done(v.tensor_tensor(cnt[:], cnt[:], chosen[:, 0, :], ALU.add))
                nth(1)
                done(v.tensor_reduce(out=pk[:], in_=sel[:], axis=AX.X, op=ALU.add))
                nth(2)
                done(v.tensor_tensor(cnt[:], cnt[:], chosen[:, 1, :], ALU.add))
                need(dve, "p_exp", p[0])
                done(v.reciprocal(rsum[:], esum[:]))
                nth(4)
                done(v.tensor_copy(cnt16[:], cnt[:]))
                done(v.scalar_tensor_tensor(out=slot[:], in0=ixf[:], scalar=float(CAP), in1=pk[:],
                                            op0=ALU.mult, op1=ALU.add))
                done(v.tensor_scalar(over[:], pk[:], float(CAP), float(SKIP), ALU.is_ge, ALU.mult))
                nth(5)
                done(v.tensor_tensor(p6[:], e6[:], bc(rsum[:], TOPK), ALU.mult))
                done(v.tensor_scalar(fits[:], pk[:], float(CAP), None, ALU.is_lt))
                nth(9)
                done(v.tensor_reduce(out=s6[:], in_=p6[:], axis=AX.X, op=ALU.add))
                wait(dve, sc_table[p[2]], p[1] * (TPB * TOPK * 16))
                done(v.tensor_tensor(slot_i[p[2]][:].rearrange("p (t k) -> p t k", t=TPB), slot[:], over[:],
                                     ALU.add))
                nth(11)
                done(v.tensor_scalar(s6e[:], s6[:], 1e-20, None, ALU.add))
                done(v.tensor_tensor(pay[p[2]][:], pay[1 - p[2]][:], step_pay[:], ALU.add))
                nth(13)
                done(v.reciprocal(r6[:], s6e[:]))
                nth(15)
                done(v.tensor_tensor(w6[:], p6[:], bc(r6[:], TOPK), ALU.mult))
                nth(16)
                done(v.tensor_tensor(w_all[:, bass.ts(p[0], TPB * TOPK)].rearrange("p (t k) -> p t k", t=TPB),
                                     w6[:], fits[:], ALU.mult))

            pipeline(dve, NB, [0, 1, 2, 3, 4, 5], mamba, peel=2)
            dve.wait_ge(cnt_ps, 1)
            v.tensor_copy(cnt_i[:, 0:NE], bank[0][:, 0:NE]).then_inc(cnt_sb, 1)
            v.tensor_reduce(out=cnt[:, 0:1], in_=bank[0][:, 0:NE], axis=AX.X, op=ALU.max).then_inc(cnt_sb, 1)
            dve.wait_ge(cnt_sb, 2)
            v.tensor_copy(cnt_i[:, NE:NE + 1], cnt[:, 0:1]).then_inc(cnt_sb, 1)

            phase_a_over(dve)
            dve.wait_ge(tab_ps, 2 * NQ)
            for q in range(NQ):
                v.tensor_copy(tok_idx[:, bass.ts(q, P)], bank[0][:, bass.ts(q, P)]).then_inc(tab_sb, 1)
                v.tensor_copy(row_idx[:, bass.ts(q, P)], bank[1][:, bass.ts(q, P)]).then_inc(tab_sb, 1)
            dve.wait_ge(const_pool, 5)
            tails = dve.alloc_register("dve_tails")
            dve.reg_mov(tails, 0)

            def expert(t, g, d):
                if t:
                    need(dve, "e_T_ps", t[0])
                    need(dve, "e_G_ps", t[0] - 2)
                    v.tensor_copy(xgT[t[2]][:, 1, :], bank[1][:]).then_inc(S["e_xTv"], 1)
                if g:
                    need(dve, "e_D_ps", g[0] - 2)
                    need(dve, "e_G_ps", g[0])
                    need(dve, "e_silu", g[0], 1)
                    v.tensor_tensor(hid[g[2]][:, 0, :], sg[g[2]][:, 0, :], bank[3][:], ALU.mult
                                    ).then_inc(S["e_hid"], 1)
                    need(dve, "e_silu", g[0])
                    v.tensor_tensor(hid[g[2]][0:F1, 1, :], sg[g[2]][0:F1, 1, :], bank[4][UO:UO + F1], ALU.mult
                                    ).then_inc(S["e_hid"], 1)
                    n = dve.value_load(cnt_i[0:1, bass.ds(g[0], 1)])
                    with dve.If(n > MR):
                        r = dve.snap(tails)
                        for j in range(EXTRA):
                            i = r * EXTRA + j
                            dve.wait_ge(t_silu, (i + 1) * 2)
                            v.tensor_tensor(t_hd[:, 0, :], t_sg[:, 0, :], bank[7][:, P:2 * P], ALU.mult
                                            ).then_inc(t_hid, 1)
                            v.tensor_tensor(t_hd[0:F1, 1, :], t_sg[0:F1, 1, :], bank[7][UO:UO + F1, 2 * P:3 * P],
                                            ALU.mult).then_inc(t_hid, 1)
                        dve.reg_add(tails, tails, 1)
                    dve.nop()
                if d:
                    need(dve, "e_D_ps", d[0])
                    wait(dve, sc_y[d[2]], d[1] * (MAIN * 16))
                    v.tensor_copy(eo[d[2]][:, 2:4, :].rearrange("p j d -> p (j d)"), bank[6][:]
                                  ).then_inc(S["e_eov"], 1)
            pipeline(dve, NE, [2, 3, 4], expert, peel=2)

            def shared(u, d):
                if u:
                    o = 3 * u[2]
                    need(dve, "s_D_ps", u[0] - 1)
                    need(dve, "s_U_ps", u[0])
                    need(dve, "s_silu", u[0])
                    v.tensor_tensor(s_hd[:, 0:2, :].rearrange("p k s -> p (k s)"),
                                    s_sg[:, 0:2, :].rearrange("p k s -> p (k s)"), bank[o + 1][:], ALU.mult
                                    ).then_inc(S["s_hid"], 1)
                    v.tensor_tensor(s_hd[0:F2, 2, :], s_sg[0:F2, 2, :], bank[o + 2][0:F2, SEQ:2 * SEQ], ALU.mult
                                    ).then_inc(S["s_hid"], 1)
                if d:
                    def nth(n):
                        need(dve, "s_acc", d[0], n)

                    def done(ins):
                        ins.then_inc(S["s_acc"], 1)

                    need(dve, "s_acc", d[0] - 1)
                    done(v.tensor_copy(wb[:].rearrange("p t k -> p (t k)"),
                                       w_all[:, bass.ts(d[0], TPB * TOPK)]))
                    nth(1)
                    wait(dve, ld_y[d[2]], (d[1] + 1) * 16)
                    need(dve, "s_D_ps", d[0])
                    for k in range(TOPK):
                        for t in range(TPB):
                            if k:
                                nth(2 * k + t)
                            prev = cacc[:, t] if k else bank[6 + d[2]][:, bass.ts(t, DM)]
                            done(v.scalar_tensor_tensor(out=cacc[:, t], in0=yb[d[2]][:, t, k, :],
                                                        scalar=wb[:, t, k:k + 1], in1=prev,
                                                        op0=ALU.mult, op1=ALU.add))
                    nth(13)
                    moments(("s_acc", d[0]), 13, lambda t: cacc[:, t], c_st, c_mv, c_ve)
                    need(dve, "s_rs", d[0])
                    need(dve, "s_out", d[0] - 1)
                    for t in range(TPB):
                        done(v.tensor_scalar(cn[:, t], cacc[:, t], c_mv[:, t, 0:1], c_rs[:, t:t + 1],
                                             ALU.subtract, ALU.mult))

            pipeline(dve, NB, [0, 1], shared)


def kernel(**inputs):
    import concourse.bacc as bacc
    from concourse.bass_utils import run_bass_kernel_spmd

    g = {n.removeprefix("L0_"): np.asarray(a) for n, a in inputs.items()}

    def on_partitions(a):
        return np.ascontiguousarray(a.reshape(-1, P, a.shape[-1]).transpose(1, 0, 2))

    gate_t, up_t, down_t = (g[n].transpose(0, 2, 1) for n in ("ffn_w_gate", "ffn_w_up", "ffn_w_down"))
    gu = np.zeros((NE, DM, GW), np.float32)
    gu[:, :, 0:P], gu[:, :, P:2 * P] = gate_t[:, :, 0:P], up_t[:, :, 0:P]
    gu[:, :, 2 * P:2 * P + F1], gu[:, :, 2 * P + UO:] = gate_t[:, :, P:], up_t[:, :, P:]
    gu = gu.reshape(NE, KD, P, GW).transpose(0, 2, 1, 3).reshape(NE, P, KD * GW)
    sd = np.zeros((FT * P, DM), np.float32)
    sd[:FS] = g["ffn_sh_down"].T
    arrays = dict(
        x=np.ascontiguousarray(g["attn_x"].reshape(NT, DM)),
        win=on_partitions(g["attn_in_proj_w"].T),
        wo=on_partitions(g["attn_out_proj_w"].T),
        convp=on_partitions(np.concatenate([g["attn_conv_w"], g["attn_conv_b"][:, None]], axis=1)),
        normw=np.ascontiguousarray(g["attn_norm_w"].reshape(XT, P).T),
        hpar=np.stack([g["attn_dt_bias"], g["attn_A_log"], g["attn_D"]]),
        wg=on_partitions(g["ffn_gate_w"].T),
        wsu=on_partitions(np.concatenate([g["ffn_sh_gate"].T, g["ffn_sh_up"].T], axis=1)),
        wsd=on_partitions(sd),
        we=np.ascontiguousarray(np.concatenate([gu, down_t[:, 0:P, :]], axis=2).reshape(NE * P, -1)),
        we1=np.ascontiguousarray(down_t[:, P:, :].reshape(NE * F1, DM)),
    )
    nc = bacc.Bacc("TRN2", target_bir_lowering=False, num_devices=1)
    T = {n: nc.dram_tensor("in_" + n, a.shape, mybir.dt.from_np(a.dtype), kind="ExternalInput").ap()
         for n, a in arrays.items()}
    T["out"] = nc.dram_tensor("out", (NT, DM), FP32, kind="ExternalOutput").ap()
    build(nc, T)
    r = run_bass_kernel_spmd(nc, [{"in_" + n: a for n, a in arrays.items()}], core_ids=[0])
    return r.results[0]["out"].reshape(NB, SEQ, DM)
```

```python
from contextlib import ExitStack

import numpy as np
import concourse.bass as bass
from concourse import mybir

FP32 = mybir.dt.float32
BF16 = mybir.dt.bfloat16
I32 = mybir.dt.int32
U32 = mybir.dt.uint32
ALU = mybir.AluOpType
ACT = mybir.ActivationFunctionType
AX = mybir.AxisListType

P = 128
NB, SEQ, DM = 16, 256, 256
NT = NB * SEQ
TPB = SEQ // P
KD = DM // P
DI, DS, NH, HD, KW = 512, 128, 8, 64, 4
CD = DI + 2 * DS
CT = CD // P
XT = DI // P
CB, CC = XT, XT + 1
DIN = 2 * DI + 2 * DS + NH
NE, TOPK, FE, FS = 64, 6, 176, 352
CAP = 2 * ((NT * TOPK + NE - 1) // NE)
CAPT = CAP // P
MAIN = 3
WIDE = MAIN + 1
WR = WIDE * P
TAIL = CAPT - WIDE
F1 = FE - P
UO = 64
GW = 2 * P + UO + F1
FT = (FS + P - 1) // P
F2 = FS - (FT - 1) * P
NSLOT = NE * CAP
FIRST = 3
EARLY = 4
OWN = 3
NQ = NE * CAPT // P
SKIP = 1 << 20
EPS = 1e-5
LANE = 32
PR = 2 * LANE + NH
PAIRS = (CB, 0, 2)
LOW = -1e30

PER = dict(
    tensor=dict(a_xT_ps=1, a_xbc_ps=CT // 2, a_z_ps=TPB, a_dt_ps=1,
                b_small_ps=1, b_cumT_ps=1, b_cum_ps=TPB, b_xs_ps=TPB, b_st_ps=1, b_yd_ps=TPB, b_yo_ps=1,
                d_yT_ps=TPB, d_out_ps=1, c_hT_ps=1, c_lg_ps=1, p_pos_ps=1,
                e_T_ps=KD, e_G_ps=3, e_tail=1, e_D_ps=2, s_U_ps=3, s_D_ps=1),
    scalar=dict(n_norm=TPB, d_hn=TPB, b_gb=2, a_xT=1, a_conv0=CT, a_act=2, a_z=TPB, a_sp=3,
                b_hi=1, b_edge=2, b_exp=TPB * NH, b_xs=TPB, b_st=1, d_ss=TPB, d_yT=TPB, c_hT=2, p_exp=2 * TPB,
                e_xTa=1, e_silu=2, e_eoa=1, s_silu=2, s_keep=1,
                y_wa=1, y_mul=TPB * (TOPK - OWN)),
    vector=dict(n_stats=6, a_conv=(KW - 1) * CT, a_dtx=1, a_dt=2,
                b_small=2, b_piece=4, b_xdt=3, b_m1=1, b_y=4, d_ms=1, d_ao=7, d_aon=TPB, d_h=6,
                c_top=9, p_slot=17, e_xTv=1, e_hid=2, e_eov=1, s_hid=2, s_acc=15),
    gpsimd=dict(n_rstd=2, b_m0=1, b_skip=TPB, b_yg=TPB, d_rms=1, d_rs=1, d_x1=TPB, d_hrs=2,
                e_gidx=1, e_sidx=1, y_sum=2, s_rs=1, s_out=TPB),
)
ROUND = {name: k for per in PER.values() for name, k in per.items()}
CREDIT = 2


def build(nc, T):
    ctx = ExitStack()
    with ctx:
        def sb(name, shape, dt=FP32, stack=ctx):
            return stack.enter_context(nc.sbuf_tensor(name, shape, dt))

        def sem(name):
            return ctx.enter_context(nc.semaphore(name))

        def pair(name):
            return [sem(name + "0"), sem(name + "1")]

        S = {name: sem(name) for name in ROUND}
        ld_x0, ld_x1, ld_w, ld_small, ld_c = (sem("ld_" + n) for n in "x0 x1 w small c".split())
        st_table, st_h, ld_table = sem("st_table"), pair("st_h"), sem("ld_table")
        sc_table, ld_gu, ld_dn, ga_x, sc_y, ld_y, st_out = (
            pair(n) for n in "sc_table ld_gu ld_dn ga_x sc_y ld_y st_out".split())
        const_pool, const_dve, const_act = sem("const_pool"), sem("const_dve"), sem("const_act")
        tick_sp, tick_pool, tick_dve, tick_act, tick_pe = (sem("tick_" + n) for n in "sp pool dve act pe".split())
        cnt_ps, cnt_sb, tab_ps, tab_sb = sem("cnt_ps"), sem("cnt_sb"), sem("tab_ps"), sem("tab_sb")
        y_zero, y_ready = sem("y_zero"), sem("y_ready")
        ga_w, sc_w, w_idx = pair("ga_w"), pair("sc_w"), sem("w_idx")
        t_idx, t_ga, t_T_ps, t_xT, t_G_ps, t_silu, t_hid, t_D_ps, t_eo, t_sc, t_free = (
            sem("t_" + n) for n in "idx ga T_ps xT G_ps silu hid D_ps eo sc free".split())

        x_all = sb("x_all", [P, NT // P * DM])
        hT_all = sb("hT_all", [P, KD, NT])
        w_all = sb("w_all", [P, NT // P * TOPK])
        ident = sb("ident", [P, P])
        ones = sb("ones", [P, P])
        neghalf = sb("neghalf", [P, TPB])
        zero_row = sb("zero_row", [P, DM])
        wsu = sb("wsu", [P, KD, 2 * FS])
        wsd = sb("wsd", [P, FT, DM])
        cnt_i = sb("cnt_i", [P, NE + 1], I32)
        we = [sb(f"we{i}", [P, KD * GW + DM]) for i in range(2)]
        we1 = [sb(f"we1{i}", [P, DM]) for i in range(2)]
        tok_idx = sb("tok_idx", [P, NE * CAPT], I32)
        row_idx = sb("row_idx", [P, NE * CAPT], I32)

        pa = ExitStack()

        def sa(name, shape, dt=FP32):
            return sb(name, shape, dt, pa)

        win = sa("win", [P, KD, DIN])
        wo = sa("wo", [P, XT, DM])
        acc = sa("acc", [P, CT, SEQ])
        xbc = [sa(f"xbc{i}", [P, CT, SEQ]) for i in range(2)]
        tri = sa("tri", [P, P])
        tri_strict = sa("tri_strict", [P, P], BF16)
        ones16 = sa("ones16", [P, P], BF16)
        ident16 = sa("ident16", [P, P], BF16)
        mask4 = sa("mask4", [P, NH // 2 * P], BF16)
        cnt = sa("cnt", [P, NE])
        cnt16 = sa("cnt16", [P, NE], BF16)
        wg = sa("wg", [P, KD, NE])
        convp = sa("convp", [P, CT, KW + 1])
        normw = sa("normw", [P, XT])
        hpar = sa("hpar", [P, 3, NH])
        expA = sa("expA", [P, NH])
        negA = sa("negA", [P, NH])
        Dx = sa("Dx", [P, NH, HD])
        iota_e = sa("iota_e", [P, NE])
        table0 = sa("table0", [P, NSLOT // P, 2])
        pay = [sa(f"pay{i}", [P, TPB * TOPK, 2]) for i in range(2)]
        step_pay = sa("step_pay", [P, TPB * TOPK, 2])
        a_st, a_mv, a_ve, a_rs = sa("a_st", [P, TPB, 6]), sa("a_mv", [P, TPB, 2]), sa("a_ve", [P, TPB]), sa("a_rs", [P, TPB])
        a_nm, a_nb, h_nm, h_nb = (sa(n, [P, TPB]) for n in "a_nm a_nb h_nm h_nb".split())
        xn = sa("xn", [P, TPB, DM])
        xT = sa("xT", [P, KD, SEQ])
        zs = [sa(f"zs{i}", [P, TPB, DI]) for i in range(2)]
        dtx, dta, dte, dtl = (sa(n, [P, TPB, NH]) for n in "dtx dta dte dtl".split())
        dt = [sa(f"dt{i}", [P, TPB, NH]) for i in range(2)]
        dA3 = [sa(f"dA3{i}", [P, TPB, 3, LANE]) for i in range(2)]
        pick = sa("pick", [3 * LANE, NH, P], BF16)
        parts = sa("parts", [3 * LANE, SEQ], BF16)
        parts_r = sa("parts_r", [3 * LANE, SEQ])
        parts_m = sa("parts_m", [3 * LANE, SEQ], BF16)
        Gm = sa("Gm", [P, TPB, P])
        ncum = sa("ncum", [P, TPB, NH])
        left = sa("left", [P, NH])
        BT = sa("BT", [P, P])
        M = sa("M", [P, TPB, NH, P])
        xs, xdt, skip, yg, yT = (sa(n, [P, TPB, DI]) for n in "xs xdt skip yg yT".split())
        xw, state, yoff, junk = (sa(n, [P, DI]) for n in "xw state yoff junk".split())
        wleft, ecum = sa("wleft", [P, NH]), sa("ecum", [P, NH])
        ss, ms, rms = (sa(n, [P, TPB]) for n in "ss ms rms".split())
        ao, aon, h = (sa(n, [P, TPB, DM]) for n in "ao aon h".split())
        b_stt, b_mv, b_ve, b_rst = sa("b_stt", [P, TPB, 6]), sa("b_mv", [P, TPB, 2]), sa("b_ve", [P, TPB]), sa("b_rst", [P, TPB])
        h_st, h_mv, h_ve, h_rst = sa("h_st", [P, TPB, 6]), sa("h_mv", [P, TPB, 2]), sa("h_ve", [P, TPB]), sa("h_rst", [P, TPB])
        hTb = sa("hTb", [P, KD, SEQ])
        lg = sa("lg", [P, TPB, NE])
        mx = sa("mx", [P, TPB, 8])
        ix = sa("ix", [P, TPB, 8], U32)
        nmx, esum, rsum, s6, s6e, r6 = (sa(n, [P, TPB]) for n in "nmx esum rsum s6 s6e r6".split())
        e64 = sa("e64", [P, TPB, NE])
        ixf, e6, pk, slot, over, fits, p6, w6 = (
            sa(n, [P, TPB, TOPK]) for n in "ixf e6 pk slot over fits p6 w6".split())
        oh = sa("oh", [P, TPB, TOPK, NE])
        sel = sa("sel", [P, TPB, TOPK, NE])
        chosen = sa("chosen", [P, TPB, NE], BF16)
        slot_i = [sa(f"slot_i{i}", [P, TPB * TOPK], I32) for i in range(2)]
        pa.close()

        pb = ExitStack()

        def sbb(name, shape, dt=FP32):
            return sb(name, shape, dt, pb)

        s_sg, s_hd = sbb("s_sg", [P, FT, SEQ]), sbb("s_hd", [P, FT, SEQ])
        kept = sbb("kept", [P, NB * TPB * DM])
        tab = sbb("tab", [P, NQ, P, 2])
        def sbe(name, shape, dt=FP32):
            return sb(name, shape, dt, experts)

        experts = ExitStack()
        xg = [sbe(f"xg{i}", [P, WIDE, DM]) for i in range(2)]
        xgT = [sbe(f"xgT{i}", [P, KD, WR]) for i in range(2)]
        g_idx = [sbe(f"g_idx{i}", [P, WIDE], I32) for i in range(2)]
        s_idx = [sbe(f"s_idx{i}", [P, WIDE], I32) for i in range(2)]
        sg = [sbe(f"sg{i}", [P, 2, WR]) for i in range(2)]
        hid = [sbe(f"hid{i}", [P, 2, WR]) for i in range(2)]
        eo = [sbe(f"eo{i}", [P, WIDE, DM]) for i in range(2)]
        t_xg, t_out = (sbe(n, [P, TAIL, DM]) for n in "t_xg t_out".split())
        t_xgT, t_sg, t_hd = (sbe(n, [P, 2, TAIL * P]) for n in "t_xgT t_sg t_hd".split())
        t_gi, t_si = sbe("t_gi", [P, TAIL], I32), sbe("t_si", [P, TAIL], I32)
        dummy = [sbe(f"dummy{i}", [P, 2]) for i in range(2)]
        experts.close()
        yb = [sbb(f"yb{i}", [P, TPB, TOPK, DM]) for i in range(2)]
        wb, wa = sbb("wb", [P, TPB, TOPK]), sbb("wa", [P, TPB, TOPK])
        rest = [sbb(f"rest{i}", [P, TPB, DM]) for i in range(2)]
        cacc, cn = sbb("cacc", [P, TPB, DM]), sbb("cn", [P, TPB, DM])
        c_st, c_mv, c_ve, c_rs = sbb("c_st", [P, TPB, 6]), sbb("c_mv", [P, TPB, 2]), sbb("c_ve", [P, TPB]), sbb("c_rs", [P, TPB])
        fin = [sbb(f"fin{i}", [P, TPB, DM]) for i in range(2)]
        pb.close()

        bank = [ctx.enter_context(nc.psum_tensor(f"bank{i}", [P, 512], FP32)) for i in range(8)]

        h_dram = nc.dram_tensor("h_rows", [NT, DM], FP32, kind="Internal").ap()
        table = nc.dram_tensor("slot_table", [NSLOT, 2], FP32, kind="Internal").ap()
        y_rows = nc.dram_tensor("y_rows", [NT * TOPK, DM], FP32, kind="Internal").ap()

        def start(eng, which):
            for name, k in PER[which].items():
                eng.sem_inc(S[name], CREDIT * k)

        def hold(eng):
            if eng is nc.gpsimd:
                eng.sem_inc(tick_pool, 1)
            elif eng is nc.sync:
                eng.sem_inc(tick_sp, 1)

        def hold_dve(i):
            if not isinstance(i, int):
                nc.vector.sem_inc(tick_dve, 1)

        def wait(eng, s, value):
            if isinstance(value, int) and value == 0:
                return
            eng.wait_ge(s, value)
            if not isinstance(value, int):
                hold(eng)

        def need(eng, name, i, n=None):
            if isinstance(i, int):
                if i < 0:
                    return
                if name[0] in "nabdcp":
                    i = min(i, NB - 1)
            k = ROUND[name]
            wait(eng, S[name], i * k + ((k if n is None else n) + CREDIT * k))

        def pipeline(eng, items, lags, work, peel=0, first=0):
            lo = max(lags) + max(lags) % 2 + peel
            hi = items + min(lags)
            hi -= (hi - lo) % 2

            def at(m, par, n=None):
                out = []
                for lag in lags:
                    q = par - lag
                    on = n is None or 0 <= n - lag < items
                    out.append((m * 2 + (q + first), m + (q + first) // 2, (q + first) % 2) if on else None)
                return out

            for n in range(min(lags), lo):
                work(*at(n // 2, n % 2, n))
            if hi > lo:
                with eng.Fori(lo // 2, hi // 2) as m:
                    for par in range(2):
                        work(*at(m, par))
            for n in range(max(lo, hi), items + max(lags)):
                work(*at(n // 2, n % 2, n))

        def sooner(u):
            return (u[0] - EARLY, u[1] - EARLY // 2, u[2])

        def count_of(eng, e):
            if eng is nc.vector:
                eng.sem_inc(tick_dve, 1)
            elif eng is nc.tensor:
                eng.sem_inc(tick_pe, 1)
            return eng.value_load(cnt_i[0:1, bass.ds(e, 1)])

        def counters(eng, *names):
            regs = [eng.alloc_register(n) for n in names]
            for reg in regs:
                eng.reg_mov(reg, 0)
            return regs

        def phase_a_over(eng):
            eng.wait_ge(cnt_sb, 3)
            for q in range(2):
                eng.wait_ge(sc_table[q], NB // 2 * TPB * TOPK * 16)
                eng.wait_ge(st_h[q], (NB // 2 + 1) * 16)

        def phase_b_over(eng):
            for q in range(2):
                eng.wait_ge(sc_y[q], NE // 2 * MAIN * 16)
            eng.wait_ge(const_pool, 9)
            eng.wait_ge(w_idx, 1)

        block = ctx.enter_context(nc.Block())

        @block.sync
        def _(sp):
            for q in range(2):
                sp.sem_inc(st_h[q], 16)
            sp.dma_start(x_all[:, 0:TPB * DM].rearrange("p (t d) -> p t d", d=DM),
                         T["x"][0:SEQ].rearrange("(t p) d -> p t d", p=P)).then_inc(ld_x0, 16)
            sp.dma_start(hpar[:], T["hpar"][None, :, :].to_broadcast([P, 3, NH])).then_inc(ld_small, 16)
            sp.dma_start(convp[:], T["convp"]).then_inc(ld_small, 16)
            sp.dma_start(normw[:], T["normw"]).then_inc(ld_small, 16)
            sp.dma_start(wo[:], T["wo"]).then_inc(ld_small, 16)
            sp.dma_start(wg[:], T["wg"]).then_inc(ld_small, 16)
            sp.dma_start(win[:], T["win"]).then_inc(ld_w, 16)
            sp.dma_start(x_all[:, TPB * DM:].rearrange("p (t d) -> p t d", d=DM),
                         T["x"][SEQ:].rearrange("(t p) d -> p t d", p=P)).then_inc(ld_x1, 16)
            sp.dma_start(wsu[:], T["wsu"]).then_inc(ld_c, 16)
            sp.dma_start(wsd[:], T["wsd"]).then_inc(ld_c, 16)
            sp.wait_ge(const_pool, 2)
            sp.dma_start(table.rearrange("(p s) c -> p s c", p=P), table0[:]).then_inc(st_table, 16)

            def load_gate_up(e, m, par):
                need(sp, "e_G_ps", e - 2)
                need(sp, "e_tail", e - 2)
                sp.dma_start(we[par][:, 0:KD * GW], T["we"][bass.ts(e, P), 0:KD * GW]).then_inc(ld_gu[par], 16)

            def load_down(e, m, par):
                need(sp, "e_D_ps", e - 2)
                need(sp, "e_tail", e - 2)
                sp.dma_start(we[par][:, KD * GW:], T["we"][bass.ts(e, P), KD * GW:]).then_inc(ld_dn[par], 16)
                sp.dma_start(we1[par][0:F1, :], T["we1"][bass.ts(e, F1), :]).then_inc(ld_dn[par], 16)

            for e in range(2):
                load_gate_up(e, 0, e)
                load_down(e, 0, e)

            def store_h(b):
                if b:
                    need(sp, "d_hn", b[0])
                    sp.dma_start(h_dram[bass.ts(b[0], SEQ), :].rearrange("(t p) d -> p t d", p=P), h[:]
                                 ).then_inc(st_h[b[2]], 16)

            pipeline(sp, NB, [3], store_h)
            phase_a_over(sp)
            sp.dma_start(tab[:], table.rearrange("(q g s) c -> g q s c", g=P, s=P)).then_inc(ld_table, 16)
            most = sp.value_load(cnt_i[0:1, NE:NE + 1])
            with sp.If(most > CAP):
                sp.dma_start(y_rows.rearrange("(p r) d -> p r d", p=P),
                             zero_row[:, None, :].to_broadcast([P, NT * TOPK // P, DM])).then_inc(y_zero, 16)
                sp.wait_ge(y_zero, 16)
                sp.sem_inc(tick_sp, 1)
            sp.sem_inc(y_ready, 1)

            load_gate_up(2, 1, 0)
            load_gate_up(3, 1, 1)
            load_down(2, 1, 0)
            with sp.Fori(2, NE // 2) as m:
                for par in range(2):
                    load_gate_up(m * 2 + par, m, par)
                    load_down(m * 2 + par - 1, m - 1 + par, 1 - par)
            load_down(NE - 1, NE // 2 - 1, 1)

            def load_y(b, m, par):
                need(sp, "s_acc", b - 2, 7)
                need(sp, "y_sum", b - 2)
                sp.dma_start(yb[par][:], y_rows[bass.ts(b, SEQ * TOPK), :].rearrange(
                    "(t p k) d -> p t k d", p=P, k=TOPK)).then_inc(ld_y[par], 16)

            def store_out(b, m, par):
                need(sp, "s_out", b)
                sp.dma_start(T["out"][bass.ts(b, SEQ), :].rearrange("(t p) d -> p t d", p=P), fin[par][:]
                             ).then_inc(st_out[par], 16)

            phase_b_over(sp)
            sp.wait_ge(y_ready, 1)
            load_y(0, 0, 0)
            load_y(1, 0, 1)
            with sp.Fori(1, NB // 2) as m:
                for par in range(2):
                    load_y(m * 2 + par, m, par)
                    store_out(m * 2 + par - 2, m - 1, par)
            for b in range(NB - 2, NB):
                store_out(b, b // 2, b % 2)
            for q in range(2):
                sp.wait_ge(st_out[q], (NB // 2 + 1) * 16)

        @block.gpsimd
        def _(pool):
            start(pool, "gpsimd")
            for q in range(2):
                pool.sem_inc(st_out[q], 16)
            pool.memset(table0[:, :, 0:1], 0.0)
            pool.memset(table0[:, :, 1:2], float(SKIP)).then_inc(const_pool, 1)
            pool.memset(we1[0][:], 0.0)
            pool.memset(we1[1][:], 0.0).then_inc(const_pool, 1)
            pool.memset(ident[:], 0.0)
            pool.memset(ones[:], 1.0)
            pool.memset(neghalf[:], -0.5)
            pool.memset(zero_row[:], 0.0)
            pool.memset(step_pay[:, :, 0:1], float(SEQ))
            pool.memset(step_pay[:, :, 1:2], float(SEQ * TOPK))
            pool.memset(mask4[:], 0.0)
            pool.memset(pick[:], 0.0)
            for i in range(2):
                pool.memset(dA3[i][:], 0.0)
            pool.memset(ones16[:], 1.0).then_inc(const_pool, 1)
            pool.wait_ge(const_pool, 3)
            pool.affine_select(out=ident[:], in_=ident[:], compare_op=ALU.not_equal, fill=1.0, base=0,
                               pattern=[[-1, P]], channel_multiplier=1)
            pool.affine_select(out=tri[:], in_=ones[:], compare_op=ALU.is_ge, fill=0.0, base=0,
                               pattern=[[1, P]], channel_multiplier=-1)
            pool.affine_select(out=ident16[:], in_=ones[:], compare_op=ALU.is_equal, fill=0.0, base=0,
                               pattern=[[-1, P]], channel_multiplier=1)
            pool.affine_select(out=mask4[:].rearrange("p (h l) -> p h l", h=NH // 2),
                               in_=mask4[:].rearrange("p (h l) -> p h l", h=NH // 2), compare_op=ALU.is_ge,
                               fill=LOW, base=0, pattern=[[0, NH // 2], [1, P]], channel_multiplier=-1)
            for i in range(3):
                pool.wait_ge(const_pool, 3 + i)
                pool.affine_select(out=pick[:], in_=pick[:], compare_op=ALU.not_equal, fill=1.0, base=-i * LANE,
                                   pattern=[[-1, NH], [0, P]], channel_multiplier=1).then_inc(const_pool, 1)
            pool.affine_select(out=tri_strict[:], in_=ones[:], compare_op=ALU.is_gt, fill=0.0, base=0,
                               pattern=[[1, P]], channel_multiplier=-1)
            pool.iota(iota_e[:], pattern=[[1, NE]], base=0, channel_multiplier=0,
                      allow_small_or_imprecise_dtypes=True)
            pool.iota(pay[1][:, :, 0].rearrange("p (t k) -> p t k", t=TPB), pattern=[[P, TPB], [0, TOPK]],
                      base=-SEQ, channel_multiplier=1, allow_small_or_imprecise_dtypes=True)
            pool.iota(pay[1][:, :, 1].rearrange("p (t k) -> p t k", t=TPB),
                      pattern=[[P * TOPK, TPB], [1, TOPK]], base=-SEQ * TOPK, channel_multiplier=TOPK,
                      allow_small_or_imprecise_dtypes=True).then_inc(const_pool, 1)
            pool.wait_ge(const_dve, 3)

            def scatter_slots(f, part):
                for k in range(part * 3, part * 3 + 3):
                    pool.indirect_dma_start(
                        table, bass.IndirectOffsetOnAxis(ap=slot_i[f[2]][:, k:k + 1], axis=0),
                        pay[f[2]][:, k, :], None, bounds_check=NSLOT - 1, oob_is_err=False
                    ).then_inc(sc_table[f[2]], 16)

            def rows(n, b, d, f):
                if f:
                    if isinstance(f[0], int) and f[0] == 0:
                        pool.wait_ge(st_table, 16)
                    need(pool, "p_slot", f[0])
                    scatter_slots(f, 0)
                if n:
                    need(pool, "n_stats", n[0])
                    need(pool, "n_norm", n[0] - 1)
                    pool.tensor_tensor(a_rs[:], a_ve[:], neghalf[:], ALU.pow).then_inc(S["n_rstd"], 1)
                    need(pool, "n_rstd", n[0], 1)
                    pool.tensor_tensor(a_nb[:], a_nm[:], a_rs[:], ALU.mult).then_inc(S["n_rstd"], 1)
                if f:
                    scatter_slots(f, 1)
                if d:
                    need(pool, "d_ms", d[0])
                    pool.tensor_tensor(rms[:], ms[:], neghalf[:], ALU.pow).then_inc(S["d_rms"], 1)
                if b:
                    need(pool, "b_gb", b[0], 1)
                    need(pool, "b_exp", b[0], NH)
                    pool.tensor_tensor(M[:, 0], M[:, 0], Gm[:, 0:1, :].to_broadcast([P, NH, P]), ALU.mult
                                       ).then_inc(S["b_m0"], 1)
                if d:
                    need(pool, "d_ao", d[0])
                    pool.tensor_tensor(b_rst[:], b_ve[:], neghalf[:], ALU.pow).then_inc(S["d_rs"], 1)
                if b:
                    need(pool, "b_y", b[0] - 1)
                    for t in range(TPB):
                        need(pool, "b_xs", b[0], t + 1)
                        pool.tensor_tensor(skip[:, t], xs[:, t], Dx[:].rearrange("p h d -> p (h d)"), ALU.mult
                                           ).then_inc(S["b_skip"], 1)
                if d:
                    for t in range(TPB):
                        need(pool, "d_aon", d[0], t + 1)
                        xrow = x_all[:, bass.ts(d[0] * TPB + t, DM)]
                        pool.tensor_tensor(xrow, xrow, aon[:, t], ALU.add).then_inc(S["d_x1"], 1)
                if f:
                    scatter_slots(f, 2)
                if d:
                    need(pool, "d_h", d[0])
                    need(pool, "d_hn", d[0] - 1)
                    pool.tensor_tensor(h_rst[:], h_ve[:], neghalf[:], ALU.pow).then_inc(S["d_hrs"], 1)
                    need(pool, "d_hrs", d[0], 1)
                    pool.tensor_tensor(h_nb[:], h_nm[:], h_rst[:], ALU.mult).then_inc(S["d_hrs"], 1)
                if b:
                    for t in range(TPB):
                        need(pool, "b_y", b[0], 1 if t == 0 else 4)
                        pool.tensor_tensor(yg[:, t], yg[:, t], zs[b[2]][:, t], ALU.mult).then_inc(S["b_yg"], 1)
                if f:
                    scatter_slots(f, 3)

            pipeline(pool, NB, [0, 2, 3, 6], rows)

            phase_a_over(pool)
            for i in range(2):
                pool.memset(hid[i][:], 0.0)
            pool.memset(t_hd[:], 0.0).then_inc(const_pool, 1)
            for i in range(2):
                pool.dma_start(dummy[i][:], table.rearrange("(p s) c -> p s c", p=P)[:, i, :]).then_inc(sc_w[i], 16)
            pool.wait_ge(tab_sb, 2 * NQ)
            pool.wait_ge(y_ready, 1)
            pool.sem_inc(t_free, 1)
            n_ga, n_sc = counters(pool, "pool_tail_gathers", "pool_tail_scatters")

            def load(to, idx, j, done):
                pool.indirect_dma_start(to[:, j, :], None, h_dram,
                                        bass.IndirectOffsetOnAxis(ap=idx[:, j:j + 1], axis=0),
                                        bounds_check=NT - 1, oob_is_err=False).then_inc(done, 16)

            def gather(e, m, par):
                need(pool, "e_T_ps", e - 2)
                pool.tensor_copy(g_idx[par][:], tok_idx[:, bass.ds(e * CAPT, WIDE)]).then_inc(S["e_gidx"], 1)
                need(pool, "e_gidx", e)
                for j in range(MAIN):
                    load(xg[par], g_idx[par], j, ga_x[par])
                n = count_of(pool, e)
                with pool.If(n > MAIN * P):
                    load(xg[par], g_idx[par], MAIN, ga_w[par])
                pool.sem_inc(tick_pool, 1)

            def gather_tail(e):
                n = count_of(pool, e)
                with pool.If(n > WR):
                    r = pool.snap(n_ga)
                    wait(pool, t_T_ps, r + 1)
                    pool.tensor_copy(t_gi[:], tok_idx[:, bass.ds(e * CAPT + WIDE, TAIL)]).then_inc(t_idx, 1)
                    wait(pool, t_idx, r + pool.snap(n_sc) + 1)
                    for j in range(TAIL):
                        load(t_xg, t_gi, j, t_ga)
                    pool.reg_add(n_ga, n_ga, 1)
                pool.sem_inc(tick_pool, 1)

            def scatter(e, m, par):
                need(pool, "e_eoa", e)
                need(pool, "e_eov", e)
                pool.tensor_copy(s_idx[par][:], row_idx[:, bass.ds(e * CAPT, WIDE)]).then_inc(S["e_sidx"], 1)
                need(pool, "e_sidx", e)

                def store(src, idx, j, done):
                    pool.indirect_dma_start(y_rows, bass.IndirectOffsetOnAxis(ap=idx[:, j:j + 1], axis=0),
                                            src[:, j, :], None, bounds_check=NT * TOPK - 1, oob_is_err=False
                                            ).then_inc(done, 16)

                for j in range(MAIN):
                    store(eo[par], s_idx[par], j, sc_y[par])
                n = count_of(pool, e)
                with pool.If(n > MAIN * P):
                    store(eo[par], s_idx[par], MAIN, sc_w[par])
                with pool.If(n > WR):
                    r = pool.snap(n_sc)
                    pool.tensor_copy(t_si[:], row_idx[:, bass.ds(e * CAPT + WIDE, TAIL)]).then_inc(t_idx, 1)
                    wait(pool, t_idx, r + pool.snap(n_ga) + 1)
                    wait(pool, t_eo, r + 2)
                    for j in range(TAIL):
                        store(t_out, t_si, j, t_sc)
                    wait(pool, t_sc, (r + 1) * (16 * TAIL))
                    pool.sem_inc(t_free, 1)
                    pool.reg_add(n_sc, n_sc, 1)
                pool.sem_inc(tick_pool, 1)

            def expert_rows(g, t, d):
                if d:
                    scatter(*d)
                if g:
                    gather(*g)
                if t:
                    gather_tail(t[0])

            pipeline(pool, NE, [0, 2, 5], expert_rows, peel=2)
            pool.sem_inc(const_pool, 1)

            phase_b_over(pool)

            def finish(c, b):
                if b:
                    need(pool, "s_acc", b[0], 13)
                    pool.tensor_tensor(c_rs[:], c_ve[:], neghalf[:], ALU.pow).then_inc(S["s_rs"], 1)
                if c:
                    need(pool, "y_mul", c[0])
                    need(pool, "s_acc", c[0] - 2, 8)
                    y, out = yb[c[2]], rest[c[2]][:]
                    pool.tensor_tensor(out, y[:, :, OWN, :], y[:, :, OWN + 1, :], ALU.add).then_inc(S["y_sum"], 1)
                    need(pool, "y_sum", c[0], 1)
                    pool.tensor_tensor(out, out, y[:, :, OWN + 2, :], ALU.add).then_inc(S["y_sum"], 1)
                if b:
                    wait(pool, st_out[b[2]], (b[1] + 1) * 16)
                    for t in range(TPB):
                        need(pool, "s_acc", b[0], 14 + t)
                        pool.tensor_tensor(fin[b[2]][:, t], cn[:, t], x_all[:, bass.ts(b[0] * TPB + t, DM)],
                                           ALU.add).then_inc(S["s_out"], 1)

            pipeline(pool, NB, [0, 1], finish)

        @block.tensor
        def _(pe):
            start(pe, "tensor")

            def mm(out, lhsT, rhs, first=True, last=True):
                return nc.tensor.matmul(out, lhsT, rhs, start=first, stop=last)

            def rotate(out, in_):
                return nc.tensor.transpose(out, in_, ident[:])

            pe.wait_ge(const_pool, 7)
            pe.wait_ge(ld_w, 16)
            pe.wait_ge(ld_small, 80)
            pe.wait_ge(const_dve, 2 + XT)

            def transposed(out, src):
                for k in range(KD):
                    for t in range(TPB):
                        last = rotate(out[:, k * SEQ + t * P:k * SEQ + (t + 1) * P], src[:, t, bass.ts(k, P)])
                return last

            def cumulate(b, t, banks):
                for half in range(2):
                    out = bank[banks[half]]
                    mm(out[:], ident16[:], mask4[:], True, False)
                    for hh in range(NH // 2):
                        last = mm(out[:, bass.ts(hh, P)], pick[0:PR, half * (NH // 2) + hh, :],
                                  parts[0:PR, bass.ts(t, P)], False, hh == NH // 2 - 1)
                last.then_inc(S["b_cum_ps"], 1)

            def project(a, i, out):
                for k in range(PAIRS[i], PAIRS[i] + 2):
                    for dd in range(KD):
                        last = mm(out[:, bass.ts(k % 2, SEQ)], win[:, dd, DI + k * P:DI + (k + 1) * P],
                                  xT[:, dd, :], dd == 0, dd == KD - 1)
                last.then_inc(S["a_xbc_ps"], 1)

            def within(b, t, out):
                for hh in range(NH):
                    last = mm(out[:, bass.ts(hh, HD)], M[:, t, hh, :], xdt[:, t, bass.ts(hh, HD)])
                last.then_inc(S["b_yd_ps"], 1)

            def mamba(a, b, d, c, p):
                if a:
                    need(pe, "n_norm", a[0])
                    need(pe, "a_z", a[0] - 1, 1)
                    transposed(bank[2], xn).then_inc(S["a_xT_ps"], 1)
                if b:
                    B = xbc[b[2]]
                    need(pe, "a_act", b[0], 1)
                    need(pe, "a_dt", b[0])
                    need(pe, "c_top", b[0] - 3, 1)
                    for t in range(TPB):
                        mm(bank[4][:, bass.ts(t, P)], B[:, CB, bass.ts(t, P)], B[:, CC, bass.ts(t, P)])
                    mm(bank[4][:, 256:256 + TPB * NH].rearrange("p (t h) -> p t h", t=TPB), tri[:],
                       dA3[b[2]][:, :, 0, 0:NH])
                    mm(bank[4][:, 272:272 + NH], ones[:], dA3[b[2]][:, 0, 0, 0:NH])
                    rotate(bank[4][:, 384:512], B[:, CB, 0:P]).then_inc(S["b_small_ps"], 1)
                    need(pe, "b_y", b[0] - 1, 1)
                    for t in range(TPB):
                        last = mm(bank[5][0:PR, SEQ + t * P:SEQ + (t + 1) * P],
                                  dA3[b[2]][:, t].rearrange("p r l -> p (r l)")[:, 0:PR], tri[:])
                    last.then_inc(S["b_cumT_ps"], 1)
                if d:
                    need(pe, "b_exp", d[0])
                    need(pe, "a_z", d[0] + 1)
                    for t in range(TPB):
                        need(pe, "b_yg", d[0], t + 1)
                        for k in range(XT):
                            last = rotate(bank[3 * t][:, bass.ts(k, P)], yg[:, t, bass.ts(k, P)])
                        last.then_inc(S["d_yT_ps"], 1)
                if p:
                    need(pe, "c_top", p[0])
                    need(pe, "p_slot", p[0] - 1)
                    need(pe, "a_xT", p[0] + 4)
                    need(pe, "a_z", p[0] + 3, 1)
                    need(pe, "b_xs", p[0] + 2, 1)
                    for t in range(TPB):
                        out = bank[2][:, bass.ts(t, NE)]
                        mm(out, tri_strict[:], chosen[:, t, :], True, False)
                        if t:
                            mm(out, ones16[:], chosen[:, 0, :], False, False)
                        last = mm(out, ones16[:], cnt16[:], False, True)
                    last.then_inc(S["p_pos_ps"], 1)
                if a:
                    need(pe, "a_xT", a[0])
                    need(pe, "b_y", a[0] - 2)
                    project(a, 0, bank[6])
                if b:
                    need(pe, "b_y", b[0] - 1, 2)
                    need(pe, "b_exp", b[0] - 1)
                    need(pe, "b_piece", b[0])
                    cumulate(b, 0, (7, 1))
                if c:
                    need(pe, "d_hn", c[0])
                    need(pe, "b_y", c[0] + 1, 1)
                    need(pe, "b_piece", c[0] + 2)
                    transposed(bank[5], h).then_inc(S["c_hT_ps"], 1)
                if d:
                    for t in range(TPB):
                        need(pe, "d_yT", d[0], t + 1)
                        for k in range(XT):
                            last = mm(bank[0][:, bass.ts(t, DM)], yT[:, t, bass.ts(k, P)], wo[:, k, :],
                                      k == 0, k == XT - 1)
                    last.then_inc(S["d_out_ps"], 1)
                if b:
                    need(pe, "a_act", b[0])
                    need(pe, "a_xT", b[0] + 1)
                    need(pe, "p_slot", b[0] - 3, 1)
                    need(pe, "d_yT", b[0] - 1)
                    for t in range(TPB):
                        for k in range(XT):
                            last = rotate(bank[2 + t][:, bass.ts(k, P)], B[:, k, bass.ts(t, P)])
                        last.then_inc(S["b_xs_ps"], 1)
                if a:
                    need(pe, "c_hT", a[0] - 3)
                    project(a, 1, bank[5])
                    need(pe, "b_exp", a[0] - 1, NH // 2)
                    project(a, 2, bank[7])
                    need(pe, "b_gb", a[0] - 1)
                    for t in range(TPB):
                        for dd in range(KD):
                            last = mm(bank[4][:, bass.ts(t, NH)], xT[:, dd, bass.ts(t, P)],
                                      win[:, dd, DI + CD:DIN], dd == 0, dd == KD - 1)
                    last.then_inc(S["a_dt_ps"], 1)
                if c:
                    need(pe, "c_hT", c[0])
                    need(pe, "b_gb", c[0] + 2)
                    for t in range(TPB):
                        for dd in range(KD):
                            last = mm(bank[4][:, P + t * NE:P + (t + 1) * NE], hTb[:, dd, bass.ts(t, P)], wg[:, dd, :],
                                      dd == 0, dd == KD - 1)
                    last.then_inc(S["c_lg_ps"], 1)
                if b:
                    need(pe, "b_exp", b[0], NH)
                    need(pe, "d_ao", b[0] - 1, 2)
                    cumulate(b, 1, (1, 0))
                if a:
                    need(pe, "b_xs", a[0] - 1)
                    for t in range(TPB):
                        for dd in range(KD):
                            last = mm(bank[2 + t][:], xT[:, dd, bass.ts(t, P)], win[:, dd, 0:DI],
                                      dd == 0, dd == KD - 1)
                        last.then_inc(S["a_z_ps"], 1)
                if b:
                    need(pe, "b_xdt", b[0])
                    need(pe, "b_gb", b[0])
                    need(pe, "a_conv", b[0] + 1, 6)
                    mm(bank[6][:], BT[:], xw[:]).then_inc(S["b_st_ps"], 1)
                    need(pe, "b_m0", b[0])
                    need(pe, "a_conv", b[0] + 1, 12)
                    within(b, 0, bank[5])
                    need(pe, "b_st", b[0])
                    need(pe, "a_conv", b[0] + 1)
                    mm(bank[7][:], B[:, CC, P:2 * P], state[:]).then_inc(S["b_yo_ps"], 1)
                    need(pe, "b_m1", b[0])
                    within(b, 1, bank[6])

            pipeline(pe, NB, [1, 2, 3, 4, 5], mamba)

            need(pe, "p_slot", NB - 1)
            mm(bank[0][:, 0:NE], ones16[:], cnt16[:]).then_inc(cnt_ps, 1)

            need(pe, "d_x1", NB - 1)
            need(pe, "c_hT", NB - 1)
            pe.wait_ge(cnt_sb, 3)
            pe.wait_ge(ld_c, 32)

            def shared(u, d):
                if u:
                    o = 3 * u[2]
                    need(pe, "s_hid", u[0] - 2)
                    cols = bass.ts(u[0], SEQ)
                    for k, parts in enumerate((((0, P), (P, P)), ((FS, P), (FS + P, P)),
                                               ((2 * P, F2), (FS + 2 * P, F2)))):
                        for i, (at, n) in enumerate(parts):
                            for dd in range(KD):
                                last = mm(bank[o + k][0:n, bass.ts(i, SEQ)], wsu[:, dd, at:at + n],
                                          hT_all[:, dd, cols], dd == 0, dd == KD - 1)
                        last.then_inc(S["s_U_ps"], 1)
                if d:
                    need(pe, "s_hid", d[0])
                    need(pe, "s_keep", d[0] - 2)
                    for t in range(TPB):
                        for f in range(FT):
                            n = P if f < FT - 1 else F2
                            last = mm(bank[6 + d[2]][:, bass.ts(t, DM)], s_hd[0:n, f, bass.ts(t, P)],
                                      wsd[0:n, f, :], f == 0, f == FT - 1)
                    last.then_inc(S["s_D_ps"], 1)

            pipeline(pe, FIRST, [0, 1], shared)

            need(pe, "s_hid", FIRST - 1)
            need(pe, "s_keep", FIRST - 1)
            phase_a_over(pe)
            pe.wait_ge(ld_table, 16)
            for q in range(NQ):
                for f in range(2):
                    rotate(bank[f][:, bass.ts(q, P)], tab[:, q, :, f]).then_inc(tab_ps, 1)
            pe.wait_ge(tab_sb, 2 * NQ)
            pipeline(pe, EARLY - FIRST, [0, 1], shared, first=FIRST)
            need(pe, "s_hid", EARLY - 1)
            need(pe, "s_keep", EARLY - 1)
            pe.wait_ge(const_pool, 8)
            pe.sem_inc(t_T_ps, 1)
            n_ga, n_tail = counters(pe, "pe_wide0", "pe_wide1"), counters(pe, "pe_tails")[0]

            def gate_up(par, xT_, at, n, done):
                for k, (col, m) in enumerate(((0, P), (P, P), (2 * P, UO + F1))):
                    for dd in range(KD):
                        last = mm(bank[2 + k][0:m, at:at + n], we[par][:, dd * GW + col:dd * GW + col + m],
                                  xT_[:, dd, at:at + n], dd == 0, dd == KD - 1)
                    if done is not None:
                        last.then_inc(done, 1)

            def down(par, out, hd, j):
                mm(out, hd[:, 0, bass.ts(j, P)], we[par][:, KD * GW:], True, False)
                return mm(out, hd[:, 1, bass.ts(j, P)], we1[par][:], False, True)

            def expert(t, g, d):
                if t:
                    need(pe, "e_xTa", t[0] - 1)
                    need(pe, "e_xTv", t[0] - 1)
                    n = count_of(pe, t[0])
                    with pe.If(n > MAIN * P):
                        r = pe.snap(n_ga[t[2]])
                        wait(pe, ga_w[t[2]], (r + 1) * 16)
                        for k in range(KD):
                            rotate(bank[k][:, bass.ts(MAIN, P)], xg[t[2]][:, MAIN, bass.ts(k, P)])
                        pe.reg_add(n_ga[t[2]], n_ga[t[2]], 1)
                    wait(pe, ga_x[t[2]], (t[1] + 1) * (MAIN * 16))
                    for k in range(KD):
                        for j in range(MAIN):
                            last = rotate(bank[k][:, bass.ts(j, P)], xg[t[2]][:, j, bass.ts(k, P)])
                        last.then_inc(S["e_T_ps"], 1)
                if d:
                    pe.wait_ge(t_eo, pe.snap(n_tail) + 1)
                    pe.sem_inc(S["e_tail"], 1)
                if g:
                    n = count_of(pe, g[0])
                    r = pe.snap(n_tail)
                    with pe.If(n > WR):
                        pe.wait_ge(t_ga, (r + 1) * (16 * TAIL))
                        for k in range(KD):
                            for j in range(TAIL):
                                last = rotate(bank[7][:, (k * TAIL + j) * P:(k * TAIL + j + 1) * P],
                                              t_xg[:, j, bass.ts(k, P)])
                        last.then_inc(t_T_ps, 1)
                    wait(pe, ld_gu[g[2]], (g[1] + 1) * 16)
                    need(pe, "e_xTa", g[0])
                    need(pe, "e_xTv", g[0])
                    need(pe, "e_silu", g[0] - 1)
                    need(pe, "e_hid", g[0] - 1)
                    with pe.If(n > MAIN * P):
                        gate_up(g[2], xgT[g[2]], MAIN * P, P, None)
                    gate_up(g[2], xgT[g[2]], 0, MAIN * P, S["e_G_ps"])
                if d:
                    wait(pe, ld_dn[d[2]], (d[1] + 1) * 32)
                    need(pe, "e_hid", d[0])
                    need(pe, "e_eoa", d[0] - 1)
                    need(pe, "e_eov", d[0] - 1)
                    m = count_of(pe, d[0])
                    with pe.If(m > MAIN * P):
                        down(d[2], bank[6][:, DM:2 * DM], hid[d[2]], MAIN)
                    for j in range(MAIN):
                        last = down(d[2], bank[5 + j // 2][:, bass.ts(j % 2, DM)], hid[d[2]], j)
                        if j:
                            last.then_inc(S["e_D_ps"], 1)
                if g:
                    with pe.If(n > WR):
                        wait(pe, ld_dn[g[2]], (g[1] + 1) * 32)
                        need(pe, "e_hid", g[0])
                        pe.wait_ge(t_xT, r + 1)
                        gate_up(g[2], t_xgT, 0, TAIL * P, t_G_ps)
                        pe.wait_ge(t_hid, (r + 1) * 2)
                        for j in range(TAIL):
                            last = down(g[2], bank[7][:, bass.ts(j, DM)], t_hd, j)
                        last.then_inc(t_D_ps, 1)
                        pe.reg_add(n_tail, n_tail, 1)

            pipeline(pe, NE, [2, 3, 4], expert)

            need(pe, "e_eoa", NE - 1)
            need(pe, "e_eov", NE - 1)
            need(pe, "e_hid", NE - 1)
            pipeline(pe, NB - EARLY, [0, 1], shared, first=EARLY)

        @block.scalar
        def _(act):
            start(act, "scalar")
            f = nc.scalar.activation
            act.wait_ge(ld_small, 80)
            act.preload_act_table_set("natural_log_exp_and_others")
            f(expA[:], hpar[:, 1, :], ACT.Exp).then_inc(const_act, 1)

            def decays(b, t, banks):
                need(act, "b_cum_ps", b[0], t + 1)
                for hh in range(NH):
                    f(M[:, t, hh, :], bank[banks[hh // 4]][:, bass.ts(hh % 4, P)], ACT.Exp,
                      bias=ncum[:, t, hh:hh + 1]).then_inc(S["b_exp"], 1)

            def last_tap(a, i, out):
                need(act, "a_xbc_ps", a[0], i + 1)
                for k in range(PAIRS[i], PAIRS[i] + 2):
                    f(acc[:, k, :], out[:, bass.ts(k % 2, SEQ)], ACT.Identity,
                      bias=convp[:, k, KW:KW + 1], scale=convp[:, k, KW - 1:KW]).then_inc(S["a_conv0"], 1)

            def mamba(n, a, b, d, c, p):
                act.preload_act_table_set("natural_log_exp_and_others")
                if d:
                    need(act, "d_ms", d[0] - 1)
                    for t in range(TPB):
                        need(act, "b_yg", d[0], t + 1)
                        if t:
                            need(act, "d_ss", d[0], t)
                        else:
                            need(act, "d_ss", d[0] - 1)
                        f(junk[:], yg[:, t], ACT.Square, accum_out=ss[:, t:t + 1]).then_inc(S["d_ss"], 1)
                if a:
                    need(act, "a_xT_ps", a[0])
                    need(act, "a_z_ps", a[0] - 1)
                    f(xT[:].rearrange("p k s -> p (k s)"), bank[2][:], ACT.Copy).then_inc(S["a_xT"], 1)
                if b:
                    need(act, "b_cumT_ps", b[0])
                    need(act, "b_cum_ps", b[0] - 1)
                    f(parts[0:PR], bank[5][0:PR, SEQ:], ACT.Copy).then_inc(S["b_hi"], 1)
                if p:
                    need(act, "c_top", p[0], 7)
                    need(act, "p_slot", p[0] - 1)
                    for t in range(TPB):
                        f(e64[:, t], lg[:, t], ACT.Exp, bias=nmx[:, t:t + 1], accum_out=esum[:, t:t + 1]
                          ).then_inc(S["p_exp"], 1)
                        f(e6[:, t], mx[:, t, 0:TOPK], ACT.Exp, bias=nmx[:, t:t + 1]).then_inc(S["p_exp"], 1)
                if b:
                    need(act, "b_small", b[0])
                    need(act, "b_m0", b[0] - 1)
                    need(act, "b_m1", b[0] - 1)
                    need(act, "b_st_ps", b[0] - 1)
                    need(act, "b_xdt", b[0] - 1)
                    need(act, "b_y", b[0] - 1)
                    f(wleft[:], left[:], ACT.Exp).then_inc(S["b_edge"], 1)
                    f(ecum[:], ncum[:, 1, :], ACT.Exp, scale=-1.0).then_inc(S["b_edge"], 1)
                    f(Gm[:].rearrange("p t l -> p (t l)"), bank[4][:, 0:TPB * P], ACT.Copy).then_inc(S["b_gb"], 1)
                    f(BT[:], bank[4][:, 384:512], ACT.Copy).then_inc(S["b_gb"], 1)
                if d:
                    need(act, "d_out_ps", d[0] - 1)
                    for t in range(TPB):
                        need(act, "d_yT_ps", d[0], t + 1)
                        f(yT[:, t], bank[3 * t][:], ACT.Copy).then_inc(S["d_yT"], 1)
                if a:
                    need(act, "a_act", a[0] - 1)
                    last_tap(a, 0, bank[6])
                if b:
                    need(act, "b_yd_ps", b[0] - 1)
                    decays(b, 0, (7, 1))
                if c:
                    need(act, "c_hT_ps", c[0])
                    need(act, "c_lg_ps", c[0] - 1)
                    f(hTb[:].rearrange("p k s -> p (k s)"), bank[5][:], ACT.Copy).then_inc(S["c_hT"], 1)
                    f(hT_all[:, :, bass.ts(c[0], SEQ)], bank[5][:].rearrange("p (k s) -> p k s", k=KD), ACT.Copy
                      ).then_inc(S["c_hT"], 1)
                if b:
                    need(act, "b_skip", b[0] - 1)
                    need(act, "b_xdt", b[0] - 1)
                    for t in range(TPB):
                        need(act, "b_xs_ps", b[0], t + 1)
                        f(xs[:, t], bank[2 + t][:], ACT.Copy).then_inc(S["b_xs"], 1)
                if n:
                    need(act, "n_rstd", n[0])
                    need(act, "a_xT_ps", n[0] - 1)
                    act.sem_inc(tick_act, 1)
                    for t in range(TPB):
                        f(xn[:, t], x_all[:, bass.ts(n[0] * TPB + t, DM)], ACT.Identity, bias=a_nb[:, t:t + 1],
                          scale=a_rs[:, t:t + 1]).then_inc(S["n_norm"], 1)
                if a:
                    last_tap(a, 1, bank[5])
                    last_tap(a, 2, bank[7])
                if b:
                    decays(b, 1, (1, 0))
                    need(act, "b_st_ps", b[0])
                    need(act, "b_yo_ps", b[0] - 1)
                    f(state[:], bank[6][:], ACT.Copy).then_inc(S["b_st"], 1)
                if a:
                    need(act, "a_dtx", a[0])
                    need(act, "a_dt", a[0] - 1)
                    f(dta[:], dtx[:], ACT.Abs).then_inc(S["a_sp"], 1)
                    need(act, "a_sp", a[0], 1)
                    f(dte[:], dta[:], ACT.Exp, scale=-1.0).then_inc(S["a_sp"], 1)
                    need(act, "a_sp", a[0], 2)
                    f(dtl[:], dte[:], ACT.Ln, bias=1.0).then_inc(S["a_sp"], 1)
                    act.preload_act_table_set("silu_and_others")
                    need(act, "b_yg", a[0] - 2)
                    for t in range(TPB):
                        need(act, "a_z_ps", a[0], t + 1)
                        f(zs[a[2]][:, t], bank[2 + t][:], ACT.Silu).then_inc(S["a_z"], 1)
                if a:
                    need(act, "a_conv", a[0], 6)
                    need(act, "b_yo_ps", a[0] - 2)
                    f(xbc[a[2]][:, CB:], acc[:, CB:], ACT.Silu).then_inc(S["a_act"], 1)
                    need(act, "a_conv", a[0])
                    f(xbc[a[2]][:, 0:XT], acc[:, 0:XT], ACT.Silu).then_inc(S["a_act"], 1)
                if d:
                    need(act, "d_hrs", d[0])
                    need(act, "c_hT_ps", d[0] - 1)
                    wait(act, st_h[1 - d[2]], (d[1] + (1 if d[2] == 0 else 2)) * 16)
                    act.sem_inc(tick_act, 1)
                    for t in range(TPB):
                        f(h[:, t], x_all[:, bass.ts(d[0] * TPB + t, DM)], ACT.Identity, bias=h_nb[:, t:t + 1],
                          scale=h_rst[:, t:t + 1]).then_inc(S["d_hn"], 1)

            pipeline(act, NB, [0, 1, 2, 3, 4, 5], mamba)

            def shared(u, d):
                if u:
                    o = 3 * u[2]
                    need(act, "s_hid", u[0] - 1)
                    need(act, "s_U_ps", u[0], 1)
                    f(s_sg[:, 0:2, :].rearrange("p k s -> p (k s)"), bank[o][:], ACT.Silu).then_inc(S["s_silu"], 1)
                    need(act, "s_U_ps", u[0])
                    f(s_sg[0:F2, 2, :], bank[o + 2][0:F2, 0:SEQ], ACT.Silu).then_inc(S["s_silu"], 1)
                if d:
                    need(act, "s_D_ps", d[0])
                    f(kept[:, bass.ts(d[0], TPB * DM)], bank[6 + d[2]][:], ACT.Copy).then_inc(S["s_keep"], 1)

            pipeline(act, FIRST, [0, 1], shared)

            phase_a_over(act)
            pipeline(act, EARLY - FIRST, [0, 1], shared, first=FIRST)
            n_tail, = counters(act, "act_tails")
            act.sem_inc(t_eo, 1)

            def expert(t, g, d):
                if t:
                    need(act, "e_T_ps", t[0], 1)
                    need(act, "e_G_ps", t[0] - 2)
                    f(xgT[t[2]][:, 0, :], bank[0][:], ACT.Copy).then_inc(S["e_xTa"], 1)
                if g:
                    n = count_of(act, g[0])
                    r = act.snap(n_tail)
                    with act.If(n > WR):
                        act.wait_ge(t_T_ps, r + 2)
                        f(t_xgT[:].rearrange("p k s -> p (k s)"), bank[7][:], ACT.Copy).then_inc(t_xT, 1)
                    need(act, "e_hid", g[0] - 2)
                    need(act, "e_G_ps", g[0], 1)
                    f(sg[g[2]][:, 0, :], bank[2][:], ACT.Silu).then_inc(S["e_silu"], 1)
                    need(act, "e_G_ps", g[0])
                    f(sg[g[2]][0:F1, 1, :], bank[4][0:F1], ACT.Silu).then_inc(S["e_silu"], 1)
                if d:
                    need(act, "e_D_ps", d[0], 1)
                    wait(act, sc_y[d[2]], d[1] * (MAIN * 16))
                    f(eo[d[2]][:, 0:2, :].rearrange("p j d -> p (j d)"), bank[5][:], ACT.Copy
                      ).then_inc(S["e_eoa"], 1)
                if g:
                    with act.If(n > WR):
                        act.wait_ge(t_G_ps, r * 3 + 3)
                        f(t_sg[:, 0, :], bank[2][:, 0:TAIL * P], ACT.Silu).then_inc(t_silu, 1)
                        f(t_sg[0:F1, 1, :], bank[4][0:F1, 0:TAIL * P], ACT.Silu).then_inc(t_silu, 1)
                        act.wait_ge(t_D_ps, r + 1)
                        act.wait_ge(t_free, r + 1)
                        f(t_out[:].rearrange("p j d -> p (j d)"), bank[7][:], ACT.Copy).then_inc(t_eo, 1)
                        act.reg_add(n_tail, n_tail, 1)
                    act.nop()

            pipeline(act, NE, [2, 3, 4], expert, peel=2)

            phase_b_over(act)

            def weigh(b):
                need(act, "y_mul", b[0] - 1)
                act.sem_inc(tick_act, 1)
                f(wa[:].rearrange("p t k -> p (t k)"), w_all[:, bass.ts(b[0], TPB * TOPK)], ACT.Copy
                  ).then_inc(S["y_wa"], 1)
                need(act, "y_wa", b[0])
                wait(act, ld_y[b[2]], (b[1] + 1) * 16)
                for k in range(OWN, TOPK):
                    for t in range(TPB):
                        f(yb[b[2]][:, t, k, :], yb[b[2]][:, t, k, :], ACT.Copy, scale=wa[:, t, k:k + 1]
                          ).then_inc(S["y_mul"], 1)

            def last_phase(u, d):
                shared(u, d)
                if u:
                    weigh(sooner(u))

            pipeline(act, NB - EARLY, [0, 1], last_phase, first=EARLY)
            pipeline(act, EARLY, [0], weigh, first=NB - EARLY)

        @block.vector
        def _(dve):
            start(dve, "vector")
            v = nc.vector
            dve.wait_ge(const_pool, 7)
            dve.wait_ge(ld_small, 80)
            dve.wait_ge(const_act, 1)
            v.tensor_scalar(negA[:], expA[:], -1.0, None, ALU.mult).then_inc(const_dve, 1)
            v.tensor_copy(Dx[:], hpar[:, 2, :][:, :, None].to_broadcast([P, NH, HD])).then_inc(const_dve, 1)
            for k in range(XT):
                v.tensor_scalar(wo[:, k, :], wo[:, k, :], normw[:, k:k + 1], None, ALU.mult).then_inc(const_dve, 1)
            v.memset(cnt[:], 0.0).then_inc(const_dve, 1)
            v.memset(cnt16[:], 0.0).then_inc(const_dve, 1)
            dve.wait_ge(const_dve, 4 + XT)
            dve.wait_ge(ld_x0, 16)

            def moments(name, n, src, st, mv, ve, nm=None):
                item, base = name
                hold_dve(base)
                for t in range(TPB):
                    v.bn_stats(out=st[:, t, :], in_=src(t)).then_inc(S[item], 1)
                need(dve, item, base, n + 2)
                hold_dve(base)
                for t in range(TPB):
                    v.bn_aggr(out=mv[:, t, :], in_=st[:, t, :]).then_inc(S[item], 1)
                need(dve, item, base, n + 4)
                v.tensor_scalar(ve[:], mv[:, :, 1], EPS, None, ALU.add).then_inc(S[item], 1)
                if nm is not None:
                    v.tensor_scalar(nm[:], mv[:, :, 0], -1.0, None, ALU.mult).then_inc(S[item], 1)

            def bc(ap, n):
                shape = list(ap.shape) + [n]
                return ap[(slice(None),) * len(ap.shape) + (None,)].to_broadcast(shape)

            def heads(ap):
                return ap.rearrange("p (h d) -> p h d", h=NH)

            def taps(a, i, out):
                need(dve, "a_conv0", a[0], 2 * i + 2)
                for s in range(1, KW):
                    for k in range(PAIRS[i], PAIRS[i] + 2):
                        if s > 1:
                            need(dve, "a_conv", a[0], 2 * i * (KW - 1) + (s - 2) * 2 + k % 2 + 1)
                        v.scalar_tensor_tensor(
                            out=acc[:, k, s:], in0=out[:, k % 2 * SEQ:(k % 2 + 1) * SEQ - s],
                            scalar=convp[:, k, KW - 1 - s:KW - s], in1=acc[:, k, s:],
                            op0=ALU.mult, op1=ALU.add).then_inc(S["a_conv"], 1)

            def mamba(n, a, b, d, c, p):
                if b:
                    need(dve, "b_small_ps", b[0])
                    need(dve, "b_exp", b[0] - 1)
                    v.tensor_scalar(ncum[:].rearrange("p t h -> p (t h)"), bank[4][:, 256:272], -1.0, None, ALU.mult
                                    ).then_inc(S["b_small"], 1)
                    need(dve, "b_small", b[0], 1)
                    v.tensor_tensor(left[:], bank[4][:, 272:272 + NH], ncum[:, 0, :], ALU.add
                                    ).then_inc(S["b_small"], 1)
                    need(dve, "b_hi", b[0])
                    need(dve, "b_cum_ps", b[0] - 1)
                    v.tensor_tensor(parts_r[0:PR], bank[5][0:PR, SEQ:], parts[0:PR], ALU.subtract
                                    ).then_inc(S["b_piece"], 1)
                    lo = slice(2 * LANE, PR)
                    need(dve, "b_piece", b[0], 1)
                    v.tensor_copy(parts_m[lo], parts_r[lo]).then_inc(S["b_piece"], 1)
                    v.tensor_copy(parts[LANE:LANE + NH], parts_r[LANE:LANE + NH]).then_inc(S["b_piece"], 1)
                    need(dve, "b_piece", b[0], 2)
                    v.tensor_tensor(parts[lo], parts_r[lo], parts_m[lo], ALU.subtract).then_inc(S["b_piece"], 1)
                if d:
                    need(dve, "d_ss", d[0])
                    need(dve, "d_rms", d[0] - 1)
                    v.tensor_scalar(ms[:], ss[:], 1.0 / DI, EPS, ALU.mult, ALU.add).then_inc(S["d_ms"], 1)
                if n:
                    if isinstance(n[0], int) and n[0] == 1:
                        dve.wait_ge(ld_x1, 16)
                    need(dve, "n_rstd", n[0] - 1)
                    need(dve, "n_norm", n[0] - 1)
                    moments(("n_stats", n[0]), 0, lambda t: x_all[:, bass.ts(n[0] * TPB + t, DM)], a_st, a_mv, a_ve,
                            a_nm)
                if p:
                    places(p)
                if a:
                    taps(a, 0, bank[6])
                if d:
                    need(dve, "d_rms", d[0])
                    need(dve, "d_out_ps", d[0])
                    for t in range(TPB):
                        v.tensor_scalar(ao[:, t], bank[0][:, bass.ts(t, DM)], rms[:, t:t + 1], None, ALU.mult
                                        ).then_inc(S["d_ao"], 1)
                    need(dve, "d_ao", d[0], 2)
                    moments(("d_ao", d[0]), 2, lambda t: ao[:, t], b_stt, b_mv, b_ve)
                if b:
                    need(dve, "b_yd_ps", b[0] - 1)
                    for t in range(TPB):
                        need(dve, "b_xs", b[0], t + 1)
                        v.tensor_tensor(heads(xdt[:, t]), heads(xs[:, t]), bc(dt[b[2]][:, t, :], HD), ALU.mult
                                        ).then_inc(S["b_xdt"], 1)
                    need(dve, "b_edge", b[0], 1)
                    need(dve, "b_xdt", b[0], 1)
                    v.tensor_tensor(heads(xw[:]), heads(xdt[:, 0]), bc(wleft[:], HD), ALU.mult
                                    ).then_inc(S["b_xdt"], 1)
                if d:
                    need(dve, "d_rs", d[0])
                    for t in range(TPB):
                        v.tensor_scalar(aon[:, t], ao[:, t], b_mv[:, t, 0:1], b_rst[:, t:t + 1],
                                        ALU.subtract, ALU.mult).then_inc(S["d_aon"], 1)
                if a:
                    taps(a, 1, bank[5])
                if a:
                    taps(a, 2, bank[7])
                if a:
                    need(dve, "a_dt_ps", a[0])
                    need(dve, "c_lg_ps", a[0] - 3)
                    need(dve, "a_dt", a[0] - 1)
                    v.tensor_tensor(dtx[:], bank[4][:, 0:TPB * NH].rearrange("p (t h) -> p t h", t=TPB),
                                    hpar[:, 0:1, :].to_broadcast([P, TPB, NH]), ALU.add).then_inc(S["a_dtx"], 1)
                if c:
                    need(dve, "c_lg_ps", c[0])
                    need(dve, "p_exp", c[0] - 1)
                    v.tensor_copy(lg[:].rearrange("p t e -> p (t e)"), bank[4][:, P:P + TPB * NE]).then_inc(S["c_top"], 1)
                if b:
                    need(dve, "b_exp", b[0])
                    need(dve, "b_gb", b[0], 1)
                    v.tensor_tensor(M[:, 1], M[:, 1], Gm[:, 1:2, :].to_broadcast([P, NH, P]), ALU.mult
                                    ).then_inc(S["b_m1"], 1)
                if d:
                    need(dve, "d_x1", d[0])
                    need(dve, "d_hrs", d[0] - 1)
                    moments(("d_h", d[0]), 0, lambda t: x_all[:, bass.ts(d[0] * TPB + t, DM)], h_st, h_mv, h_ve,
                            h_nm)
                if a:
                    need(dve, "a_sp", a[0])
                    need(dve, "b_xdt", a[0] - 2)
                    need(dve, "b_cum_ps", a[0] - 2)
                    v.scalar_tensor_tensor(out=dt[a[2]][:], in0=dtx[:], scalar=0.0, in1=dtl[:], op0=ALU.max,
                                           op1=ALU.add).then_inc(S["a_dt"], 1)
                    need(dve, "a_dt", a[0], 1)
                    v.tensor_tensor(dA3[a[2]][:, :, :, 0:NH], dt[a[2]][:, :, None, :].to_broadcast([P, TPB, 3, NH]),
                                    negA[:, None, None, :].to_broadcast([P, TPB, 3, NH]), ALU.mult
                                    ).then_inc(S["a_dt"], 1)
                if b:
                    need(dve, "b_skip", b[0])
                    need(dve, "b_yd_ps", b[0], 1)
                    need(dve, "d_yT_ps", b[0] - 1)
                    need(dve, "d_ss", b[0] - 1)
                    v.tensor_tensor(yg[:, 0], bank[5][:], skip[:, 0], ALU.add).then_inc(S["b_y"], 1)
                    need(dve, "b_yo_ps", b[0])
                    need(dve, "b_edge", b[0])
                    v.tensor_tensor(heads(yoff[:]), heads(bank[7][:]), bc(ecum[:], HD), ALU.mult
                                    ).then_inc(S["b_y"], 1)
                    need(dve, "b_y", b[0], 2)
                    v.tensor_tensor(yoff[:], yoff[:], skip[:, 1], ALU.add).then_inc(S["b_y"], 1)
                if c:
                    need(dve, "p_pos_ps", c[0] - 1)
                    need(dve, "p_slot", c[0] - 1)
                    need(dve, "c_top", c[0], 1)
                    hold_dve(c[0])
                    for t in range(TPB):
                        v.max(mx[:, t, :], lg[:, t, :]).then_inc(S["c_top"], 1)
                    need(dve, "c_top", c[0], 3)
                    hold_dve(c[0])
                    for t in range(TPB):
                        v.max_index(ix[:, t, :], mx[:, t, :], lg[:, t, :]).then_inc(S["c_top"], 1)
                    v.tensor_scalar(nmx[:], mx[:, :, 0], -1.0, None, ALU.mult).then_inc(S["c_top"], 1)
                    need(dve, "c_top", c[0], 5)
                    v.tensor_copy(ixf[:], ix[:, :, 0:TOPK]).then_inc(S["c_top"], 1)
                if b:
                    need(dve, "b_yd_ps", b[0])
                    need(dve, "b_y", b[0], 3)
                    v.tensor_tensor(yg[:, 1], bank[6][:], yoff[:], ALU.add).then_inc(S["b_y"], 1)
                if c:
                    need(dve, "c_top", c[0], 7)
                    v.tensor_tensor(oh[:], iota_e[:, None, None, :].to_broadcast([P, TPB, TOPK, NE]),
                                    bc(ixf[:], NE), ALU.is_equal).then_inc(S["c_top"], 1)
                if c:
                    need(dve, "c_top", c[0], 8)
                    with nc.allow_low_precision("sums of 0 and 1"):
                        v.tensor_reduce(out=chosen[:], in_=oh[:].rearrange("p t k e -> p t e k"), axis=AX.X,
                                        op=ALU.add).then_inc(S["c_top"], 1)

            def places(p):
                def nth(i):
                    need(dve, "p_slot", p[0], i)

                def done(ins):
                    ins.then_inc(S["p_slot"], 1)

                need(dve, "p_pos_ps", p[0])
                done(v.tensor_tensor(sel[:], oh[:], bank[2][:, 0:TPB * NE].rearrange(
                    "p (t e) -> p t e", t=TPB)[:, :, None, :].to_broadcast([P, TPB, TOPK, NE]), ALU.mult))
                done(v.tensor_tensor(cnt[:], cnt[:], chosen[:, 0, :], ALU.add))
                nth(1)
                done(v.tensor_reduce(out=pk[:], in_=sel[:], axis=AX.X, op=ALU.add))
                nth(2)
                done(v.tensor_tensor(cnt[:], cnt[:], chosen[:, 1, :], ALU.add))
                need(dve, "p_exp", p[0])
                done(v.reciprocal(rsum[:], esum[:]))
                nth(4)
                done(v.tensor_copy(cnt16[:], cnt[:]))
                done(v.scalar_tensor_tensor(out=slot[:], in0=ixf[:], scalar=float(CAP), in1=pk[:],
                                            op0=ALU.mult, op1=ALU.add))
                done(v.tensor_scalar(over[:], pk[:], float(CAP), float(SKIP), ALU.is_ge, ALU.mult))
                nth(5)
                done(v.tensor_tensor(p6[:], e6[:], bc(rsum[:], TOPK), ALU.mult))
                done(v.tensor_scalar(fits[:], pk[:], float(CAP), None, ALU.is_lt))
                nth(9)
                done(v.tensor_reduce(out=s6[:], in_=p6[:], axis=AX.X, op=ALU.add))
                wait(dve, sc_table[p[2]], p[1] * (TPB * TOPK * 16))
                done(v.tensor_tensor(slot_i[p[2]][:].rearrange("p (t k) -> p t k", t=TPB), slot[:], over[:],
                                     ALU.add))
                nth(11)
                done(v.tensor_scalar(s6e[:], s6[:], 1e-20, None, ALU.add))
                done(v.tensor_tensor(pay[p[2]][:], pay[1 - p[2]][:], step_pay[:], ALU.add))
                nth(13)
                done(v.reciprocal(r6[:], s6e[:]))
                nth(15)
                done(v.tensor_tensor(w6[:], p6[:], bc(r6[:], TOPK), ALU.mult))
                nth(16)
                done(v.tensor_tensor(w_all[:, bass.ts(p[0], TPB * TOPK)].rearrange("p (t k) -> p t k", t=TPB),
                                     w6[:], fits[:], ALU.mult))

            pipeline(dve, NB, [0, 1, 2, 3, 4, 5], mamba, peel=2)
            dve.wait_ge(cnt_ps, 1)
            v.tensor_copy(cnt_i[:, 0:NE], bank[0][:, 0:NE]).then_inc(cnt_sb, 1)
            v.tensor_reduce(out=cnt[:, 0:1], in_=bank[0][:, 0:NE], axis=AX.X, op=ALU.max).then_inc(cnt_sb, 1)
            dve.wait_ge(cnt_sb, 2)
            v.tensor_copy(cnt_i[:, NE:NE + 1], cnt[:, 0:1]).then_inc(cnt_sb, 1)

            def shared(u):
                o = 3 * u[2]
                need(dve, "s_D_ps", u[0] - 1)
                need(dve, "s_U_ps", u[0])
                need(dve, "s_silu", u[0])
                v.tensor_tensor(s_hd[:, 0:2, :].rearrange("p k s -> p (k s)"),
                                s_sg[:, 0:2, :].rearrange("p k s -> p (k s)"), bank[o + 1][:], ALU.mult
                                ).then_inc(S["s_hid"], 1)
                v.tensor_tensor(s_hd[0:F2, 2, :], s_sg[0:F2, 2, :], bank[o + 2][0:F2, SEQ:2 * SEQ], ALU.mult
                                ).then_inc(S["s_hid"], 1)

            pipeline(dve, FIRST, [0], shared)

            phase_a_over(dve)
            dve.wait_ge(tab_ps, 2 * NQ)
            for q in range(NQ):
                v.tensor_copy(tok_idx[:, bass.ts(q, P)], bank[0][:, bass.ts(q, P)]).then_inc(tab_sb, 1)
                v.tensor_copy(row_idx[:, bass.ts(q, P)], bank[1][:, bass.ts(q, P)]).then_inc(tab_sb, 1)
            pipeline(dve, EARLY - FIRST, [0], shared, first=FIRST)
            dve.wait_ge(const_pool, 8)
            n_w, n_tail = counters(dve, "dve_wide0", "dve_wide1"), counters(dve, "dve_tails")[0]

            def expert(t, g, d):
                if t:
                    need(dve, "e_T_ps", t[0])
                    need(dve, "e_G_ps", t[0] - 2)
                    v.tensor_copy(xgT[t[2]][:, 1, :], bank[1][:]).then_inc(S["e_xTv"], 1)
                if g:
                    need(dve, "e_D_ps", g[0] - 2)
                    need(dve, "e_G_ps", g[0])
                    need(dve, "e_silu", g[0], 1)
                    v.tensor_tensor(hid[g[2]][:, 0, :], sg[g[2]][:, 0, :], bank[3][:], ALU.mult
                                    ).then_inc(S["e_hid"], 1)
                    need(dve, "e_silu", g[0])
                    v.tensor_tensor(hid[g[2]][0:F1, 1, :], sg[g[2]][0:F1, 1, :], bank[4][UO:UO + F1], ALU.mult
                                    ).then_inc(S["e_hid"], 1)
                if d:
                    need(dve, "e_D_ps", d[0])
                    n = count_of(dve, d[0])
                    wait(dve, sc_y[d[2]], d[1] * (MAIN * 16))
                    r = dve.snap(n_w[d[2]])
                    wait(dve, sc_w[d[2]], (r + 1) * 16)
                    dve.sem_inc(tick_dve, 1)
                    with dve.If(n > MAIN * P):
                        v.tensor_copy(eo[d[2]][:, MAIN, :], bank[6][:, DM:2 * DM])
                        dve.reg_add(n_w[d[2]], n_w[d[2]], 1)
                    v.tensor_copy(eo[d[2]][:, 2, :], bank[6][:, 0:DM]).then_inc(S["e_eov"], 1)
                if g:
                    n = count_of(dve, g[0])
                    with dve.If(n > WR):
                        r = dve.snap(n_tail)
                        dve.wait_ge(t_silu, r * 2 + 2)
                        v.tensor_tensor(t_hd[:, 0, :], t_sg[:, 0, :], bank[3][:, 0:TAIL * P], ALU.mult
                                        ).then_inc(t_hid, 1)
                        v.tensor_tensor(t_hd[0:F1, 1, :], t_sg[0:F1, 1, :], bank[4][UO:UO + F1, 0:TAIL * P],
                                        ALU.mult).then_inc(t_hid, 1)
                        dve.reg_add(n_tail, n_tail, 1)
                    dve.nop()

            pipeline(dve, NE, [2, 3, 4], expert, peel=2)
            for i in range(2):
                dve.wait_ge(sc_w[i], dve.snap(n_w[i]) * 16 + 16)
                dve.sem_inc(tick_dve, 1)
            dve.sem_inc(w_idx, 1)

            phase_b_over(dve)

            def combine(d):
                def nth(n):
                    need(dve, "s_acc", d[0], n)

                def done(ins):
                    ins.then_inc(S["s_acc"], 1)

                need(dve, "s_acc", d[0] - 1)
                done(v.tensor_copy(wb[:].rearrange("p t k -> p (t k)"), w_all[:, bass.ts(d[0], TPB * TOPK)]))
                nth(1)
                wait(dve, ld_y[d[2]], (d[1] + 1) * 16)
                need(dve, "s_keep", d[0])
                for k in range(OWN):
                    for t in range(TPB):
                        if k:
                            nth(2 * k + t)
                            prev = cacc[:, t]
                        else:
                            prev = kept[:, bass.ts(d[0] * TPB + t, DM)]
                        done(v.scalar_tensor_tensor(out=cacc[:, t], in0=yb[d[2]][:, t, k, :],
                                                    scalar=wb[:, t, k:k + 1], in1=prev,
                                                    op0=ALU.mult, op1=ALU.add))
                need(dve, "y_sum", d[0])
                nth(7)
                done(v.tensor_tensor(cacc[:], cacc[:], rest[d[2]][:], ALU.add))
                nth(8)
                moments(("s_acc", d[0]), 8, lambda t: cacc[:, t], c_st, c_mv, c_ve)
                need(dve, "s_rs", d[0])
                need(dve, "s_out", d[0] - 1)
                for t in range(TPB):
                    done(v.tensor_scalar(cn[:, t], cacc[:, t], c_mv[:, t, 0:1], c_rs[:, t:t + 1],
                                         ALU.subtract, ALU.mult))

            def last_phase(u):
                shared(u)
                combine(sooner(u))

            pipeline(dve, NB - EARLY, [0], last_phase, first=EARLY)
            pipeline(dve, EARLY, [0], combine, first=NB - EARLY)


def kernel(**inputs):
    import concourse.bacc as bacc
    from concourse.bass_utils import run_bass_kernel_spmd

    g = {n.removeprefix("L0_"): np.asarray(a) for n, a in inputs.items()}

    def on_partitions(a):
        return np.ascontiguousarray(a.reshape(-1, P, a.shape[-1]).transpose(1, 0, 2))

    gate_t, up_t, down_t = (g[n].transpose(0, 2, 1) for n in ("ffn_w_gate", "ffn_w_up", "ffn_w_down"))
    gu = np.zeros((NE, DM, GW), np.float32)
    gu[:, :, 0:P], gu[:, :, P:2 * P] = gate_t[:, :, 0:P], up_t[:, :, 0:P]
    gu[:, :, 2 * P:2 * P + F1], gu[:, :, 2 * P + UO:] = gate_t[:, :, P:], up_t[:, :, P:]
    gu = gu.reshape(NE, KD, P, GW).transpose(0, 2, 1, 3).reshape(NE, P, KD * GW)
    sd = np.zeros((FT * P, DM), np.float32)
    sd[:FS] = g["ffn_sh_down"].T
    arrays = dict(
        x=np.ascontiguousarray(g["attn_x"].reshape(NT, DM)),
        win=on_partitions(g["attn_in_proj_w"].T),
        wo=on_partitions(g["attn_out_proj_w"].T),
        convp=on_partitions(np.concatenate([g["attn_conv_w"], g["attn_conv_b"][:, None]], axis=1)),
        normw=np.ascontiguousarray(g["attn_norm_w"].reshape(XT, P).T),
        hpar=np.stack([g["attn_dt_bias"], g["attn_A_log"], g["attn_D"]]),
        wg=on_partitions(g["ffn_gate_w"].T),
        wsu=on_partitions(np.concatenate([g["ffn_sh_gate"].T, g["ffn_sh_up"].T], axis=1)),
        wsd=on_partitions(sd),
        we=np.ascontiguousarray(np.concatenate([gu, down_t[:, 0:P, :]], axis=2).reshape(NE * P, -1)),
        we1=np.ascontiguousarray(down_t[:, P:, :].reshape(NE * F1, DM)),
    )
    nc = bacc.Bacc("TRN2", target_bir_lowering=False, num_devices=1)
    T = {n: nc.dram_tensor("in_" + n, a.shape, mybir.dt.from_np(a.dtype), kind="ExternalInput").ap()
         for n, a in arrays.items()}
    T["out"] = nc.dram_tensor("out", (NT, DM), FP32, kind="ExternalOutput").ap()
    build(nc, T)
    r = run_bass_kernel_spmd(nc, [{"in_" + n: a for n, a in arrays.items()}], core_ids=[0])
    return r.results[0]["out"].reshape(NB, SEQ, DM)
```
